# Optimizing a Trainium2 kernel written in Bass

```python
import numpy as np
import jax
import jax.numpy as jnp

def _softmax(x, axis=-1):
    return jax.nn.softmax(x, axis=axis)

def _gelu(x):
    return jax.nn.gelu(x, approximate=True)

def _silu(x):
    return jax.nn.silu(x)

def _sigmoid(x):
    return jax.nn.sigmoid(x)

def _layernorm(x, axis=-1, eps=1e-05):
    m = jnp.mean(x, axis=axis, keepdims=True)
    v = jnp.var(x, axis=axis, keepdims=True)
    return (x - m) / jnp.sqrt(v + eps)

def _scatter_add(tgt, idx, src, axis=0):
    return tgt.at[idx].add(src)

def _segment_sum(src, seg, n):
    return jax.ops.segment_sum(src, seg, n)
kernel_name = 'mk_metaformer_d1_conv_nchw256_r4_d8863b'

def setup_inputs(seed: int=0):
    np.random.seed(seed)
    _w = jnp.asarray

    def _rec_inputs():
        import jax
        import jax.numpy as jnp
        _gk = jax.random.key(seed)
        x = -0.0003957 + 1 * jax.random.normal(jax.random.fold_in(_gk, 1), (16, 64, 56, 56), jnp.float32)
        return x
    x = _rec_inputs()

    def _L0_conv_setup():
        import jax, jax.numpy as jnp
        import numpy as np
        BITS_I, BITS_W = (8, 8)
        GROUP = 36
        DIR_I = (0, 1, 2, 3)
        DIR_W = (0, 1, 2, 3)

        def bfp_quantize(x, bits, group_size, perm):
            inv_perm = tuple(np.argsort(perm))
            xp = jnp.transpose(x, perm)
            shape = xp.shape
            flat = xp.reshape(-1)
            n = flat.shape[0]
            pad = -n % group_size
            flat = jnp.pad(flat, (0, pad))
            g = flat.reshape(-1, group_size)
            maxabs = jnp.max(jnp.abs(g), axis=1, keepdims=True)
            e = jnp.floor(jnp.log2(jnp.maximum(maxabs, jnp.float32(1e-38))))
            scale = jnp.exp2(e - (bits - 1))
            qmax = 2 ** (bits - 1) - 1
            q = jnp.clip(jnp.round(g / scale), -qmax - 1, qmax) * scale
            q = jnp.where(maxabs == 0, jnp.float32(0), q)
            out = q.reshape(-1)[:n].reshape(shape)
            return jnp.transpose(out, inv_perm)

        def conv2d(x, w, b, stride=1, padding=1, dilation=1, groups=1):
            out = jax.lax.conv_general_dilated(x, w, window_strides=(stride, stride), padding=[(padding, padding), (padding, padding)], rhs_dilation=(dilation, dilation), feature_group_count=groups, dimension_numbers=('NCHW', 'OIHW', 'NCHW'))
            if b is not None:
                out = out + b[None, :, None, None]
            return out
        key = jax.random.key(seed)
        k1, k2, k3 = jax.random.split(key, 3)
        x = jax.random.normal(k1, (16, 64, 56, 56), dtype=jnp.float32)
        fan_in = 64 * 3 * 3
        bound = 1.0 / np.sqrt(fan_in)
        weight = jax.random.uniform(k2, (64, 64, 3, 3), dtype=jnp.float32, minval=-np.sqrt(6.0 / fan_in), maxval=np.sqrt(6.0 / fan_in))
        bias = jax.random.uniform(k3, (64,), dtype=jnp.float32, minval=-bound, maxval=bound)
        return {'x': x, 'weight': weight, 'bias': bias}
    _L0_conv_all = _L0_conv_setup()
    _L0_conv_in = {k: v for k, v in _L0_conv_all.items() if k in ('weight', 'bias')}
    del _L0_conv_all

    def _L0_ffn_setup():
        import jax, jax.numpy as jnp
        import numpy as np
        B, N, D = (16, 1024, 64)
        NUM_EXPERTS, TOP_K, HEADS = (4, 2, 4)
        N_EDGES = 262144
        LN_EPS = 1e-05

        def _layernorm(x, g, b):
            mu = x.mean(-1, keepdims=True)
            var = ((x - mu) ** 2).mean(-1, keepdims=True)
            return (x - mu) * jax.lax.rsqrt(var + LN_EPS) * g + b

        def _forward(x, edge_index, W_gat, att_src, att_dst, b_gat, ln_gamma, ln_beta, W1, b1, W2, b2):
            Bc, Nc, Dc = x.shape
            M = Bc * Nc
            x_flat = x.reshape(M, Dc)
            h = (x_flat @ W_gat).reshape(M, HEADS, NUM_EXPERTS)
            loops = jnp.arange(M, dtype=edge_index.dtype)
            src = jnp.concatenate([edge_index[0], loops])
            dst = jnp.concatenate([edge_index[1], loops])
            a_src = (h * att_src).sum(-1)
            a_dst = (h * att_dst).sum(-1)
            e = jax.nn.leaky_relu(a_src[src] + a_dst[dst], negative_slope=0.2)
            e_max = jax.ops.segment_max(e, dst, num_segments=M)
            ee = jnp.exp(e - e_max[dst])
            denom = jax.ops.segment_sum(ee, dst, num_segments=M)
            alpha = ee / (denom[dst] + 1e-16)
            msg = h[src] * alpha[:, :, None]
            agg = jax.ops.segment_sum(msg, dst, num_segments=M).reshape(M, HEADS * NUM_EXPERTS) + b_gat
            scores = _layernorm(agg, ln_gamma, ln_beta).reshape(M, HEADS, NUM_EXPERTS).mean(1)
            scores = scores.reshape(Bc, Nc, NUM_EXPERTS)
            topk_s, topk_i = jax.lax.top_k(scores, TOP_K)
            w = jax.nn.softmax(topk_s, axis=-1)
            out = jnp.zeros_like(x)
            for ei in range(NUM_EXPERTS):
                g = jnp.where(topk_i == ei, w, 0.0).sum(-1)
                hh = jax.nn.gelu(x @ W1[ei] + b1[ei], approximate=False)
                out = out + g[..., None] * (hh @ W2[ei] + b2[ei])
            return out
        key = jax.random.key(seed)
        ks = jax.random.split(key, 8)
        s = 0.05
        return {'x': jax.random.normal(ks[0], (B, N, D), jnp.float32), 'W_gat': jax.random.normal(ks[1], (D, HEADS * NUM_EXPERTS), jnp.float32) * s, 'att_src': jax.random.normal(ks[2], (HEADS, NUM_EXPERTS), jnp.float32) * s, 'att_dst': jax.random.normal(ks[3], (HEADS, NUM_EXPERTS), jnp.float32) * s, 'b_gat': jnp.zeros((HEADS * NUM_EXPERTS,), jnp.float32), 'ln_gamma': jnp.ones((HEADS * NUM_EXPERTS,), jnp.float32), 'ln_beta': jnp.zeros((HEADS * NUM_EXPERTS,), jnp.float32), 'W1': jax.random.normal(ks[4], (NUM_EXPERTS, D, 2 * D), jnp.float32) * s, 'b1': jnp.zeros((NUM_EXPERTS, 2 * D), jnp.float32), 'W2': jax.random.normal(ks[5], (NUM_EXPERTS, 2 * D, D), jnp.float32) * s, 'b2': jnp.zeros((NUM_EXPERTS, D), jnp.float32), 'edge_index': jax.random.randint(ks[6], (2, N_EDGES), 0, B * N, jnp.int32)}
    _L0_ffn_all = _L0_ffn_setup()
    _L0_ffn_in = {k: v for k, v in _L0_ffn_all.items() if k in ('W_gat', 'att_src', 'att_dst', 'b_gat', 'ln_gamma', 'ln_beta', 'W1', 'b1', 'W2', 'b2', 'edge_index')}
    del _L0_ffn_all
    return {'x': x, 'L0_conv_weight': _L0_conv_in['weight'], 'L0_conv_bias': _L0_conv_in['bias'], 'L0_ffn_W_gat': _L0_ffn_in['W_gat'], 'L0_ffn_att_src': _L0_ffn_in['att_src'], 'L0_ffn_att_dst': _L0_ffn_in['att_dst'], 'L0_ffn_b_gat': _L0_ffn_in['b_gat'], 'L0_ffn_ln_gamma': _L0_ffn_in['ln_gamma'], 'L0_ffn_ln_beta': _L0_ffn_in['ln_beta'], 'L0_ffn_W1': _L0_ffn_in['W1'], 'L0_ffn_b1': _L0_ffn_in['b1'], 'L0_ffn_W2': _L0_ffn_in['W2'], 'L0_ffn_b2': _L0_ffn_in['b2'], 'L0_ffn_edge_index': _L0_ffn_in['edge_index']}

def reference(x, L0_conv_weight, L0_conv_bias, L0_ffn_W_gat, L0_ffn_att_src, L0_ffn_att_dst, L0_ffn_b_gat, L0_ffn_ln_gamma, L0_ffn_ln_beta, L0_ffn_W1, L0_ffn_b1, L0_ffn_W2, L0_ffn_b2, L0_ffn_edge_index):
    import jax
    import jax.numpy as jnp

    def _L0_conv_ref(x, weight, bias):
        import jax, jax.numpy as jnp
        import numpy as np
        BITS_I, BITS_W = (8, 8)
        GROUP = 36
        DIR_I = (0, 1, 2, 3)
        DIR_W = (0, 1, 2, 3)

        def bfp_quantize(x, bits, group_size, perm):
            inv_perm = tuple(np.argsort(perm))
            xp = jnp.transpose(x, perm)
            shape = xp.shape
            flat = xp.reshape(-1)
            n = flat.shape[0]
            pad = -n % group_size
            flat = jnp.pad(flat, (0, pad))
            g = flat.reshape(-1, group_size)
            maxabs = jnp.max(jnp.abs(g), axis=1, keepdims=True)
            e = jnp.floor(jnp.log2(jnp.maximum(maxabs, jnp.float32(1e-38))))
            scale = jnp.exp2(e - (bits - 1))
            qmax = 2 ** (bits - 1) - 1
            q = jnp.clip(jnp.round(g / scale), -qmax - 1, qmax) * scale
            q = jnp.where(maxabs == 0, jnp.float32(0), q)
            out = q.reshape(-1)[:n].reshape(shape)
            return jnp.transpose(out, inv_perm)

        def conv2d(x, w, b, stride=1, padding=1, dilation=1, groups=1):
            out = jax.lax.conv_general_dilated(x, w, window_strides=(stride, stride), padding=[(padding, padding), (padding, padding)], rhs_dilation=(dilation, dilation), feature_group_count=groups, dimension_numbers=('NCHW', 'OIHW', 'NCHW'))
            if b is not None:
                out = out + b[None, :, None, None]
            return out
        xq = bfp_quantize(x, BITS_I, GROUP, DIR_I)
        wq = bfp_quantize(weight, BITS_W, GROUP, DIR_W)
        return conv2d(xq, wq, bias, stride=1, padding=1, dilation=1, groups=1)

    def _L0_ffn_ref(x, W_gat, att_src, att_dst, b_gat, ln_gamma, ln_beta, W1, b1, W2, b2, edge_index):
        import jax, jax.numpy as jnp
        import numpy as np
        B, N, D = (16, 1024, 64)
        NUM_EXPERTS, TOP_K, HEADS = (4, 2, 4)
        N_EDGES = 262144
        LN_EPS = 1e-05

        def _layernorm(x, g, b):
            mu = x.mean(-1, keepdims=True)
            var = ((x - mu) ** 2).mean(-1, keepdims=True)
            return (x - mu) * jax.lax.rsqrt(var + LN_EPS) * g + b

        def _forward(x, edge_index, W_gat, att_src, att_dst, b_gat, ln_gamma, ln_beta, W1, b1, W2, b2):
            Bc, Nc, Dc = x.shape
            M = Bc * Nc
            x_flat = x.reshape(M, Dc)
            h = (x_flat @ W_gat).reshape(M, HEADS, NUM_EXPERTS)
            loops = jnp.arange(M, dtype=edge_index.dtype)
            src = jnp.concatenate([edge_index[0], loops])
            dst = jnp.concatenate([edge_index[1], loops])
            a_src = (h * att_src).sum(-1)
            a_dst = (h * att_dst).sum(-1)
            e = jax.nn.leaky_relu(a_src[src] + a_dst[dst], negative_slope=0.2)
            e_max = jax.ops.segment_max(e, dst, num_segments=M)
            ee = jnp.exp(e - e_max[dst])
            denom = jax.ops.segment_sum(ee, dst, num_segments=M)
            alpha = ee / (denom[dst] + 1e-16)
            msg = h[src] * alpha[:, :, None]
            agg = jax.ops.segment_sum(msg, dst, num_segments=M).reshape(M, HEADS * NUM_EXPERTS) + b_gat
            scores = _layernorm(agg, ln_gamma, ln_beta).reshape(M, HEADS, NUM_EXPERTS).mean(1)
            scores = scores.reshape(Bc, Nc, NUM_EXPERTS)
            topk_s, topk_i = jax.lax.top_k(scores, TOP_K)
            w = jax.nn.softmax(topk_s, axis=-1)
            out = jnp.zeros_like(x)
            for ei in range(NUM_EXPERTS):
                g = jnp.where(topk_i == ei, w, 0.0).sum(-1)
                hh = jax.nn.gelu(x @ W1[ei] + b1[ei], approximate=False)
                out = out + g[..., None] * (hh @ W2[ei] + b2[ei])
            return out
        return _forward(x, edge_index, W_gat, att_src, att_dst, b_gat, ln_gamma, ln_beta, W1, b1, W2, b2)

    def _gn(v, G=32, eps=1e-05):
        B_, C_, H_, W_ = v.shape
        g = v.reshape(B_, G, C_ // G, H_, W_)
        m = jnp.mean(g, axis=(2, 3, 4), keepdims=True)
        s = jnp.var(g, axis=(2, 3, 4), keepdims=True)
        return ((g - m) / jnp.sqrt(s + eps)).reshape(v.shape)

    def _ln_c(v, eps=1e-06):
        m = jnp.mean(v, axis=1, keepdims=True)
        s = jnp.var(v, axis=1, keepdims=True)
        return (v - m) / jnp.sqrt(s + eps)

    def _ln_t(v, eps=1e-05):
        m = jnp.mean(v, axis=-1, keepdims=True)
        s = jnp.var(v, axis=-1, keepdims=True)
        return (v - m) / jnp.sqrt(s + eps)

    def _to_tokens(v):
        B_, C_, H_, W_ = v.shape
        return v.reshape(B_, C_, H_ * W_).transpose(0, 2, 1)

    def _from_tokens(t, like):
        B_, C_, H_, W_ = like.shape
        return t.transpose(0, 2, 1).reshape(B_, C_, H_, W_)
    x = x + _L0_conv_ref(_ln_c(x), L0_conv_weight, L0_conv_bias)
    t = _to_tokens(x)
    t = t + _L0_ffn_ref(_ln_t(t), L0_ffn_W_gat, L0_ffn_att_src, L0_ffn_att_dst, L0_ffn_b_gat, L0_ffn_ln_gamma, L0_ffn_ln_beta, L0_ffn_W1, L0_ffn_b1, L0_ffn_W2, L0_ffn_b2, L0_ffn_edge_index)
    x = _from_tokens(t, x)
    return x

_drawn_inputs = setup_inputs


def setup_inputs(seed=0):
    import zlib

    import numpy as np

    out = dict(_drawn_inputs(seed))
    spreads = {'L0_ffn_b_gat': (0.0, 0.1),
     'L0_ffn_ln_gamma': (1.0, 0.6),
     'L0_ffn_ln_beta': (0.0, 0.464),
     'L0_ffn_b1': (0.0, 0.531),
     'L0_ffn_b2': (0.0, 0.1)}
    factors = {'L0_conv_bias': 3.014, 'L0_ffn_att_src': 8.0, 'L0_ffn_att_dst': 8.0}
    for name, (base, spread) in spreads.items():
        noise = np.random.default_rng([zlib.crc32(name.encode()), seed]).standard_normal(out[name].shape)
        drawn = base * np.exp(spread * noise) if base else spread * noise
        out[name] = jnp.asarray(drawn.astype(out[name].dtype))
    for name, factor in factors.items():
        out[name] = (out[name] * factor).astype(out[name].dtype)
    return out
```

```python
from contextlib import ExitStack, contextmanager

import concourse.bass as bass
from concourse import mybir

F32 = mybir.dt.float32
BF16 = mybir.dt.bfloat16
I32 = mybir.dt.int32
U32 = mybir.dt.uint32
U16 = mybir.dt.uint16
ALU = mybir.AluOpType
ACT = mybir.ActivationFunctionType
AX = mybir.AxisListType

P = 128

B, CH, HGT, WID = 16, 64, 56, 56
HALF_ROWS = HGT // 2
HALF = HALF_ROWS * WID
CHUNKS = 4
CHUNK = HALF // CHUNKS
CHUNK_ROWS = HALF_ROWS // CHUNKS
TAPS = 9
M = B * HGT * WID
TOK = 112
TOK_TILES = HALF // TOK

GROUP = 36
FLAT = B * CH * HGT * WID
GROUPS_P = -(-FLAT // (GROUP * P))
QCHUNKS = 17
QGROUPS = GROUPS_P // QCHUNKS
FLAT_P = GROUPS_P * GROUP
assert QCHUNKS * QGROUPS == GROUPS_P
MAGIC = 1.5 * 2.0 ** 23
TINY = 2.0 ** -100
EXP_BITS = 0x7F800000
INV_BITS = 0x7F000000

EDGES = 262144
ECOLS = EDGES // P
HEADS, DIM = 4, 4
FEAT = HEADS * DIM
ROW = FEAT + 2 * HEADS
VALS = FEAT + HEADS
BLK = 1024
BLK_BITS, LO_BITS = 10, 7
HI = BLK // P
NB = M // BLK
NQ = M // P
G = 8
BUFS = 4
MAX_TILES = (EDGES + NB * (P - 1)) // P
NG = -(-MAX_TILES // (G * BUFS)) * BUFS
TILES = NG * G
ID_W = -(-(TILES + G) // P)
PAD_DST = 1 << 20
RANK_COLS = 512
SEND = 16

EXPERTS, HID = 4, 128
GQ = 8
PAIR_Q = 2 * HGT * WID // P


class Signal:

    def __init__(self, sem):
        self.sem, self.base, self.k = sem, 0, 0

    @property
    def value(self):
        return self.base + self.k


def link(eng, instr, sig):
    instr.then_inc(sig.sem, 1)
    sig.k += 1
    eng.wait_ge(sig.sem, sig.value)


def hold(eng, sem, value, turns):
    eng.wait_ge(sem, value)
    eng.sem_inc(turns, 1)


@contextmanager
def rolled(eng, start, stop, sig, per_trip):
    first = sig.value
    with eng.Fori(start, stop) as i:
        sig.base, sig.k = (i - start) * per_trip + first, 0
        yield i
        assert sig.k == per_trip, sig.k
    sig.base, sig.k = first + (stop - start) * per_trip, 0


def build(nc, x, conv_w, conv_b, w_gat, att_src, att_dst, b_gat, ln_g, ln_b, w1, b1, w2, b2, edges, out):
    ctx = ExitStack()
    with ctx:
        def sb(name, shape, dt=F32):
            return ctx.enter_context(nc.sbuf_tensor(name, shape, dt))

        def sems(names):
            return {n: ctx.enter_context(nc.semaphore(n)) for n in names.split()}

        def dram(name, shape, dt=F32):
            return nc.dram_tensor(name, shape, dt).ap()

        xn_d = dram("xn_d", [P * FLAT_P])
        xq_d = dram("xq_d", [P * FLAT_P], BF16)
        x1_d = dram("x1_d", [B, 2, CH, HALF])
        t_d = dram("t_d", [B, 2, CH, HALF])
        node_d = dram("node_d", [M, ROW])
        edge_d = dram("edge_d", [P * TILES, 2], I32)
        blk_d = dram("blk_d", [P * ID_W], I32)
        gate_d = dram("gate_d", [NQ // GQ, GQ, 3 * EXPERTS, P], BF16)

        ident = sb("ident", [P, P])
        ident_h = sb("ident_h", [P, P], BF16)
        ones = sb("ones", [P, P])
        below = sb("below", [P, P])
        halves = sb("halves", [P, P])
        lane = sb("lane", [P, P])
        tile_no = sb("tile_no", [P, ID_W])
        zero_row = sb("zero_row", [P, 512])
        eps_c = sb("eps_c", [P, 1])
        eps_t = sb("eps_t", [P, 1])
        scratch_i = sb("scratch_i", [P, P], I32)

        cw = sb("cw", [P, CH, TAPS])
        cwq = sb("cwq", [P, CH, TAPS], BF16)
        cw_bd = sb("cw_bd", [P, TAPS, P], BF16)
        cw_t = sb("cw_t", [P, TAPS, P], BF16)
        cbias = sb("cbias", [P, 1])
        proj = sb("proj", [P, 2, ROW])
        att = sb("att", [P, 2, FEAT])
        attw = sb("attw", [P, FEAT])
        vecs = sb("vecs", [P, 3, FEAT])
        w1s = sb("w1s", [P, EXPERTS, HID])
        b1s = sb("b1s", [P, EXPERTS])
        w2s = sb("w2s", [P, EXPERTS, CH])
        b2s = sb("b2s", [3 * EXPERTS, CH])
        b2h = sb("b2h", [3 * EXPERTS, 3, CH], BF16)
        pick = sb("pick", [3 * EXPERTS, EXPERTS, P], BF16)

        A = ctx.enter_context(nc.psum_tensor("A", [P, 4, 512], F32))
        C = ctx.enter_context(nc.psum_tensor("C", [P, 4, 512], F32))
        with ExitStack() as ph:
            def tb(name, shape, dt=F32):
                return ph.enter_context(nc.sbuf_tensor(name, shape, dt))

            X = tb("X", [P, CHUNKS, CHUNK])
            D = tb("D", [P, CHUNKS, CHUNK])
            S = tb("S", [P, CHUNKS, CHUNK])
            Q = tb("Q", [P, HALF_ROWS + 2, WID + 2], BF16)
            rows = tb("rows", [TOK, TOK_TILES, 2 * ROW])
            F = tb("F", [P, QGROUPS, GROUP])
            Fq = tb("Fq", [P, QGROUPS, GROUP], BF16)
            gmax = tb("gmax", [P, QGROUPS])
            ginv = tb("ginv", [P, QGROUPS])
            gscale = tb("gscale", [P, QGROUPS])

            src = tb("src", [P, ECOLS], I32)
            dst = tb("dst", [P, ECOLS], I32)
            rec = tb("rec", [P, ECOLS, 2], I32)
            blk_h = tb("blk_h", [P, ECOLS], BF16)
            mask_h = tb("mask_h", [P, ECOLS], BF16)
            zero_h = tb("zero_h", [P, RANK_COLS], BF16)
            run = tb("run", [P, RANK_COLS])
            pos = tb("pos", [P, ECOLS])
            pos_i = tb("pos_i", [P, ECOLS], I32)
            count = tb("count", [P, NB])
            total_i = tb("total_i", [P, NB], I32)
            tiles_b = tb("tiles_b", [P, NB])
            end_b = tb("end_b", [P, NB])
            start_b = tb("start_b", [P, NB])
            passed = tb("passed", [P, ID_W, NB])
            tile_blk = tb("tile_blk", [P, ID_W])
            tile_blk_i = tb("tile_blk_i", [P, ID_W], I32)
            slots = tb("slots", [P, BUFS, SEND], U32)
            rec_slots = tb("rec_slots", [P, BUFS, SEND, 2], I32)
            pad_rec = tb("pad_rec", [P, TILES // 8, 2], I32)


            s = sems(
                "const_ready weights_loaded edges_loaded vstep pstep counted prefix_ready blocks_ready blk_stored "
                "ranked pads_written xn_pad "
                "x_loaded mean_ready centred squared var_ready deviated normed xn_stored "
                "f_loaded quantised q_stored w_blocks w_turned w_ready "
                "c_loaded conv_done summed mean2_ready centred2 squared2 var2_ready deviated2 tokens_ready "
                "projected rows_ready c_stored sp_turns pool_turns"
            )
            sent = [ctx.enter_context(nc.semaphore(f"sent{k}")) for k in range(BUFS)]
            block = ph.enter_context(nc.Block())

            def pixels(t, b, h):
                return t.rearrange("b c (s r) w -> b s c (r w)", s=2)[b, h]

            xn_img = xn_d[0:FLAT].rearrange("(b c s n) -> b s c n", b=B, c=CH, s=2)
            xq_img = xq_d[0:FLAT].rearrange("(b c r w) -> b c r w", b=B, c=CH, r=HGT)
            xn_flat = xn_d.rearrange("(p j g e) -> p j g e", p=P, j=QCHUNKS, e=GROUP)
            xq_flat = xq_d.rearrange("(p j g e) -> p j g e", p=P, j=QCHUNKS, e=GROUP)
            node_img = node_d.rearrange("(b s j l) f -> b s l j f", b=B, s=2, l=TOK)
            WEIGHT_LOADS = 2 + 2 + 2 + 2 + 3 + 2 + 1 + 1 + 3

            @block.sync
            def _(sp):
                e_v = edges.rearrange("k (p t) -> k p t", p=P)
                sp.dma_start(dst[:], e_v[1]).then_inc(s["edges_loaded"], 16)
                sp.dma_start(src[:], e_v[0]).then_inc(s["edges_loaded"], 16)
                for h in range(2):
                    a = h * CH
                    sp.dma_start(cw[a:a + CH], conv_w.rearrange("o i h w -> o i (h w)")).then_inc(s["weights_loaded"], 16)
                    sp.dma_start(cbias[a:a + CH], conv_b.rearrange("(p k) -> p k", k=1)).then_inc(s["weights_loaded"], 16)
                    sp.dma_start(proj[a:a + CH, h, 0:FEAT], w_gat).then_inc(s["weights_loaded"], 16)
                    sp.dma_start(w1s[a:a + CH], w1.rearrange("e d f -> d e f")).then_inc(s["weights_loaded"], 16)
                for k, v in enumerate((b_gat, ln_g, ln_b)):
                    sp.dma_start(vecs[:, k, :], v.rearrange("(k f) -> k f", k=1).broadcast_to([P, FEAT])).then_inc(s["weights_loaded"], 16)
                for k, v in enumerate((att_src, att_dst)):
                    sp.dma_start(att[:, k, :], v.rearrange("(k h) d -> k (h d)", k=1).broadcast_to([P, FEAT])).then_inc(s["weights_loaded"], 16)
                sp.dma_start(b1s[:], b1.rearrange("e f -> f e"), allow_slow_non_contiguous=True).then_inc(s["weights_loaded"], 16)
                sp.dma_start(w2s[:], w2.rearrange("e f d -> f e d")).then_inc(s["weights_loaded"], 16)
                for k in range(3):
                    sp.dma_start(b2s[k * EXPERTS:(k + 1) * EXPERTS], b2).then_inc(s["weights_loaded"], 16)
                sp.wait_ge(s["const_ready"], 1)
                sp.dma_start(xn_d[FLAT:P * FLAT_P].rearrange("(k n) -> k n", k=1), zero_row[0:1, 0:P * FLAT_P - FLAT]).then_inc(s["xn_pad"], 16)
                with sp.Fori(0, B) as b:
                    for h in range(2):
                        sp.dma_start(X[h * CH:(h + 1) * CH].rearrange("p c n -> p (c n)"), pixels(x, b, h)).then_inc(s["x_loaded"], 16)
                    hold(sp, s["normed"], b + 1, s["sp_turns"])
                    for h in range(2):
                        sp.dma_start(xn_img[b, h], D[h * CH:(h + 1) * CH].rearrange("p c n -> p (c n)")).then_inc(s["xn_stored"], 16)
                    hold(sp, s["xn_stored"], b * 32 + 32, s["sp_turns"])
                sp.wait_ge(s["xn_pad"], 16)
                with sp.Fori(0, QCHUNKS) as j:
                    sp.dma_start(F[:], xn_flat[:, j]).then_inc(s["f_loaded"], 16)
                    hold(sp, s["quantised"], j + 1, s["sp_turns"])
                    sp.dma_start(xq_flat[:, j], Fq[:]).then_inc(s["q_stored"], 16)
                    hold(sp, s["q_stored"], j * 16 + 16, s["sp_turns"])
                with sp.Fori(0, B) as b:
                    for h in range(2):
                        r = 0 if h == 0 else HALF_ROWS - 1
                        sp.dma_start(Q[h * CH:(h + 1) * CH, 1 - h:1 - h + HALF_ROWS + 1, 1:WID + 1],
                                     xq_img[b, :, r:r + HALF_ROWS + 1, :]).then_inc(s["c_loaded"], 16)
                        sp.dma_start(X[h * CH:(h + 1) * CH].rearrange("p c n -> p (c n)"), pixels(x, b, h)).then_inc(s["c_loaded"], 16)
                    hold(sp, s["summed"], b + 1, s["sp_turns"])
                    sp.dma_start(x1_d.rearrange("b s c n -> b (s c) n")[b], X[:].rearrange("p c n -> p (c n)")).then_inc(s["c_stored"], 16)
                    hold(sp, s["tokens_ready"], b + 1, s["sp_turns"])
                    sp.dma_start(t_d.rearrange("b s c n -> b (s c) n")[b], D[:].rearrange("p c n -> p (c n)")).then_inc(s["c_stored"], 16)
                    hold(sp, s["rows_ready"], b + 1, s["sp_turns"])
                    for h in range(2):
                        sp.dma_start(node_img[b, h], rows[:, :, h * ROW:(h + 1) * ROW]).then_inc(s["c_stored"], 16)
                    hold(sp, s["c_stored"], b * 64 + 64, s["sp_turns"])
                sp.wait_ge(s["blk_stored"], 16)

            @block.gpsimd
            def _(pool):
                step = Signal(s["pstep"])
                link(pool, pool.memset(ident[:], 0.0), step)
                link(pool, pool.affine_select(out=ident[:], in_=ident[:], compare_op=ALU.not_equal, fill=1.0, base=0,
                                              pattern=[[-1, P]], channel_multiplier=1), step)
                link(pool, pool.tensor_copy(ident_h[:], ident[:]), step)
                link(pool, pool.memset(ones[:], 1.0), step)
                link(pool, pool.affine_select(out=below[:], in_=ones[:], compare_op=ALU.is_gt, fill=0.0, base=0,
                                              pattern=[[1, P]], channel_multiplier=-1), step)
                link(pool, pool.iota(scratch_i[:], pattern=[[1, P]], base=0, channel_multiplier=0), step)
                link(pool, pool.tensor_copy(lane[:], scratch_i[:]), step)
                link(pool, pool.iota(scratch_i[:, 0:ID_W], pattern=[[1, ID_W]], base=0, channel_multiplier=ID_W), step)
                link(pool, pool.tensor_copy(tile_no[:], scratch_i[:, 0:ID_W]), step)
                link(pool, pool.memset(zero_row[:], 0.0), step)
                link(pool, pool.memset(halves[:], 0.0), step)
                for h in range(2):
                    link(pool, pool.memset(halves[h * CH:(h + 1) * CH, h * CH:(h + 1) * CH], 1.0 / CH), step)
                link(pool, pool.memset(eps_c[:], 1e-6), step)
                link(pool, pool.memset(eps_t[:], 1e-5), step)
                link(pool, pool.memset(Q[:], 0.0), step)
                link(pool, pool.memset(cw_bd[:], 0.0), step)
                link(pool, pool.memset(zero_h[:], 0.0), step)
                link(pool, pool.memset(pad_rec[:, :, 0:1], 0), step)
                link(pool, pool.memset(pad_rec[:, :, 1:2], PAD_DST), step)
                link(pool, pool.memset(pick[:], 0.0), step)
                for r in range(3):
                    link(pool, pool.affine_select(out=pick[:], in_=pick[:], compare_op=ALU.not_equal, fill=1.0, base=-r * EXPERTS,
                                                  pattern=[[-1, EXPERTS], [0, P]], channel_multiplier=1), step)
                pool.memset(scratch_i[:], 0).then_inc(s["const_ready"], 1)
                for k in range(8):
                    pool.dma_start(edge_d.rearrange("(p k c) r -> p k (c r)", p=P, k=8)[:, k],
                                   pad_rec[:].rearrange("p c r -> p (c r)")).then_inc(s["pads_written"], 16)


                pool.wait_ge(s["pads_written"], 8 * 16)
                ROUND = BUFS * SEND
                per_rank = RANK_COLS // ROUND

                def send_round(i, first):
                    for k in range(BUFS):
                        if not first:
                            pool.wait_ge(sent[k], i * (SEND * 16))
                        col = (i * BUFS + k) * SEND
                        pool.tensor_copy(rec_slots[:, k], rec[:, bass.ds(col, SEND), :]).then_inc(s["pstep"], 1)
                        step.k += 1
                        link(pool, pool.tensor_copy(slots[:, k, :].bitcast(I32), pos_i[:, bass.ds(col, SEND)]), step)
                        pool.sem_inc(s["pool_turns"], 1)
                        for c in range(SEND):
                            pool.indirect_dma_start(edge_d, bass.IndirectOffsetOnAxis(ap=slots[:, k, c:c + 1], axis=0),
                                                    rec_slots[:, k, c, :], None).then_inc(sent[k], 16)
                for r in range(ECOLS // RANK_COLS):
                    pool.wait_ge(s["ranked"], r + 1)
                    lo = r * per_rank
                    if r == 0:
                        send_round(0, True)
                        lo += 1
                    with rolled(pool, lo, (r + 1) * per_rank, step, 2 * BUFS) as i:
                        send_round(i, False)
                for k in range(BUFS):
                    pool.wait_ge(sent[k], ECOLS // BUFS * 16)

            def mean_of(pe, src_t, dst_ps, done):
                for c in range(CHUNKS):
                    mm = pe.matmul(dst_ps[:, c, 0:CHUNK], halves[:], src_t[:, c, :], start=True, stop=True)
                mm.then_inc(done, 1)

            @block.tensor
            def _(pe):
                pe.wait_ge(s["const_ready"], 1)
                pe.wait_ge(s["counted"], 1)
                pe.matmul(A[:, 0, 0:NB], below[:], count[:], start=True, stop=True)
                pe.matmul(A[:, 1, 0:NB], ones[:], count[:], start=True, stop=True).then_inc(s["prefix_ready"], 1)
                pe.wait_ge(s["w_blocks"], 1)
                for t in range(TAPS):
                    mm = pe.transpose(C[:].bitcast(BF16)[:, t // 4, (t % 4) * P:(t % 4 + 1) * P], cw_bd[:, t, :], ident_h[:])
                mm.then_inc(s["w_turned"], 1)
                pe.wait_ge(s["w_ready"], 1)
                with pe.Fori(0, B) as b:
                    pe.wait_ge(s["x_loaded"], b * 32 + 32)
                    mean_of(pe, X, A, s["mean_ready"])
                    pe.wait_ge(s["squared"], b + 1)
                    mean_of(pe, S, C, s["var_ready"])
                with pe.Fori(0, B) as b:
                    pe.wait_ge(s["c_loaded"], b * 64 + 64)
                    for c in range(CHUNKS):
                        for t in range(TAPS):
                            r0 = c * CHUNK_ROWS + t // 3
                            mm = pe.matmul(A[:, c, 0:CHUNK], cw_t[:, t, :], Q[:, r0:r0 + CHUNK_ROWS, t % 3:t % 3 + WID],
                                           start=(t == 0), stop=(t == TAPS - 1))
                    mm.then_inc(s["conv_done"], 1)
                    pe.wait_ge(s["summed"], b + 1)
                    mean_of(pe, X, C, s["mean2_ready"])
                    pe.wait_ge(s["squared2"], b + 1)
                    mean_of(pe, S, A, s["var2_ready"])
                    pe.wait_ge(s["tokens_ready"], b + 1)
                    tokens = D[:].rearrange("p c n -> p (c n)")
                    for j in range(TOK_TILES):
                        mm = pe.matmul(C[0:TOK, j // 7, (j % 7) * 2 * ROW:(j % 7 + 1) * 2 * ROW],
                                       tokens[:, j * TOK:(j + 1) * TOK], proj[:].rearrange("p s f -> p (s f)"), start=True, stop=True)
                    mm.then_inc(s["projected"], 1)

            @block.scalar
            def _(act):
                act.wait_ge(s["const_ready"], 1)
                act.wait_ge(s["blocks_ready"], 1)
                act.dma_start(blk_d.rearrange("(p k) -> p k", p=P), tile_blk_i[:]).then_inc(s["blk_stored"], 16)
                with act.Fori(0, B) as b:
                    act.wait_ge(s["centred"], b + 1)
                    act.activation(S[:], D[:], ACT.Square).then_inc(s["squared"], 1)
                    act.wait_ge(s["var_ready"], b + 1)
                    act.activation(S[:], C[:, :, 0:CHUNK], ACT.Sqrt, bias=eps_c[:]).then_inc(s["deviated"], 1)
                with act.Fori(0, B) as b:
                    act.wait_ge(s["centred2"], b + 1)
                    act.activation(S[:], D[:], ACT.Square).then_inc(s["squared2"], 1)
                    act.wait_ge(s["var2_ready"], b + 1)
                    act.activation(S[:], A[:, :, 0:CHUNK], ACT.Sqrt, bias=eps_t[:]).then_inc(s["deviated2"], 1)
                    act.wait_ge(s["projected"], b + 1)
                    act.copy(rows[:].rearrange("p (k j) f -> p k (j f)", k=2), C[0:TOK, 0:2, 0:14 * ROW]).then_inc(s["rows_ready"], 1)

            @block.vector
            def _(dve):
                step = Signal(s["vstep"])

                def L(instr):
                    link(dve, instr, step)

                dve.wait_ge(s["const_ready"], 1)
                dve.wait_ge(s["edges_loaded"], 32)
                L(dve.tensor_copy(rec[:, :, 0], src[:]))
                L(dve.tensor_copy(rec[:, :, 1], dst[:]))
                L(dve.tensor_scalar(pos_i[:], dst[:], BLK_BITS, None, ALU.arith_shift_right))
                L(dve.tensor_copy(blk_h[:], pos_i[:]))
                for b in range(NB):
                    L(dve.tensor_scalar(mask_h[:], blk_h[:], float(b), None, ALU.is_equal, ALU.add, accum_out=count[:, b:b + 1]))
                dve.engine_nop().then_inc(s["counted"], 1)

                dve.wait_ge(s["prefix_ready"], 1)
                L(dve.tensor_scalar(total_i[:], A[:, 1, 0:NB], float(P - 1), None, ALU.add))
                L(dve.tensor_scalar(total_i[:], total_i[:], LO_BITS, None, ALU.arith_shift_right))
                L(dve.tensor_copy(tiles_b[:], total_i[:]))
                L(dve.tensor_tensor_scan(end_b[:], tiles_b[:], zero_row[:, 0:NB], 0.0, ALU.add, ALU.add))
                L(dve.tensor_tensor(start_b[:], end_b[:], tiles_b[:], ALU.subtract))
                L(dve.tensor_scalar(start_b[:], start_b[:], float(P), -1.0, ALU.mult, ALU.add))
                L(dve.tensor_tensor(start_b[:], start_b[:], A[:, 0, 0:NB], ALU.add))
                L(dve.tensor_tensor(passed[:], end_b[:].rearrange("p (k n) -> p k n", k=1).broadcast_to([P, ID_W, NB]),
                                    tile_no[:].rearrange("p (n k) -> p n k", k=1).broadcast_to([P, ID_W, NB]), ALU.is_le))
                L(dve.tensor_reduce(tile_blk[:], passed[:], AX.X, ALU.add))
                L(dve.tensor_scalar(tile_blk_i[:], tile_blk[:], float(NB - 1), float(HI), ALU.min, ALU.mult))
                dve.engine_nop().then_inc(s["blocks_ready"], 1)

                for r in range(ECOLS // RANK_COLS):
                    cols = slice(r * RANK_COLS, (r + 1) * RANK_COLS)
                    L(dve.memset(pos[:, cols], 0.0))
                    for b in range(NB):
                        L(dve.tensor_scalar(mask_h[:, 0:RANK_COLS], blk_h[:, cols], float(b), None, ALU.is_equal))
                        L(dve.tensor_tensor_scan(run[:], mask_h[:, 0:RANK_COLS], zero_h[:], start_b[:, b:b + 1], ALU.add, ALU.add))
                        L(dve.copy_predicated(pos[:, cols], mask_h[:, 0:RANK_COLS].bitcast(U16), run[:]))
                        L(dve.tensor_copy(start_b[:, b:b + 1], run[:, RANK_COLS - 1:RANK_COLS]))
                    L(dve.tensor_copy(pos_i[:, cols], pos[:, cols]))
                    L(dve.tensor_scalar(dst[:, cols], pos_i[:, cols], P - 1, None, ALU.bitwise_and))
                    L(dve.tensor_scalar(pos_i[:, cols], pos_i[:, cols], LO_BITS, None, ALU.arith_shift_right))
                    L(dve.scalar_tensor_tensor(out=pos[:, cols], in0=dst[:, cols], scalar=float(TILES), in1=pos_i[:, cols], op0=ALU.mult, op1=ALU.add))
                    L(dve.tensor_copy(pos_i[:, cols], pos[:, cols]))
                    dve.engine_nop().then_inc(s["ranked"], 1)

                def quantise(vals, whole, quant, n):
                    def wide(v):
                        return v.rearrange("p (n k) -> p n k", k=1).broadcast_to([P, n, GROUP])
                    L(dve.tensor_reduce(gmax[:, 0:n], vals, AX.X, ALU.max, apply_absolute_value=True))
                    L(dve.tensor_scalar(gmax[:, 0:n], gmax[:, 0:n], TINY, None, ALU.max))
                    L(dve.tensor_scalar(gscale[:, 0:n].bitcast(I32), gmax[:, 0:n].bitcast(I32), EXP_BITS, None, ALU.bitwise_and))
                    L(dve.tensor_scalar(ginv[:, 0:n].bitcast(I32), gscale[:, 0:n].bitcast(I32), -1.0, float(INV_BITS), ALU.mult, ALU.add))
                    L(dve.tensor_scalar(ginv[:, 0:n], ginv[:, 0:n], 128.0, None, ALU.mult))
                    L(dve.tensor_scalar(gscale[:, 0:n], gscale[:, 0:n], 1.0 / 128.0, None, ALU.mult))
                    L(dve.tensor_tensor(vals, vals, wide(ginv[:, 0:n]), ALU.mult))
                    L(dve.tensor_scalar(vals, vals, MAGIC, MAGIC + 127.0, ALU.add, ALU.min))
                    L(dve.tensor_scalar(whole, vals, MAGIC - 128.0, MAGIC, ALU.max, ALU.subtract))
                    return dve.tensor_tensor(quant, whole, wide(gscale[:, 0:n]), ALU.mult)

                dve.wait_ge(s["weights_loaded"], 16 * WEIGHT_LOADS)
                v = cw[:].rearrange("p (n i) t -> p n (i t)", i=GROUP // TAPS)
                vq = cwq[:].rearrange("p (n i) t -> p n (i t)", i=GROUP // TAPS)
                L(quantise(v, vq, vq, CH * TAPS // GROUP))
                for h in range(2):
                    L(dve.tensor_copy(cw_bd[h * CH:(h + 1) * CH, :, h * CH:(h + 1) * CH],
                                      cwq[h * CH:(h + 1) * CH].rearrange("p i t -> p t i")))
                for h in range(2):
                    L(dve.memset(proj[(1 - h) * CH:(2 - h) * CH, h, :], 0.0))
                for h in range(2):
                    a = slice(h * CH, (h + 1) * CH)
                    for k in range(2):
                        L(dve.tensor_tensor(attw[a, :], proj[a, h, 0:FEAT], att[a, k, :], ALU.mult))
                        L(dve.tensor_reduce(proj[a, h, FEAT + k * HEADS:FEAT + (k + 1) * HEADS],
                                            attw[a, :].rearrange("p (h d) -> p h d", h=HEADS), AX.X, ALU.add))
                dve.engine_nop().then_inc(s["w_blocks"], 1)
                dve.wait_ge(s["w_turned"], 1)
                L(dve.tensor_copy(cw_t[:, 0:8].rearrange("p (b t) o -> p b (t o)", b=2), C[:].bitcast(BF16)[:, 0:2, 0:512]))
                dve.tensor_copy(cw_t[:, 8], C[:].bitcast(BF16)[:, 2, 0:P]).then_inc(s["w_ready"], 1)

                with rolled(dve, 0, B, step, 1) as b:
                    dve.wait_ge(s["mean_ready"], b + 1)
                    dve.tensor_tensor(D[:], X[:], A[:, :, 0:CHUNK], ALU.subtract).then_inc(s["centred"], 1)
                    dve.wait_ge(s["deviated"], b + 1)
                    L(dve.reciprocal(S[:], S[:]))
                    dve.tensor_tensor(D[:], D[:], S[:], ALU.mult).then_inc(s["normed"], 1)
                with rolled(dve, 0, QCHUNKS, step, 9) as j:
                    dve.wait_ge(s["f_loaded"], j * 16 + 16)
                    quantise(F[:], Fq[:], Fq[:], QGROUPS).then_inc(s["quantised"], 1)
                with rolled(dve, 0, B, step, 1) as b:
                    dve.wait_ge(s["conv_done"], b + 1)
                    dve.scalar_tensor_tensor(out=X[:], in0=A[:, :, 0:CHUNK], scalar=cbias[:], in1=X[:],
                                             op0=ALU.add, op1=ALU.add).then_inc(s["summed"], 1)
                    dve.wait_ge(s["mean2_ready"], b + 1)
                    dve.tensor_tensor(D[:], X[:], C[:, :, 0:CHUNK], ALU.subtract).then_inc(s["centred2"], 1)
                    dve.wait_ge(s["deviated2"], b + 1)
                    L(dve.reciprocal(S[:], S[:]))
                    dve.tensor_tensor(D[:], D[:], S[:], ALU.mult).then_inc(s["tokens_ready"], 1)

        with ExitStack() as ph:
            def tb(name, shape, dt=F32):
                return ph.enter_context(nc.sbuf_tensor(name, shape, dt))

            nodes = tb("nodes", [P, NQ, ROW])
            acc = tb("acc", [P, NQ, VALS])
            srt = tb("srt", [P, TILES + G, 2], I32)
            lo = tb("lo", [P, TILES + G])
            hi = tb("hi", [P, TILES + G])
            bits = tb("bits", [P, TILES + G], I32)
            blk_row = tb("blk_row", [1, P * ID_W], I32)
            amax = tb("amax", [P, HEADS])
            amax_t = tb("amax_t", [HEADS, 1])
            amax_d = tb("amax_d", [HEADS, HEADS])
            na = tb("na", [P, NQ, HEADS])
            nb = tb("nb", [P, NQ, HEADS])
            lo_hot = tb("lo_hot", [P, BUFS, G, P])
            hi_hot = tb("hi_hot", [P, BUFS, G, HI])
            lo_hot_t = tb("lo_hot_t", [P, G, P])
            gath = tb("gath", [P, BUFS, G, ROW])
            places = tb("places", [P, BUFS, G], U32)
            picked = tb("picked", [P, G, HEADS, HI])
            adst = tb("adst", [P, G, HEADS])
            shift = tb("shift", [P, G, HEADS])
            logit = tb("logit", [P, G, HEADS])
            weight = tb("weight", [P, G, HEADS])
            vals = tb("vals", [P, G, VALS])
            spread = tb("spread", [P, G, HI, VALS])
            gate_rows = tb("gate_rows", [GQ * 3 * EXPERTS, 4, P], BF16)
            s = sems(
                "nodes_loaded sorted_loaded vstep2 amax_rows amax_turned amax_diag amax_spread self_logits self_weights "
                "lo_hot_ready turned turned_copied picked_ready picked_read logits_ready weights_ready rows_used "
                "spread_ready scattered acc_ready places_ready pool_turns2 "
                "squares_ready sqvar_ready sqrt_ready exp_in exp_ready gates_split gates_turned gates_copied gates_stored"
            )
            gathered = [ctx.enter_context(nc.semaphore(f"gathered{k}")) for k in range(BUFS)]
            gate_stored = [ctx.enter_context(nc.semaphore(f"gate_stored{k}")) for k in range(4)]
            block = ph.enter_context(nc.Block())

            parts = nodes[:].rearrange("p q f -> p (q f)")[:, 0:NQ * 3 * EXPERTS // 2].bitcast(BF16).rearrange("p (q e) -> p q e", e=3 * EXPERTS)

            def over_nodes(v, n):
                return v.rearrange("p (k f) -> p k f", k=1).broadcast_to([P, NQ, n])

            def bank_of(j):
                return j // 3, (j % 3) * HI * VALS

            @block.sync
            def _(sp):
                sp.dma_start(srt[:, 0:TILES, :].rearrange("p c k -> p (c k)"), edge_d.rearrange("(p c) k -> p (c k)", p=P)).then_inc(s["sorted_loaded"], 16)
                sp.dma_start(blk_row[:], blk_d.rearrange("(k n) -> k n", k=1)).then_inc(s["sorted_loaded"], 16)
                for k in range(4):
                    n = NQ // 4
                    sp.dma_start(nodes[:, k * n:(k + 1) * n, :], node_d.rearrange("(q l) f -> l q f", l=P)[:, k * n:(k + 1) * n, :]).then_inc(s["nodes_loaded"], 16)
                for k in range(NQ // GQ):
                    sp.wait_ge(s["gates_copied"], k + 1)
                    sp.dma_start(gate_d[k].rearrange("q e l -> (q e) l"), gate_rows[:, k % 4, :]).then_inc(gate_stored[k % 4], 16)
                for k in range(4):
                    sp.wait_ge(gate_stored[k], 16 * len(range(k, NQ // GQ, 4)))

            @block.gpsimd
            def _(pool):
                step = Signal(s["places_ready"])
                pool.wait_ge(s["sorted_loaded"], 32)
                pool.wait_ge(s["nodes_loaded"], 64)

                def gather(i, k):
                    if not (isinstance(i, int) and i == 0):
                        pool.wait_ge(s["rows_used"], (i - 1) * BUFS + k + 1)
                    link(pool, pool.tensor_copy(places[:, k, :].bitcast(I32), srt[:, bass.ds((i * BUFS + k) * G, G), 0]), step)
                    pool.sem_inc(s["pool_turns2"], 1)
                    for j in range(G):
                        pool.indirect_dma_start(gath[:, k, j, :], None, node_d,
                                                bass.IndirectOffsetOnAxis(ap=places[:, k, j:j + 1], axis=0)).then_inc(gathered[k], 16)
                for k in range(BUFS):
                    gather(0, k)
                with rolled(pool, 1, NG // BUFS, step, BUFS) as i:
                    for k in range(BUFS):
                        gather(i, k)

            @block.scalar
            def _(act):
                act.wait_ge(s["self_logits"], 1)
                act.activation(nb[:], nb[:], ACT.Exp).then_inc(s["self_weights"], 1)

                def turned_copy(g):
                    act.wait_ge(s["turned"], g + 1)
                    if not (isinstance(g, int) and g == 0):
                        act.wait_ge(s["picked_ready"], g)
                    for c in range(2):
                        act.copy(lo_hot_t[:, c * 4:c * 4 + 4, :].rearrange("p t e -> p (t e)"), A[:, c, :]).then_inc(s["turned_copied"], 1)

                def weigh(g):
                    act.wait_ge(s["logits_ready"], g + 1)
                    act.activation(weight[:], logit[:], ACT.Exp).then_inc(s["weights_ready"], 1)

                turned_copy(0)
                for g in range(BUFS):
                    weigh(g)
                    turned_copy(g + 1)
                with act.Fori(1, NG // BUFS) as i:
                    for k in range(BUFS):
                        weigh(i * BUFS + k)
                        turned_copy(i * BUFS + k + 1)
                act.wait_ge(s["squares_ready"], 1)
                act.activation(acc[:, :, 0:FEAT], nodes[:, :, 0:FEAT], ACT.Square).then_inc(s["sqvar_ready"], 1)
                act.wait_ge(s["squares_ready"], 2)
                act.activation(na[:, :, 1], na[:, :, 0], ACT.Sqrt, bias=eps_t[:], scale=1.0 / FEAT).then_inc(s["sqrt_ready"], 1)
                act.wait_ge(s["exp_in"], 1)
                act.activation(nb[:], nb[:], ACT.Exp).then_inc(s["exp_ready"], 1)

            @block.tensor
            def _(pe):
                pe.wait_ge(s["amax_rows"], 1)
                pe.transpose(C[0:HEADS, 3, 0:P], amax[:], ident[:]).then_inc(s["amax_turned"], 1)
                pe.wait_ge(s["amax_diag"], 1)
                pe.matmul(A[:, 3, 0:HEADS], ones[0:HEADS, :], amax_d[:], start=True, stop=True).then_inc(s["amax_spread"], 1)

                def turn(g, k):
                    pe.wait_ge(s["lo_hot_ready"], g + 1)
                    if not (isinstance(g, int) and g == 0):
                        pe.wait_ge(s["turned_copied"], g * 2)
                    for j in range(G):
                        mm = pe.transpose(A[:, j // 4, (j % 4) * P:(j % 4 + 1) * P], lo_hot[:, k, j, :], ident[:])
                    mm.then_inc(s["turned"], 1)

                def pick_dst(g):
                    pe.wait_ge(s["turned_copied"], g * 2 + 2)
                    if not (isinstance(g, int) and g == 0):
                        pe.wait_ge(s["picked_read"], g)
                    for j in range(G):
                        q = pe.value_load(blk_row[0:1, bass.ds(g * G + j, 1)], min_val=0, max_val=NQ - HI)
                        mm = pe.matmul(A[:, 2, j * HI * HEADS:(j + 1) * HI * HEADS], lo_hot_t[:, j, :],
                                       nodes[:, bass.ds(q, HI), FEAT + HEADS:ROW], start=True, stop=True)
                    mm.then_inc(s["picked_ready"], 1)

                def scatter(g, k):
                    pe.wait_ge(s["spread_ready"], g + 1)
                    for j in range(G):
                        bank, at = bank_of(j)
                        mm = pe.matmul(C[:, bank, at:at + HI * VALS], lo_hot[:, k, j, :],
                                       spread[:, j].rearrange("p h v -> p (h v)"), start=True, stop=True)
                        if j % 3 == 2 or j == G - 1:
                            mm.then_inc(s["scattered"], 1)

                pe.wait_ge(s["sorted_loaded"], 32)
                pe.wait_ge(s["nodes_loaded"], 64)
                turn(0, 0)
                pick_dst(0)
                for g in range(BUFS):
                    turn(g + 1, (g + 1) % BUFS)
                    pick_dst(g + 1)
                    scatter(g, g)
                with pe.Fori(1, NG // BUFS) as i:
                    for k in range(BUFS):
                        g = i * BUFS + k
                        turn(g + 1, (k + 1) % BUFS)
                        pick_dst(g + 1)
                        scatter(g, k)
                for k in range(NQ // GQ):
                    if k == 0:
                        pe.wait_ge(s["gates_split"], 1)
                    if k >= 4:
                        pe.wait_ge(s["gates_copied"], k - 3)
                    pe.transpose(A[0:GQ * 3 * EXPERTS, k % 4, 0:P // 2].bitcast(BF16), parts[:, k * GQ:(k + 1) * GQ, :].rearrange("p q e -> p (q e)"), ident_h[:]).then_inc(s["gates_turned"], 1)


            @block.vector
            def _(dve):
                step = Signal(s["vstep2"])

                def L(instr):
                    link(dve, instr, step)

                L(dve.memset(srt[:, TILES:TILES + G, :], 0))
                dve.wait_ge(s["sorted_loaded"], 32)
                L(dve.tensor_scalar(bits[:], srt[:, :, 1], P - 1, None, ALU.bitwise_and))
                L(dve.tensor_copy(lo[:], bits[:]))
                L(dve.tensor_scalar(bits[:], srt[:, :, 1], LO_BITS, HI - 1, ALU.arith_shift_right, ALU.bitwise_and))
                L(dve.tensor_copy(hi[:], bits[:]))
                L(dve.tensor_scalar(bits[:], srt[:, :, 1], PAD_DST.bit_length() - 1, None, ALU.arith_shift_right))
                L(dve.scalar_tensor_tensor(out=hi[:], in0=bits[:], scalar=float(HI), in1=hi[:], op0=ALU.mult, op1=ALU.add))

                dve.wait_ge(s["nodes_loaded"], 64)
                a_src, a_dst = nodes[:, :, FEAT:FEAT + HEADS], nodes[:, :, FEAT + HEADS:ROW]
                dve.tensor_reduce(amax[:], a_src.rearrange("p q f -> p f q"), AX.X, ALU.max).then_inc(s["amax_rows"], 1)
                dve.wait_ge(s["amax_turned"], 1)
                L(dve.tensor_reduce(amax_t[:], C[0:HEADS, 3, 0:P], AX.X, ALU.max))
                dve.tensor_scalar(amax_d[:], ident[0:HEADS, 0:HEADS], amax_t[:], None, ALU.mult).then_inc(s["amax_diag"], 1)
                dve.wait_ge(s["amax_spread"], 1)
                L(dve.tensor_copy(amax[:], A[:, 3, 0:HEADS]))

                def leaky(out_t, v):
                    return dve.scalar_tensor_tensor(out=out_t, in0=v, scalar=0.2, in1=v, op0=ALU.mult, op1=ALU.max)

                L(dve.tensor_tensor(na[:], a_dst, over_nodes(amax[:], HEADS), ALU.add))
                L(leaky(na[:], na[:]))
                L(dve.tensor_tensor(nb[:], a_src, a_dst, ALU.add))
                L(leaky(nb[:], nb[:]))
                dve.tensor_tensor(nb[:], nb[:], na[:], ALU.subtract).then_inc(s["self_logits"], 1)
                dve.wait_ge(s["self_weights"], 1)
                L(dve.tensor_copy(acc[:, :, FEAT:VALS], nb[:]))
                for h in range(HEADS):
                    L(dve.tensor_tensor(acc[:, :, h * DIM:(h + 1) * DIM], nodes[:, :, h * DIM:(h + 1) * DIM],
                                        nb[:, :, h:h + 1].broadcast_to([P, NQ, DIM]), ALU.mult))

                def per_edge(v):
                    return v.rearrange("p (k f) -> p k f", k=1).broadcast_to([P, G, HEADS])

                def one_hots(g, k):
                    L(dve.tensor_tensor(hi_hot[:, k], lane[:, 0:HI].rearrange("p (k h) -> p k h", k=1).broadcast_to([P, G, HI]),
                                        hi[:, bass.ds(g * G, G)].rearrange("p (t k) -> p t k", k=1).broadcast_to([P, G, HI]), ALU.is_equal))
                    dve.tensor_tensor(lo_hot[:, k], lane[:].rearrange("p (k h) -> p k h", k=1).broadcast_to([P, G, P]),
                                      lo[:, bass.ds(g * G, G)].rearrange("p (t k) -> p t k", k=1).broadcast_to([P, G, P]),
                                      ALU.is_equal).then_inc(s["lo_hot_ready"], 1)

                def logits(g, i, k):
                    dve.wait_ge(s["picked_ready"], g + 1)
                    dve.tensor_tensor(picked[:], A[:, 2, 0:G * HI * HEADS].rearrange("p (t h f) -> p t f h", t=G, h=HI),
                                      hi_hot[:, k].rearrange("p t (k h) -> p t k h", k=1).broadcast_to([P, G, HEADS, HI]),
                                      ALU.mult).then_inc(s["picked_read"], 1)
                    dve.wait_ge(s["picked_read"], g + 1)
                    L(dve.tensor_reduce(adst[:], picked[:], AX.X, ALU.add))
                    L(dve.tensor_tensor(shift[:], adst[:], per_edge(amax[:]), ALU.add))
                    L(leaky(shift[:], shift[:]))
                    dve.wait_ge(gathered[k], (i + 1) * (G * 16))
                    L(dve.tensor_tensor(adst[:], adst[:], gath[:, k, :, FEAT:FEAT + HEADS], ALU.add))
                    L(leaky(adst[:], adst[:]))
                    dve.tensor_tensor(logit[:], adst[:], shift[:], ALU.subtract).then_inc(s["logits_ready"], 1)

                def add_up(g):
                    for j in range(G):
                        bank, at = bank_of(j)
                        if j % 3 == 0:
                            dve.wait_ge(s["scattered"], g * 3 + bank + 1)
                        q = dve.value_load(blk_row[0:1, bass.ds(g * G + j, 1)], min_val=0, max_val=NQ - HI)
                        L(dve.tensor_tensor(acc[:, bass.ds(q, HI), :], acc[:, bass.ds(q, HI), :],
                                            C[:, bank, at:at + HI * VALS].rearrange("p (h v) -> p h v", h=HI), ALU.add))

                def spread_out(g, k):
                    dve.wait_ge(s["weights_ready"], g + 1)
                    L(dve.tensor_copy(vals[:, :, FEAT:VALS], weight[:]))
                    h4 = vals[:, :, 0:FEAT].rearrange("p t (h d) -> p t h d", h=HEADS)
                    dve.tensor_tensor(h4, gath[:, k, :, 0:FEAT].rearrange("p t (h d) -> p t h d", h=HEADS),
                                      weight[:].rearrange("p t (h k) -> p t h k", k=1).broadcast_to([P, G, HEADS, DIM]),
                                      ALU.mult).then_inc(s["rows_used"], 1)
                    dve.wait_ge(s["rows_used"], g + 1)
                    dve.tensor_tensor(spread[:], hi_hot[:, k].rearrange("p t (h k) -> p t h k", k=1).broadcast_to([P, G, HI, VALS]),
                                      vals[:].rearrange("p t (k v) -> p t k v", k=1).broadcast_to([P, G, HI, VALS]),
                                      ALU.mult).then_inc(s["spread_ready"], 1)

                def body(i, k, first):
                    g = i * BUFS + k
                    logits(g, i, k)
                    if not first:
                        add_up(g - 1)
                    one_hots(g + 1, (k + 1) % BUFS)
                    spread_out(g, k)

                one_hots(0, 0)
                for k in range(BUFS):
                    body(0, k, k == 0)
                with rolled(dve, 1, NG // BUFS, step, BUFS * (5 + G + 2)) as i:
                    for k in range(BUFS):
                        body(i, k, False)
                add_up(NG - 1)

                agg, den = acc[:, :, 0:FEAT], acc[:, :, FEAT:VALS]
                L(dve.tensor_scalar(na[:], den, 1e-16, None, ALU.add))
                L(dve.reciprocal(nb[:], na[:]))
                dev = nodes[:, :, 0:FEAT]
                for h in range(HEADS):
                    L(dve.tensor_tensor(dev[:, :, h * DIM:(h + 1) * DIM], agg[:, :, h * DIM:(h + 1) * DIM],
                                        nb[:, :, h:h + 1].broadcast_to([P, NQ, DIM]), ALU.mult))
                L(dve.tensor_tensor(dev, dev, over_nodes(vecs[:, 0, :], FEAT), ALU.add))
                L(dve.tensor_reduce(na[:, :, 0], dev, AX.X, ALU.add))
                L(dve.tensor_scalar(na[:, :, 1], na[:, :, 0], 1.0 / FEAT, None, ALU.mult))
                dve.tensor_tensor(dev, dev, na[:, :, 1:2].broadcast_to([P, NQ, FEAT]), ALU.subtract).then_inc(s["squares_ready"], 1)
                dve.wait_ge(s["sqvar_ready"], 1)
                dve.tensor_reduce(na[:, :, 0], agg, AX.X, ALU.add).then_inc(s["squares_ready"], 1)
                dve.wait_ge(s["sqrt_ready"], 1)
                L(dve.reciprocal(na[:, :, 2], na[:, :, 1]))
                L(dve.tensor_tensor(dev, dev, na[:, :, 2:3].broadcast_to([P, NQ, FEAT]), ALU.mult))
                L(dve.tensor_tensor(dev, dev, over_nodes(vecs[:, 1, :], FEAT), ALU.mult))
                L(dve.tensor_tensor(dev, dev, over_nodes(vecs[:, 2, :], FEAT), ALU.add))
                L(dve.tensor_reduce(na[:], dev.rearrange("p q (h d) -> p q d h", h=HEADS), AX.X, ALU.add))
                L(dve.tensor_scalar(na[:], na[:], 1.0 / HEADS, None, ALU.mult))
                rank, beat = acc[:, :, 0:EXPERTS], acc[:, :, EXPERTS]
                for e in range(EXPERTS):
                    L(dve.memset(rank[:, :, e], float(EXPERTS - 1 - e)))
                for e in range(EXPERTS):
                    for f in range(e + 1, EXPERTS):
                        L(dve.tensor_tensor(beat, na[:, :, e], na[:, :, f], ALU.is_ge))
                        L(dve.tensor_tensor(rank[:, :, e], rank[:, :, e], beat, ALU.subtract))
                        L(dve.tensor_tensor(rank[:, :, f], rank[:, :, f], beat, ALU.add))
                top, total = acc[:, :, EXPERTS], acc[:, :, EXPERTS + 1]
                L(dve.tensor_reduce(top, na[:], AX.X, ALU.max))
                dve.tensor_tensor(nb[:], na[:], acc[:, :, EXPERTS:EXPERTS + 1].broadcast_to([P, NQ, EXPERTS]), ALU.subtract).then_inc(s["exp_in"], 1)
                dve.wait_ge(s["exp_ready"], 1)
                L(dve.tensor_scalar(rank, rank, 1.5, None, ALU.is_lt))
                L(dve.tensor_tensor(nb[:], nb[:], rank, ALU.mult))
                L(dve.tensor_reduce(total, nb[:], AX.X, ALU.add))
                L(dve.reciprocal(top, total))
                L(dve.tensor_tensor(nb[:], nb[:], acc[:, :, EXPERTS:EXPERTS + 1].broadcast_to([P, NQ, EXPERTS]), ALU.mult))
                for r in range(3):
                    part = parts[:, :, r * EXPERTS:(r + 1) * EXPERTS]
                    if r < 2:
                        L(dve.tensor_copy(part, nb[:]))
                        L(dve.tensor_tensor(nb[:], nb[:], part, ALU.subtract))
                    else:
                        dve.tensor_copy(part, nb[:]).then_inc(s["gates_split"], 1)
                for k in range(NQ // GQ):
                    dve.wait_ge(s["gates_turned"], k + 1)
                    if k >= 4:
                        dve.wait_ge(gate_stored[k % 4], 16 * (k // 4))
                    dve.tensor_copy(gate_rows[:, k % 4, :], A[0:GQ * 3 * EXPERTS, k % 4, 0:P // 2].bitcast(BF16)).then_inc(s["gates_copied"], 1)

        with ExitStack() as ph:
            def tb(name, shape, dt=F32):
                return ph.enter_context(nc.sbuf_tensor(name, shape, dt))

            gate_t = tb("gate_t", [3 * EXPERTS, 2, PAIR_Q, P], BF16)
            T = tb("T", [P, 2, CHUNKS, CHUNK])
            X1 = tb("X1", [P, 2, CHUNKS, CHUNK])
            hid = tb("hid", [P, 2, CHUNK])
            s = sems("b2_split vstep3 pair_loaded hidden gelu_ready gate_ready gated expert_done summed3 out_stored sp_turns3")
            block = ph.enter_context(nc.Block())
            PAIRS = B // 2
            UNITS = 2 * CHUNKS * 2
            STEPS = UNITS * EXPERTS

            def unit(u):
                return u // (2 * CHUNKS), u // 2 % CHUNKS, u % 2

            @block.sync
            def _(sp):
                def load(p, buf, done):
                    sp.dma_start(gate_t[:, buf], gate_d.rearrange("k q e l -> e (k q) l")[:, bass.ds(p * PAIR_Q, PAIR_Q), :]).then_inc(done, 16)
                    for i in range(2):
                        sp.dma_start(T[:, i].rearrange("p c n -> p (c n)"), t_d.rearrange("b s c n -> b (s c) n")[p * 2 + i]).then_inc(done, 16)
                        sp.dma_start(X1[:, i].rearrange("p c n -> p (c n)"), x1_d.rearrange("b s c n -> b (s c) n")[p * 2 + i]).then_inc(done, 16)
                with sp.Fori(0, PAIRS) as p:
                    load(p, 0, s["pair_loaded"])
                    for i in range(2):
                        hold(sp, s["summed3"], p * (UNITS // 2) + (i + 1) * CHUNKS, s["sp_turns3"])
                        for h in range(2):
                            sp.dma_start(pixels(out, p * 2 + i, h), X1[h * CH:(h + 1) * CH, i].rearrange("p c n -> p (c n)")).then_inc(s["out_stored"], 16)
                    hold(sp, s["out_stored"], p * 64 + 64, s["sp_turns3"])

            @block.scalar
            def _(act):
                with act.Fori(0, PAIRS) as p:
                    for k in range(STEPS):
                        e = k % EXPERTS
                        act.wait_ge(s["hidden"], p * STEPS + k + 1)
                        if k >= 2:
                            act.wait_ge(s["expert_done"], p * STEPS + k - 1)
                        act.activation(hid[:, k % 2, :], A[:, k % 2, 0:CHUNK], ACT.Gelu, bias=b1s[:, e:e + 1]).then_inc(s["gelu_ready"], 1)

            @block.tensor
            def _(pe):
                def up(p, k):
                    (i, c, h), e = unit(k // EXPERTS), k % EXPERTS
                    a = slice(h * CH, (h + 1) * CH)
                    if k >= 2:
                        pe.wait_ge(s["gelu_ready"], p * STEPS + k - 1)
                    pe.matmul(A[:, k % 2, 0:CHUNK], w1s[a, e, :], T[a, i, c, :], start=True, stop=True).then_inc(s["hidden"], 1)
                    n = i * HGT * WID + h * HALF + c * CHUNK
                    if k >= 2:
                        pe.wait_ge(s["gated"], p * STEPS + k - 1)
                    pe.matmul(A[:, 2 + k % 2, 0:CHUNK], pick[:, e, :], gate_t[:, 0].rearrange("e q l -> e (q l)")[:, n:n + CHUNK],
                              start=True, stop=True).then_inc(s["gate_ready"], 1)

                def down(p, k):
                    (i, c, h), e = unit(k // EXPERTS), k % EXPERTS
                    a = slice(h * CH, (h + 1) * CH)
                    u = k // EXPERTS
                    if e == 0 and h == 0 and u >= 4:
                        pe.wait_ge(s["summed3"], p * (UNITS // 2) + u // 2 - 1)
                    if e == 0:
                        n = i * HGT * WID + h * HALF + c * CHUNK
                        for r in range(3):
                            pe.matmul(C[a, c % 2, 0:CHUNK], b2h[:, r, :], gate_t[:, 0].rearrange("e q l -> e (q l)")[:, n:n + CHUNK],
                                      start=(r == 0), stop=False)
                    pe.wait_ge(s["gated"], p * STEPS + k + 1)
                    pe.matmul(C[a, c % 2, 0:CHUNK], w2s[:, e, :], hid[:, k % 2, :], start=False, stop=(e == EXPERTS - 1)).then_inc(s["expert_done"], 1)

                pe.wait_ge(s["b2_split"], 1)
                with pe.Fori(0, PAIRS) as p:
                    pe.wait_ge(s["pair_loaded"], p * 80 + 80)
                    for k in range(STEPS):
                        up(p, k)
                        if k:
                            down(p, k - 1)
                    down(p, STEPS - 1)

            def out_chunk(dve, p, v):
                i, c = v // CHUNKS, v % CHUNKS
                dve.wait_ge(s["expert_done"], p * STEPS + (v + 1) * 2 * EXPERTS)
                ins = dve.tensor_tensor(X1[:, i, c, :], X1[:, i, c, :], C[:, c % 2, 0:CHUNK], ALU.add)
                ins.then_inc(s["summed3"], 1)

            @block.vector
            def _(dve):
                step = Signal(s["vstep3"])

                def L(instr):
                    link(dve, instr, step)
                for r in range(3):
                    L(dve.tensor_copy(b2h[:, r, :], b2s[:]))
                    L(dve.tensor_tensor(b2s[:], b2s[:], b2h[:, r, :], ALU.subtract))
                dve.engine_nop().then_inc(s["b2_split"], 1)
                with dve.Fori(0, PAIRS) as p:
                    for k in range(STEPS):
                        (i, c, h), e = unit(k // EXPERTS), k % EXPERTS
                        dve.wait_ge(s["gelu_ready"], p * STEPS + k + 1)
                        dve.wait_ge(s["gate_ready"], p * STEPS + k + 1)
                        dve.tensor_tensor(hid[:, k % 2, :], hid[:, k % 2, :], A[:, 2 + k % 2, 0:CHUNK], ALU.mult).then_inc(s["gated"], 1)
                        if e == 1 and k > 1 and h == 0:
                            v = k // (2 * EXPERTS) - 1
                            out_chunk(dve, p, v)
                    out_chunk(dve, p, UNITS // 2 - 1)


_INS = ['x', 'L0_conv_weight', 'L0_conv_bias', 'L0_ffn_W_gat', 'L0_ffn_att_src', 'L0_ffn_att_dst', 'L0_ffn_b_gat',
        'L0_ffn_ln_gamma', 'L0_ffn_ln_beta', 'L0_ffn_W1', 'L0_ffn_b1', 'L0_ffn_W2', 'L0_ffn_b2', 'L0_ffn_edge_index']


def kernel(**inputs):
    import numpy as _np
    import concourse.bacc as _bacc
    from concourse.bass_utils import run_bass_kernel_spmd as _run

    nc = _bacc.Bacc("TRN2", target_bir_lowering=False, num_devices=1)
    arrays, args = {}, []
    for name in _INS:
        a = _np.ascontiguousarray(inputs[name])
        arrays[f"in_{name}"] = a
        args.append(nc.dram_tensor(f"in_{name}", a.shape, mybir.dt.from_np(a.dtype), kind="ExternalInput").ap())
    args.append(nc.dram_tensor("out_0", (B, CH, HGT, WID), F32, kind="ExternalOutput").ap())
    build(nc, *args)
    r = _run(nc, [arrays], core_ids=[0])
    return r.results[0]["out_0"]
```

```python
from contextlib import ExitStack, contextmanager

import concourse.bass as bass
from concourse import mybir

F32 = mybir.dt.float32
BF16 = mybir.dt.bfloat16
I32 = mybir.dt.int32
U32 = mybir.dt.uint32
U16 = mybir.dt.uint16
ALU = mybir.AluOpType
ACT = mybir.ActivationFunctionType
AX = mybir.AxisListType

P = 128

B, CH, HGT, WID = 16, 64, 56, 56
HALF_ROWS = HGT // 2
HALF = HALF_ROWS * WID
CHUNKS = 4
CHUNK = HALF // CHUNKS
CHUNK_ROWS = HALF_ROWS // CHUNKS
TAPS = 9
M = B * HGT * WID
TOK = 112
TOK_TILES = HALF // TOK

GROUP = 36
FLAT = B * CH * HGT * WID
GROUPS_P = -(-FLAT // (GROUP * P))
QCHUNKS = 17
QGROUPS = GROUPS_P // QCHUNKS
FLAT_P = GROUPS_P * GROUP
assert QCHUNKS * QGROUPS == GROUPS_P
MAGIC = 1.5 * 2.0 ** 23
TINY = 2.0 ** -100
EXP_BITS = 0x7F800000
INV_BITS = 0x7F000000

EDGES = 262144
ECOLS = EDGES // P
HEADS, DIM = 4, 4
FEAT = HEADS * DIM
ROW = FEAT + 2 * HEADS
VALS = FEAT + HEADS
BLK = 1024
BLK_BITS, LO_BITS = 10, 7
HI = BLK // P
NB = M // BLK
NQ = M // P
U = 2
UNIT_BITS = 8
UG = 8
G = UG * U
BUFS = 2
UNROLL = 4
MAX_UNITS = (EDGES + NB * (U * P - 1)) // (U * P)
NG = -(-MAX_UNITS // (UG * UNROLL)) * UNROLL
TILES = NG * G
ID_W = -(-NG * UG // P)
SEND_BUFS = 4
PAD_DST = 1 << 20
RANK_COLS = 512
SEND = 16

EXPERTS, HID = 4, 128
GQ = 8
PAIR_Q = 2 * HGT * WID // P


class Signal:

    def __init__(self, sem):
        self.sem, self.base, self.k = sem, 0, 0

    @property
    def value(self):
        return self.base + self.k


def link(eng, instr, sig):
    instr.then_inc(sig.sem, 1)
    sig.k += 1
    eng.wait_ge(sig.sem, sig.value)


def hold(eng, sem, value, turns):
    eng.wait_ge(sem, value)
    eng.sem_inc(turns, 1)


@contextmanager
def rolled(eng, start, stop, sig, per_trip):
    first = sig.value
    with eng.Fori(start, stop) as i:
        sig.base, sig.k = (i - start) * per_trip + first, 0
        yield i
        assert sig.k == per_trip, sig.k
    sig.base, sig.k = first + (stop - start) * per_trip, 0


def build(nc, x, conv_w, conv_b, w_gat, att_src, att_dst, b_gat, ln_g, ln_b, w1, b1, w2, b2, edges, out):
    ctx = ExitStack()
    with ctx:
        def sb(name, shape, dt=F32):
            return ctx.enter_context(nc.sbuf_tensor(name, shape, dt))

        def sems(names):
            return {n: ctx.enter_context(nc.semaphore(n)) for n in names.split()}

        def dram(name, shape, dt=F32):
            return nc.dram_tensor(name, shape, dt).ap()

        xn_d = dram("xn_d", [P * FLAT_P])
        xq_d = dram("xq_d", [P * FLAT_P], BF16)
        x1_d = dram("x1_d", [B * CHUNKS, P, CHUNK])
        t_d = dram("t_d", [B * CHUNKS, P, CHUNK])
        mlp_d = dram("mlp_d", [B * CHUNKS, 2, P, 2, CHUNK])
        node_d = dram("node_d", [M, ROW])
        edge_d = dram("edge_d", [P * TILES, 2], I32)
        blk_d = dram("blk_d", [P * ID_W], I32)
        gate_d = dram("gate_d", [NQ // GQ, GQ, 3 * EXPERTS, P], BF16)

        ident = sb("ident", [P, P])
        ident_h = sb("ident_h", [P, P], BF16)
        ones = sb("ones", [P, P])
        below = sb("below", [P, P])
        halves = sb("halves", [P, P])
        lane = sb("lane", [P, P])
        unit_no = sb("unit_no", [P, ID_W])
        zero_row = sb("zero_row", [P, 512])
        eps_c = sb("eps_c", [P, 1])
        eps_t = sb("eps_t", [P, 1])
        scratch_i = sb("scratch_i", [P, P], I32)

        cbias = sb("cbias", [P, 1])
        proj = sb("proj", [P, 2, ROW])
        att = sb("att", [P, 2, FEAT])
        attw = sb("attw", [P, FEAT])
        vecs = sb("vecs", [P, 3, FEAT])
        w1s = sb("w1s", [P, EXPERTS, HID])
        b1s = sb("b1s", [P, EXPERTS])
        w2s = sb("w2s", [P, EXPERTS, CH])
        b2s = sb("b2s", [P, 2])
        pick = sb("pick", [3 * EXPERTS, EXPERTS, CH], BF16)
        fold = sb("fold", [P, CH])

        A = ctx.enter_context(nc.psum_tensor("A", [P, 4, 512], F32))
        C = ctx.enter_context(nc.psum_tensor("C", [P, 4, 512], F32))
        with ExitStack() as ph:
            def tb(name, shape, dt=F32):
                return ph.enter_context(nc.sbuf_tensor(name, shape, dt))

            cw = tb("cw", [P, CH, TAPS])
            cwq = tb("cwq", [P, CH, TAPS], BF16)
            cw_bd = tb("cw_bd", [P, TAPS, P], BF16)
            cw_t = tb("cw_t", [P, TAPS, P], BF16)
            X = tb("X", [P, CHUNKS, CHUNK])
            D = tb("D", [P, CHUNKS, CHUNK])
            S = tb("S", [P, CHUNKS, CHUNK])
            Q = tb("Q", [P, HALF_ROWS + 2, WID + 2], BF16)
            rows = tb("rows", [TOK, TOK_TILES, 2 * ROW])
            F = tb("F", [P, QGROUPS, GROUP])
            Fq = tb("Fq", [P, QGROUPS, GROUP], BF16)
            gmax = tb("gmax", [P, QGROUPS])
            ginv = tb("ginv", [P, QGROUPS])
            gscale = tb("gscale", [P, QGROUPS])

            src = tb("src", [P, ECOLS], I32)
            dst = tb("dst", [P, ECOLS], I32)
            rec = tb("rec", [P, ECOLS, 2], I32)
            blk_h = tb("blk_h", [P, ECOLS], BF16)
            mask_h = tb("mask_h", [P, ECOLS], BF16)
            zero_h = tb("zero_h", [P, RANK_COLS], BF16)
            run = tb("run", [P, RANK_COLS])
            pos = tb("pos", [P, ECOLS])
            pos_i = tb("pos_i", [P, ECOLS], I32)
            count = tb("count", [P, NB])
            total_i = tb("total_i", [P, NB], I32)
            units_b = tb("units_b", [P, NB])
            end_b = tb("end_b", [P, NB])
            start_b = tb("start_b", [P, NB])
            passed = tb("passed", [P, ID_W, NB])
            unit_blk = tb("unit_blk", [P, ID_W])
            unit_blk_i = tb("unit_blk_i", [P, ID_W], I32)
            slots = tb("slots", [P, SEND_BUFS, SEND], U32)
            rec_slots = tb("rec_slots", [P, SEND_BUFS, SEND, 2], I32)
            pad_rec = tb("pad_rec", [P, TILES // 8, 2], I32)


            s = sems(
                "const_ready weights_loaded edges_loaded vstep pstep counted prefix_ready blocks_ready blk_stored "
                "ranked pads_written xn_pad "
                "x_loaded mean_ready centred squared var_ready deviated normed xn_stored "
                "f_loaded quantised q_stored w_blocks w_turned w_ready "
                "c_loaded conv_done summed mean2_ready centred2 squared2 var2_ready deviated2 tokens_ready "
                "projected rows_ready c_stored sp_turns pool_turns"
            )
            sent = [ctx.enter_context(nc.semaphore(f"sent{k}")) for k in range(SEND_BUFS)]
            block = ph.enter_context(nc.Block())

            def pixels(t, b, h):
                return t.rearrange("b c (s r) w -> b s c (r w)", s=2)[b, h]

            xn_img = xn_d[0:FLAT].rearrange("(b c s n) -> b s c n", b=B, c=CH, s=2)
            xq_img = xq_d[0:FLAT].rearrange("(b c r w) -> b c r w", b=B, c=CH, r=HGT)
            xn_flat = xn_d.rearrange("(p j g e) -> p j g e", p=P, j=QCHUNKS, e=GROUP)
            xq_flat = xq_d.rearrange("(p j g e) -> p j g e", p=P, j=QCHUNKS, e=GROUP)
            node_img = node_d.rearrange("(b s j l) f -> b s l j f", b=B, s=2, l=TOK)
            WEIGHT_LOADS = 2 + 2 + 2 + 2 + 3 + 2 + 1 + 1 + 2

            @block.sync
            def _(sp):
                e_v = edges.rearrange("k (p t) -> k p t", p=P)
                sp.dma_start(dst[:], e_v[1]).then_inc(s["edges_loaded"], 16)
                sp.dma_start(src[:], e_v[0]).then_inc(s["edges_loaded"], 16)
                for h in range(2):
                    a = h * CH
                    sp.dma_start(cw[a:a + CH], conv_w.rearrange("o i h w -> o i (h w)")).then_inc(s["weights_loaded"], 16)
                    sp.dma_start(cbias[a:a + CH], conv_b.rearrange("(p k) -> p k", k=1)).then_inc(s["weights_loaded"], 16)
                    sp.dma_start(proj[a:a + CH, h, 0:FEAT], w_gat).then_inc(s["weights_loaded"], 16)
                    sp.dma_start(w1s[a:a + CH], w1.rearrange("e d f -> d e f")).then_inc(s["weights_loaded"], 16)
                for k, v in enumerate((b_gat, ln_g, ln_b)):
                    sp.dma_start(vecs[:, k, :], v.rearrange("(k f) -> k f", k=1).broadcast_to([P, FEAT])).then_inc(s["weights_loaded"], 16)
                for k, v in enumerate((att_src, att_dst)):
                    sp.dma_start(att[:, k, :], v.rearrange("(k h) d -> k (h d)", k=1).broadcast_to([P, FEAT])).then_inc(s["weights_loaded"], 16)
                sp.dma_start(b1s[:], b1.rearrange("e f -> f e"), allow_slow_non_contiguous=True).then_inc(s["weights_loaded"], 16)
                sp.dma_start(w2s[:], w2.rearrange("e f d -> f e d")).then_inc(s["weights_loaded"], 16)
                for k in range(2):
                    sp.dma_start(b2s[k * CH:(k + 1) * CH, :], b2.rearrange("(j k) c -> k c j", k=2)[k], allow_slow_non_contiguous=True).then_inc(s["weights_loaded"], 16)
                sp.wait_ge(s["const_ready"], 1)
                sp.dma_start(xn_d[FLAT:P * FLAT_P].rearrange("(k n) -> k n", k=1), zero_row[0:1, 0:P * FLAT_P - FLAT]).then_inc(s["xn_pad"], 16)
                with sp.Fori(0, B) as b:
                    for h in range(2):
                        sp.dma_start(X[h * CH:(h + 1) * CH].rearrange("p c n -> p (c n)"), pixels(x, b, h)).then_inc(s["x_loaded"], 16)
                    hold(sp, s["normed"], b + 1, s["sp_turns"])
                    for h in range(2):
                        sp.dma_start(xn_img[b, h], D[h * CH:(h + 1) * CH].rearrange("p c n -> p (c n)")).then_inc(s["xn_stored"], 16)
                    hold(sp, s["xn_stored"], b * 32 + 32, s["sp_turns"])
                sp.wait_ge(s["xn_pad"], 16)
                with sp.Fori(0, QCHUNKS) as j:
                    sp.dma_start(F[:], xn_flat[:, j]).then_inc(s["f_loaded"], 16)
                    hold(sp, s["quantised"], j + 1, s["sp_turns"])
                    sp.dma_start(xq_flat[:, j], Fq[:]).then_inc(s["q_stored"], 16)
                    hold(sp, s["q_stored"], j * 16 + 16, s["sp_turns"])
                with sp.Fori(0, B) as b:
                    for h in range(2):
                        r = 0 if h == 0 else HALF_ROWS - 1
                        sp.dma_start(Q[h * CH:(h + 1) * CH, 1 - h:1 - h + HALF_ROWS + 1, 1:WID + 1],
                                     xq_img[b, :, r:r + HALF_ROWS + 1, :]).then_inc(s["c_loaded"], 16)
                        sp.dma_start(X[h * CH:(h + 1) * CH].rearrange("p c n -> p (c n)"), pixels(x, b, h)).then_inc(s["c_loaded"], 16)
                    hold(sp, s["summed"], b + 1, s["sp_turns"])
                    sp.dma_start(x1_d[bass.ds(b * CHUNKS, CHUNKS)].rearrange("c p n -> p c n"), X[:]).then_inc(s["c_stored"], 16)
                    hold(sp, s["tokens_ready"], b + 1, s["sp_turns"])
                    sp.dma_start(t_d[bass.ds(b * CHUNKS, CHUNKS)].rearrange("c p n -> p c n"), D[:]).then_inc(s["c_stored"], 16)
                    hold(sp, s["rows_ready"], b + 1, s["sp_turns"])
                    for h in range(2):
                        sp.dma_start(node_img[b, h], rows[:, :, h * ROW:(h + 1) * ROW]).then_inc(s["c_stored"], 16)
                    hold(sp, s["c_stored"], b * 64 + 64, s["sp_turns"])
                sp.wait_ge(s["blk_stored"], 16)

            @block.gpsimd
            def _(pool):
                step = Signal(s["pstep"])
                link(pool, pool.memset(ident[:], 0.0), step)
                link(pool, pool.affine_select(out=ident[:], in_=ident[:], compare_op=ALU.not_equal, fill=1.0, base=0,
                                              pattern=[[-1, P]], channel_multiplier=1), step)
                link(pool, pool.tensor_copy(ident_h[:], ident[:]), step)
                link(pool, pool.memset(ones[:], 1.0), step)
                link(pool, pool.affine_select(out=below[:], in_=ones[:], compare_op=ALU.is_gt, fill=0.0, base=0,
                                              pattern=[[1, P]], channel_multiplier=-1), step)
                link(pool, pool.iota(scratch_i[:], pattern=[[1, P]], base=0, channel_multiplier=0), step)
                link(pool, pool.tensor_copy(lane[:], scratch_i[:]), step)
                link(pool, pool.iota(scratch_i[:, 0:ID_W], pattern=[[1, ID_W]], base=0, channel_multiplier=ID_W), step)
                link(pool, pool.tensor_copy(unit_no[:], scratch_i[:, 0:ID_W]), step)
                link(pool, pool.memset(zero_row[:], 0.0), step)
                link(pool, pool.memset(halves[:], 0.0), step)
                for h in range(2):
                    link(pool, pool.memset(halves[h * CH:(h + 1) * CH, h * CH:(h + 1) * CH], 1.0 / CH), step)
                link(pool, pool.memset(eps_c[:], 1e-6), step)
                link(pool, pool.memset(eps_t[:], 1e-5), step)
                link(pool, pool.memset(Q[:], 0.0), step)
                link(pool, pool.memset(cw_bd[:], 0.0), step)
                link(pool, pool.memset(zero_h[:], 0.0), step)
                link(pool, pool.memset(pad_rec[:, :, 0:1], 0), step)
                link(pool, pool.memset(pad_rec[:, :, 1:2], PAD_DST), step)
                link(pool, pool.memset(pick[:], 0.0), step)
                for r in range(3):
                    link(pool, pool.affine_select(out=pick[:], in_=pick[:], compare_op=ALU.not_equal, fill=1.0, base=-r * EXPERTS,
                                                  pattern=[[-1, EXPERTS], [0, CH]], channel_multiplier=1), step)
                link(pool, pool.memset(fold[:], 0.0), step)
                for r in range(2):
                    link(pool, pool.affine_select(out=fold[:], in_=fold[:], compare_op=ALU.not_equal, fill=1.0, base=-r * CH,
                                                  pattern=[[-1, CH]], channel_multiplier=1), step)
                pool.memset(scratch_i[:], 0).then_inc(s["const_ready"], 1)
                for k in range(8):
                    pool.dma_start(edge_d.rearrange("(p k c) r -> p k (c r)", p=P, k=8)[:, k],
                                   pad_rec[:].rearrange("p c r -> p (c r)")).then_inc(s["pads_written"], 16)


                pool.wait_ge(s["pads_written"], 8 * 16)
                ROUND = SEND_BUFS * SEND
                per_rank = RANK_COLS // ROUND

                def send_round(i, first):
                    for k in range(SEND_BUFS):
                        if not first:
                            pool.wait_ge(sent[k], i * (SEND * 16))
                        col = (i * SEND_BUFS + k) * SEND
                        pool.tensor_copy(rec_slots[:, k], rec[:, bass.ds(col, SEND), :]).then_inc(s["pstep"], 1)
                        step.k += 1
                        link(pool, pool.tensor_copy(slots[:, k, :].bitcast(I32), pos_i[:, bass.ds(col, SEND)]), step)
                        pool.sem_inc(s["pool_turns"], 1)
                        for c in range(SEND):
                            pool.indirect_dma_start(edge_d, bass.IndirectOffsetOnAxis(ap=slots[:, k, c:c + 1], axis=0),
                                                    rec_slots[:, k, c, :], None).then_inc(sent[k], 16)
                for r in range(ECOLS // RANK_COLS):
                    pool.wait_ge(s["ranked"], r + 1)
                    lo = r * per_rank
                    if r == 0:
                        send_round(0, True)
                        lo += 1
                    with rolled(pool, lo, (r + 1) * per_rank, step, 2 * SEND_BUFS) as i:
                        send_round(i, False)
                for k in range(SEND_BUFS):
                    pool.wait_ge(sent[k], ECOLS // SEND_BUFS * 16)

            def mean_of(pe, src_t, dst_ps, done):
                for c in range(CHUNKS):
                    mm = pe.matmul(dst_ps[:, c, 0:CHUNK], halves[:], src_t[:, c, :], start=True, stop=True)
                mm.then_inc(done, 1)

            @block.tensor
            def _(pe):
                pe.wait_ge(s["const_ready"], 1)
                pe.wait_ge(s["counted"], 1)
                pe.matmul(A[:, 0, 0:NB], below[:], count[:], start=True, stop=True)
                pe.matmul(A[:, 1, 0:NB], ones[:], count[:], start=True, stop=True).then_inc(s["prefix_ready"], 1)
                pe.wait_ge(s["w_blocks"], 1)
                for t in range(TAPS):
                    mm = pe.transpose(C[:].bitcast(BF16)[:, t // 4, (t % 4) * P:(t % 4 + 1) * P], cw_bd[:, t, :], ident_h[:])
                mm.then_inc(s["w_turned"], 1)
                pe.wait_ge(s["w_ready"], 1)
                with pe.Fori(0, B) as b:
                    pe.wait_ge(s["x_loaded"], b * 32 + 32)
                    mean_of(pe, X, A, s["mean_ready"])
                    pe.wait_ge(s["squared"], b + 1)
                    mean_of(pe, S, C, s["var_ready"])
                with pe.Fori(0, B) as b:
                    pe.wait_ge(s["c_loaded"], b * 64 + 64)
                    for c in range(CHUNKS):
                        for t in range(TAPS):
                            r0 = c * CHUNK_ROWS + t // 3
                            mm = pe.matmul(A[:, c, 0:CHUNK], cw_t[:, t, :], Q[:, r0:r0 + CHUNK_ROWS, t % 3:t % 3 + WID],
                                           start=(t == 0), stop=(t == TAPS - 1))
                    mm.then_inc(s["conv_done"], 1)
                    pe.wait_ge(s["summed"], b + 1)
                    mean_of(pe, X, C, s["mean2_ready"])
                    pe.wait_ge(s["squared2"], b + 1)
                    mean_of(pe, S, A, s["var2_ready"])
                    pe.wait_ge(s["tokens_ready"], b + 1)
                    tokens = D[:].rearrange("p c n -> p (c n)")
                    for j in range(TOK_TILES):
                        mm = pe.matmul(C[0:TOK, j // 7, (j % 7) * 2 * ROW:(j % 7 + 1) * 2 * ROW],
                                       tokens[:, j * TOK:(j + 1) * TOK], proj[:].rearrange("p s f -> p (s f)"), start=True, stop=True)
                    mm.then_inc(s["projected"], 1)

            @block.scalar
            def _(act):
                act.wait_ge(s["const_ready"], 1)
                act.wait_ge(s["blocks_ready"], 1)
                act.dma_start(blk_d.rearrange("(p k) -> p k", p=P), unit_blk_i[:]).then_inc(s["blk_stored"], 16)
                with act.Fori(0, B) as b:
                    act.wait_ge(s["centred"], b + 1)
                    act.activation(S[:], D[:], ACT.Square).then_inc(s["squared"], 1)
                    act.wait_ge(s["var_ready"], b + 1)
                    act.activation(S[:], C[:, :, 0:CHUNK], ACT.Sqrt, bias=eps_c[:]).then_inc(s["deviated"], 1)
                with act.Fori(0, B) as b:
                    act.wait_ge(s["centred2"], b + 1)
                    act.activation(S[:], D[:], ACT.Square).then_inc(s["squared2"], 1)
                    act.wait_ge(s["var2_ready"], b + 1)
                    act.activation(S[:], A[:, :, 0:CHUNK], ACT.Sqrt, bias=eps_t[:]).then_inc(s["deviated2"], 1)
                    act.wait_ge(s["projected"], b + 1)
                    act.copy(rows[:].rearrange("p (k j) f -> p k (j f)", k=2), C[0:TOK, 0:2, 0:14 * ROW]).then_inc(s["rows_ready"], 1)

            @block.vector
            def _(dve):
                step = Signal(s["vstep"])

                def L(instr):
                    link(dve, instr, step)

                dve.wait_ge(s["const_ready"], 1)
                dve.wait_ge(s["edges_loaded"], 32)
                L(dve.tensor_copy(rec[:, :, 0], src[:]))
                L(dve.tensor_copy(rec[:, :, 1], dst[:]))
                L(dve.tensor_scalar(pos_i[:], dst[:], BLK_BITS, None, ALU.arith_shift_right))
                L(dve.tensor_copy(blk_h[:], pos_i[:]))
                for b in range(NB):
                    L(dve.tensor_scalar(mask_h[:], blk_h[:], float(b), None, ALU.is_equal, ALU.add, accum_out=count[:, b:b + 1]))
                dve.engine_nop().then_inc(s["counted"], 1)

                dve.wait_ge(s["prefix_ready"], 1)
                L(dve.tensor_scalar(total_i[:], A[:, 1, 0:NB], float(U * P - 1), None, ALU.add))
                L(dve.tensor_scalar(total_i[:], total_i[:], UNIT_BITS, None, ALU.arith_shift_right))
                L(dve.tensor_copy(units_b[:], total_i[:]))
                L(dve.tensor_tensor_scan(end_b[:], units_b[:], zero_row[:, 0:NB], 0.0, ALU.add, ALU.add))
                L(dve.tensor_tensor(start_b[:], end_b[:], units_b[:], ALU.subtract))
                L(dve.tensor_scalar(start_b[:], start_b[:], float(U * P), -1.0, ALU.mult, ALU.add))
                L(dve.tensor_tensor(start_b[:], start_b[:], A[:, 0, 0:NB], ALU.add))
                L(dve.tensor_tensor(passed[:], end_b[:].rearrange("p (k n) -> p k n", k=1).broadcast_to([P, ID_W, NB]),
                                    unit_no[:].rearrange("p (n k) -> p n k", k=1).broadcast_to([P, ID_W, NB]), ALU.is_le))
                L(dve.tensor_reduce(unit_blk[:], passed[:], AX.X, ALU.add))
                L(dve.tensor_scalar(unit_blk_i[:], unit_blk[:], float(NB - 1), float(HI), ALU.min, ALU.mult))
                dve.engine_nop().then_inc(s["blocks_ready"], 1)

                for r in range(ECOLS // RANK_COLS):
                    cols = slice(r * RANK_COLS, (r + 1) * RANK_COLS)
                    L(dve.memset(pos[:, cols], 0.0))
                    for b in range(NB):
                        L(dve.tensor_scalar(mask_h[:, 0:RANK_COLS], blk_h[:, cols], float(b), None, ALU.is_equal))
                        L(dve.tensor_tensor_scan(run[:], mask_h[:, 0:RANK_COLS], zero_h[:], start_b[:, b:b + 1], ALU.add, ALU.add))
                        L(dve.copy_predicated(pos[:, cols], mask_h[:, 0:RANK_COLS].bitcast(U16), run[:]))
                        L(dve.tensor_copy(start_b[:, b:b + 1], run[:, RANK_COLS - 1:RANK_COLS]))
                    L(dve.tensor_copy(pos_i[:, cols], pos[:, cols]))
                    L(dve.tensor_scalar(dst[:, cols], pos_i[:, cols], P - 1, None, ALU.bitwise_and))
                    L(dve.tensor_scalar(pos_i[:, cols], pos_i[:, cols], LO_BITS, None, ALU.arith_shift_right))
                    L(dve.scalar_tensor_tensor(out=pos[:, cols], in0=dst[:, cols], scalar=float(TILES), in1=pos_i[:, cols], op0=ALU.mult, op1=ALU.add))
                    L(dve.tensor_copy(pos_i[:, cols], pos[:, cols]))
                    dve.engine_nop().then_inc(s["ranked"], 1)

                def quantise(vals, whole, quant, n):
                    def wide(v):
                        return v.rearrange("p (n k) -> p n k", k=1).broadcast_to([P, n, GROUP])
                    L(dve.tensor_reduce(gmax[:, 0:n], vals, AX.X, ALU.max, apply_absolute_value=True))
                    L(dve.tensor_scalar(gmax[:, 0:n], gmax[:, 0:n], TINY, None, ALU.max))
                    L(dve.tensor_scalar(gscale[:, 0:n].bitcast(I32), gmax[:, 0:n].bitcast(I32), EXP_BITS, None, ALU.bitwise_and))
                    L(dve.tensor_scalar(ginv[:, 0:n].bitcast(I32), gscale[:, 0:n].bitcast(I32), -1.0, float(INV_BITS), ALU.mult, ALU.add))
                    L(dve.tensor_scalar(ginv[:, 0:n], ginv[:, 0:n], 128.0, None, ALU.mult))
                    L(dve.tensor_scalar(gscale[:, 0:n], gscale[:, 0:n], 1.0 / 128.0, None, ALU.mult))
                    L(dve.tensor_tensor(vals, vals, wide(ginv[:, 0:n]), ALU.mult))
                    L(dve.tensor_scalar(vals, vals, MAGIC, MAGIC + 127.0, ALU.add, ALU.min))
                    L(dve.tensor_scalar(whole, vals, MAGIC - 128.0, MAGIC, ALU.max, ALU.subtract))
                    return dve.tensor_tensor(quant, whole, wide(gscale[:, 0:n]), ALU.mult)

                dve.wait_ge(s["weights_loaded"], 16 * WEIGHT_LOADS)
                v = cw[:].rearrange("p (n i) t -> p n (i t)", i=GROUP // TAPS)
                vq = cwq[:].rearrange("p (n i) t -> p n (i t)", i=GROUP // TAPS)
                L(quantise(v, vq, vq, CH * TAPS // GROUP))
                for h in range(2):
                    L(dve.tensor_copy(cw_bd[h * CH:(h + 1) * CH, :, h * CH:(h + 1) * CH],
                                      cwq[h * CH:(h + 1) * CH].rearrange("p i t -> p t i")))
                for h in range(2):
                    L(dve.memset(proj[(1 - h) * CH:(2 - h) * CH, h, :], 0.0))
                for h in range(2):
                    a = slice(h * CH, (h + 1) * CH)
                    for k in range(2):
                        L(dve.tensor_tensor(attw[a, :], proj[a, h, 0:FEAT], att[a, k, :], ALU.mult))
                        L(dve.tensor_reduce(proj[a, h, FEAT + k * HEADS:FEAT + (k + 1) * HEADS],
                                            attw[a, :].rearrange("p (h d) -> p h d", h=HEADS), AX.X, ALU.add))
                dve.engine_nop().then_inc(s["w_blocks"], 1)
                dve.wait_ge(s["w_turned"], 1)
                L(dve.tensor_copy(cw_t[:, 0:8].rearrange("p (b t) o -> p b (t o)", b=2), C[:].bitcast(BF16)[:, 0:2, 0:512]))
                dve.tensor_copy(cw_t[:, 8], C[:].bitcast(BF16)[:, 2, 0:P]).then_inc(s["w_ready"], 1)

                with rolled(dve, 0, B, step, 1) as b:
                    dve.wait_ge(s["mean_ready"], b + 1)
                    dve.tensor_tensor(D[:], X[:], A[:, :, 0:CHUNK], ALU.subtract).then_inc(s["centred"], 1)
                    dve.wait_ge(s["deviated"], b + 1)
                    L(dve.reciprocal(S[:], S[:]))
                    dve.tensor_tensor(D[:], D[:], S[:], ALU.mult).then_inc(s["normed"], 1)
                with rolled(dve, 0, QCHUNKS, step, 9) as j:
                    dve.wait_ge(s["f_loaded"], j * 16 + 16)
                    quantise(F[:], Fq[:], Fq[:], QGROUPS).then_inc(s["quantised"], 1)
                with rolled(dve, 0, B, step, 1) as b:
                    dve.wait_ge(s["conv_done"], b + 1)
                    dve.scalar_tensor_tensor(out=X[:], in0=A[:, :, 0:CHUNK], scalar=cbias[:], in1=X[:],
                                             op0=ALU.add, op1=ALU.add).then_inc(s["summed"], 1)
                    dve.wait_ge(s["mean2_ready"], b + 1)
                    dve.tensor_tensor(D[:], X[:], C[:, :, 0:CHUNK], ALU.subtract).then_inc(s["centred2"], 1)
                    dve.wait_ge(s["deviated2"], b + 1)
                    L(dve.reciprocal(S[:], S[:]))
                    dve.tensor_tensor(D[:], D[:], S[:], ALU.mult).then_inc(s["tokens_ready"], 1)

        with ExitStack() as ph:
            def tb(name, shape, dt=F32):
                return ph.enter_context(nc.sbuf_tensor(name, shape, dt))

            nodes = tb("nodes", [P, NQ, ROW])
            acc = tb("acc", [P, NQ, VALS])
            srt = tb("srt", [P, TILES, 2], I32)
            lo = tb("lo", [P, TILES], BF16)
            hi = tb("hi", [P, TILES], BF16)
            blk_row = tb("blk_row", [1, P * ID_W], I32)
            amax = tb("amax", [P, HEADS])
            amax_t = tb("amax_t", [HEADS, 1])
            amax_d = tb("amax_d", [HEADS, HEADS])
            na = tb("na", [P, NQ, HEADS])
            nb = tb("nb", [P, NQ, HEADS])
            lo_hot = tb("lo_hot", [P, UNROLL, G, P])
            hi_hot = tb("hi_hot", [P, UNROLL, G, HI])
            bits = lo_hot[:].rearrange("p b t l -> p (b t l)")[:, 0:TILES].bitcast(I32)
            lo_hot_t = tb("lo_hot_t", [P, G, P])
            dst_rows = tb("dst_rows", [P, 2, UG, HI, HEADS])
            gath = tb("gath", [P, BUFS, G, ROW])
            places = tb("places", [P, BUFS, G], U32)
            picked = tb("picked", [P, G, HEADS, HI])
            adst = tb("adst", [P, G, HEADS])
            shift = tb("shift", [P, G, HEADS])
            logit = tb("logit", [P, G, HEADS])
            weight = tb("weight", [P, G, HEADS])
            vals = tb("vals", [P, G, VALS])
            spread = tb("spread", [P, G, HI, VALS])
            gate_rows = tb("gate_rows", [GQ * 3 * EXPERTS, 4, P], BF16)
            T = tb("T", [P, CHUNK])
            hid = tb("hid", [P, CHUNK])
            mlp = tb("mlp", [P, 2, 2, CHUNK])
            s = sems(
                "nodes_loaded sorted_loaded vstep2 amax_rows amax_turned amax_diag amax_spread self_logits self_weights "
                "lo_hot_ready dst_rows_ready turned turned_copied picked_ready picked_read logits_ready weights_ready rows_used "
                "spread_ready scattered places_ready pool_turns2 sp_turns2 act_turns2 "
                "t_loaded0 t_loaded1 t_used0 t_used1 hidden gelu_ready pair_done pair_out "
                "squares_ready sqvar_ready sqrt_ready exp_in exp_ready gates_split gates_turned gates_copied gates_stored"
            )
            mlp_stored = [ctx.enter_context(nc.semaphore(f"mlp_stored{h}")) for h in range(2)]
            gathered = [ctx.enter_context(nc.semaphore(f"gathered{k}")) for k in range(BUFS)]
            gate_stored = [ctx.enter_context(nc.semaphore(f"gate_stored{k}")) for k in range(4)]
            block = ph.enter_context(nc.Block())

            parts = nodes[:].rearrange("p q f -> p (q f)")[:, 0:NQ * 3 * EXPERTS // 2].bitcast(BF16).rearrange("p (q e) -> p q e", e=3 * EXPERTS)

            def over_nodes(v, n):
                return v.rearrange("p (k f) -> p k f", k=1).broadcast_to([P, NQ, n])

            def bank_of(u):
                return 1 + u // 3, (u % 3) * HI * VALS

            def unit_blocks(eng, g, half):
                return nc.values_load_multi_w_load_instructions(
                    blk_row[0:1, bass.ds(g * UG + half * 4, 4)], engines=[eng.engine], min_val=0, max_val=NQ - HI,
                    skip_runtime_bounds_check_because="the blocks are clamped to the last one where they are made")[1]

            MLP_CHUNKS = B * CHUNKS
            MLP_TRIPS = MLP_CHUNKS * 2 // UNROLL
            TRIPS = NG // UNROLL
            assert MLP_TRIPS < TRIPS

            @block.sync
            def _(sp):
                sp.dma_start(srt[:].rearrange("p c k -> p (c k)"), edge_d.rearrange("(p c) k -> p (c k)", p=P)).then_inc(s["sorted_loaded"], 16)
                sp.dma_start(blk_row[:], blk_d.rearrange("(k n) -> k n", k=1)).then_inc(s["sorted_loaded"], 16)
                for k in range(4):
                    n = NQ // 4
                    sp.dma_start(nodes[:, k * n:(k + 1) * n, :], node_d.rearrange("(q l) f -> l q f", l=P)[:, k * n:(k + 1) * n, :]).then_inc(s["nodes_loaded"], 16)
                for h in range(2):
                    sp.dma_start(T[h * CH:(h + 1) * CH], t_d[0, h * CH:(h + 1) * CH]).then_inc(s[f"t_loaded{h}"], 16)
                with sp.Fori(1, MLP_CHUNKS) as m:
                    for h in range(2):
                        hold(sp, s[f"t_used{h}"], m, s["sp_turns2"])
                        sp.dma_start(T[h * CH:(h + 1) * CH], t_d[m, h * CH:(h + 1) * CH]).then_inc(s[f"t_loaded{h}"], 16)
                for k in range(NQ // GQ):
                    sp.wait_ge(s["gates_copied"], k + 1)
                    sp.dma_start(gate_d[k].rearrange("q e l -> (q e) l"), gate_rows[:, k % 4, :]).then_inc(gate_stored[k % 4], 16)
                for k in range(4):
                    sp.wait_ge(gate_stored[k], 16 * len(range(k, NQ // GQ, 4)))

            @block.gpsimd
            def _(pool):
                step = Signal(s["places_ready"])
                pool.wait_ge(s["sorted_loaded"], 32)
                pool.wait_ge(s["nodes_loaded"], 64)

                def gather(i, k):
                    if not (isinstance(i, int) and i == 0):
                        pool.wait_ge(s["rows_used"], (i - 1) * BUFS + k + 1)
                    link(pool, pool.tensor_copy(places[:, k, :].bitcast(I32), srt[:, bass.ds((i * BUFS + k) * G, G), 0]), step)
                    pool.sem_inc(s["pool_turns2"], 1)
                    for j in range(G):
                        pool.indirect_dma_start(gath[:, k, j, :], None, node_d,
                                                bass.IndirectOffsetOnAxis(ap=places[:, k, j:j + 1], axis=0)).then_inc(gathered[k], 16)
                for k in range(BUFS):
                    gather(0, k)
                with rolled(pool, 1, NG // BUFS, step, BUFS) as i:
                    for k in range(BUFS):
                        gather(i, k)

            @block.scalar
            def _(act):
                act.wait_ge(s["self_logits"], 1)
                act.activation(nb[:], nb[:], ACT.Exp).then_inc(s["self_weights"], 1)

                def turned_copy(g, half):
                    act.wait_ge(s["turned"], g * 2 + half + 1)
                    if not (isinstance(g, int) and g == 0):
                        act.wait_ge(s["picked_ready"], g * 2 - 1 + half)
                    for c in range(2):
                        t = half * UG + c * 4
                        act.copy(lo_hot_t[:, t:t + 4, :].rearrange("p t e -> p (t e)"), A[:, c, :]).then_inc(s["turned_copied"], 1)

                def weigh(g):
                    act.wait_ge(s["logits_ready"], g + 1)
                    act.activation(weight[:], logit[:], ACT.Exp).then_inc(s["weights_ready"], 1)

                def gelu(m, h, e):
                    v = (m * 2 + h) * EXPERTS + e
                    act.wait_ge(s["hidden"], v + 1)
                    act.activation(hid[:], A[:, 2, 0:CHUNK], ACT.Gelu, bias=b1s[:, e:e + 1]).then_inc(s["gelu_ready"], 1)

                def pair_out(m, h, j):
                    if j == 0 and not (isinstance(m, int) and m == 0):
                        act.wait_ge(mlp_stored[h], m * 16)
                    act.wait_ge(s["pair_done"], (m * 2 + h) * 2 + j + 1)
                    act.activation(mlp[:, h, j, :], A[:, 3, 0:CHUNK], ACT.Identity, bias=b2s[:, j:j + 1]).then_inc(s["pair_out"], 1)
                    if j == 1:
                        act.wait_ge(s["pair_out"], (m * 2 + h) * 2 + 2)
                        act.sem_inc(s["act_turns2"], 1)
                        act.dma_start(mlp_d[m, h].rearrange("p j n -> p (j n)"), mlp[:, h].rearrange("p j n -> p (j n)")).then_inc(mlp_stored[h], 16)

                def stage_dst(g, k, half):
                    if half == 0 and not (isinstance(g, int) and g < 2):
                        act.wait_ge(s["picked_ready"], g * 2 - 2)
                        act.sem_inc(s["act_turns2"], 1)
                    qs = unit_blocks(act, g, half)
                    for v in range(4):
                        act.copy(dst_rows[:, k % 2, half * 4 + v], nodes[:, bass.ds(qs[v], HI), FEAT + HEADS:ROW]).then_inc(s["dst_rows_ready"], 1)

                def body(i, k, with_mlp, last=False):
                    g = i * UNROLL + k
                    m, h = i * (UNROLL // 2) + k // 2, k % 2
                    left = UNROLL - 1 - k if last else UNROLL
                    if with_mlp:
                        gelu(m, h, 0)
                    if left >= 3:
                        stage_dst(g + 3, k + 3, 0)
                    if with_mlp:
                        gelu(m, h, 1)
                        pair_out(m, h, 0)
                        gelu(m, h, 2)
                    if left >= 2:
                        turned_copy(g + 2, 0)
                    if with_mlp:
                        gelu(m, h, 3)
                    if left >= 1:
                        weigh(g + 1)
                    if left >= 2:
                        turned_copy(g + 2, 1)
                    if with_mlp:
                        pair_out(m, h, 1)
                    if left >= 3:
                        stage_dst(g + 3, k + 3, 1)

                act.wait_ge(s["sorted_loaded"], 32)
                act.wait_ge(s["nodes_loaded"], 64)
                for k in range(2):
                    for half in range(2):
                        stage_dst(k, k, half)
                for g in range(2):
                    for half in range(2):
                        turned_copy(g, half)
                for half in range(2):
                    stage_dst(2, 2, half)
                weigh(0)
                for k in range(UNROLL):
                    body(0, k, True)
                with act.Fori(1, MLP_TRIPS) as i:
                    for k in range(UNROLL):
                        body(i, k, True)
                with act.Fori(MLP_TRIPS, TRIPS - 1) as i:
                    for k in range(UNROLL):
                        body(i, k, False)
                for k in range(UNROLL):
                    body(TRIPS - 1, k, False, True)
                for h in range(2):
                    act.wait_ge(mlp_stored[h], MLP_CHUNKS * 16)
                act.wait_ge(s["squares_ready"], 1)
                act.activation(acc[:, :, 0:FEAT], nodes[:, :, 0:FEAT], ACT.Square).then_inc(s["sqvar_ready"], 1)
                act.wait_ge(s["squares_ready"], 2)
                act.activation(na[:, :, 1], na[:, :, 0], ACT.Sqrt, bias=eps_t[:], scale=1.0 / FEAT).then_inc(s["sqrt_ready"], 1)
                act.wait_ge(s["exp_in"], 1)
                act.activation(nb[:], nb[:], ACT.Exp).then_inc(s["exp_ready"], 1)

            @block.tensor
            def _(pe):
                pe.wait_ge(s["amax_rows"], 1)
                pe.transpose(C[0:HEADS, 1, 0:P], amax[:], ident[:]).then_inc(s["amax_turned"], 1)
                pe.wait_ge(s["amax_diag"], 1)
                pe.matmul(A[:, 3, 0:HEADS], ones[0:HEADS, :], amax_d[:], start=True, stop=True).then_inc(s["amax_spread"], 1)

                def turn(g, k, half):
                    if half == 0:
                        pe.wait_ge(s["lo_hot_ready"], g + 1)
                    if not (isinstance(g, int) and g == 0 and half == 0):
                        pe.wait_ge(s["turned_copied"], g * 4 + half * 2)
                    for j in range(UG):
                        mm = pe.transpose(A[:, j // 4, (j % 4) * P:(j % 4 + 1) * P], lo_hot[:, k, half * UG + j, :], ident[:])
                    mm.then_inc(s["turned"], 1)

                def pick_dst(g, k, half):
                    pe.wait_ge(s["turned_copied"], g * 4 + half * 2 + 2)
                    if half == 0 and not (isinstance(g, int) and g == 0):
                        pe.wait_ge(s["picked_read"], g)
                    pe.wait_ge(s["dst_rows_ready"], g * UG + half * 4 + 4)
                    for j in range(UG):
                        t = half * UG + j
                        mm = pe.matmul(C[:, 0, t * HI * HEADS:(t + 1) * HI * HEADS], lo_hot_t[:, t, :],
                                       dst_rows[:, k % 2, t // U].rearrange("p h f -> p (h f)"), start=True, stop=True)
                    mm.then_inc(s["picked_ready"], 1)

                def scatter(g, k, units):
                    if units[0] == 0:
                        pe.wait_ge(s["spread_ready"], g + 1)
                    for u in units:
                        bank, at = bank_of(u)
                        for j in range(U):
                            mm = pe.matmul(C[:, bank, at:at + HI * VALS], lo_hot[:, k, u * U + j, :],
                                           spread[:, u * U + j].rearrange("p h v -> p (h v)"), start=(j == 0), stop=(j == U - 1))
                        if u % 3 == 2 or u == UG - 1:
                            mm.then_inc(s["scattered"], 1)

                def up(m, h, e):
                    a = slice(h * CH, (h + 1) * CH)
                    if e == 0:
                        pe.wait_ge(s[f"t_loaded{h}"], m * 16 + 16)
                    pe.matmul(A[:, 2, 0:CHUNK], w1s[a, e, :], T[a, :], start=True, stop=True).then_inc(s["hidden"], 1)
                    if e == EXPERTS - 1:
                        pe.wait_ge(s["hidden"], (m * 2 + h) * EXPERTS + EXPERTS)
                        pe.sem_inc(s[f"t_used{h}"], 1)

                def down(m, h, e):
                    v = m * 2 + h
                    pe.wait_ge(s["gelu_ready"], v * EXPERTS + e + 1)
                    if e % 2 == 0 and not (isinstance(m, int) and m == 0 and h == 0 and e == 0):
                        pe.wait_ge(s["pair_out"], v * 2 + e // 2)
                    a = slice(e % 2 * CH, (e % 2 + 1) * CH)
                    mm = pe.matmul(A[a, 3, 0:CHUNK], w2s[:, e, :], hid[:], start=True, stop=True)
                    if e % 2:
                        mm.then_inc(s["pair_done"], 1)

                def body(i, k, with_mlp, last=False):
                    g, k2 = i * UNROLL + k, (k + 2) % UNROLL
                    m, h = i * (UNROLL // 2) + k // 2, k % 2
                    turns = not last or k + 2 < UNROLL

                    def mlp_step(e):
                        if with_mlp:
                            if e:
                                down(m, h, e - 1)
                            if e < EXPERTS:
                                up(m, h, e)
                    mlp_step(0)
                    scatter(g, k, range(0, 3))
                    mlp_step(1)
                    scatter(g, k, range(3, UG))
                    mlp_step(2)
                    if turns:
                        turn(g + 2, k2, 0)
                    mlp_step(3)
                    if turns:
                        turn(g + 2, k2, 1)
                        pick_dst(g + 2, k2, 0)
                    mlp_step(4)
                    if turns:
                        pick_dst(g + 2, k2, 1)

                pe.wait_ge(s["sorted_loaded"], 32)
                pe.wait_ge(s["nodes_loaded"], 64)
                for g in range(2):
                    for half in range(2):
                        turn(g, g, half)
                        pick_dst(g, g, half)
                for k in range(UNROLL):
                    body(0, k, True)
                with pe.Fori(1, MLP_TRIPS) as i:
                    for k in range(UNROLL):
                        body(i, k, True)
                with pe.Fori(MLP_TRIPS, TRIPS - 1) as i:
                    for k in range(UNROLL):
                        body(i, k, False)
                for k in range(UNROLL):
                    body(TRIPS - 1, k, False, True)
                for k in range(NQ // GQ):
                    if k == 0:
                        pe.wait_ge(s["gates_split"], 1)
                    if k >= 4:
                        pe.wait_ge(s["gates_copied"], k - 3)
                    pe.transpose(A[0:GQ * 3 * EXPERTS, k % 4, 0:P // 2].bitcast(BF16), parts[:, k * GQ:(k + 1) * GQ, :].rearrange("p q e -> p (q e)"), ident_h[:]).then_inc(s["gates_turned"], 1)


            @block.vector
            def _(dve):
                step = Signal(s["vstep2"])

                def L(instr):
                    link(dve, instr, step)

                dve.wait_ge(s["sorted_loaded"], 32)
                L(dve.tensor_scalar(bits[:], srt[:, :, 1], P - 1, None, ALU.bitwise_and))
                L(dve.tensor_copy(lo[:], bits[:]))
                L(dve.tensor_scalar(bits[:], srt[:, :, 1], LO_BITS, HI - 1, ALU.arith_shift_right, ALU.bitwise_and))
                L(dve.tensor_copy(hi[:], bits[:]))
                L(dve.tensor_scalar(bits[:], srt[:, :, 1], PAD_DST.bit_length() - 1, None, ALU.arith_shift_right))
                L(dve.scalar_tensor_tensor(out=hi[:], in0=bits[:], scalar=float(HI), in1=hi[:], op0=ALU.mult, op1=ALU.add))

                dve.wait_ge(s["nodes_loaded"], 64)
                a_src, a_dst = nodes[:, :, FEAT:FEAT + HEADS], nodes[:, :, FEAT + HEADS:ROW]
                dve.tensor_reduce(amax[:], a_src.rearrange("p q f -> p f q"), AX.X, ALU.max).then_inc(s["amax_rows"], 1)
                dve.wait_ge(s["amax_turned"], 1)
                L(dve.tensor_reduce(amax_t[:], C[0:HEADS, 1, 0:P], AX.X, ALU.max))
                dve.tensor_scalar(amax_d[:], ident[0:HEADS, 0:HEADS], amax_t[:], None, ALU.mult).then_inc(s["amax_diag"], 1)
                dve.wait_ge(s["amax_spread"], 1)
                L(dve.tensor_copy(amax[:], A[:, 3, 0:HEADS]))

                def leaky(out_t, v):
                    return dve.scalar_tensor_tensor(out=out_t, in0=v, scalar=0.2, in1=v, op0=ALU.mult, op1=ALU.max)

                L(dve.tensor_tensor(na[:], a_dst, over_nodes(amax[:], HEADS), ALU.add))
                L(leaky(na[:], na[:]))
                L(dve.tensor_tensor(nb[:], a_src, a_dst, ALU.add))
                L(leaky(nb[:], nb[:]))
                dve.tensor_tensor(nb[:], nb[:], na[:], ALU.subtract).then_inc(s["self_logits"], 1)
                dve.wait_ge(s["self_weights"], 1)
                L(dve.tensor_copy(acc[:, :, FEAT:VALS], nb[:]))
                for h in range(HEADS):
                    L(dve.tensor_tensor(acc[:, :, h * DIM:(h + 1) * DIM], nodes[:, :, h * DIM:(h + 1) * DIM],
                                        nb[:, :, h:h + 1].broadcast_to([P, NQ, DIM]), ALU.mult))

                def per_edge(v):
                    return v.rearrange("p (k f) -> p k f", k=1).broadcast_to([P, G, HEADS])

                def one_hots(g, k):
                    L(dve.tensor_tensor(hi_hot[:, k], lane[:, 0:HI].rearrange("p (k h) -> p k h", k=1).broadcast_to([P, G, HI]),
                                        hi[:, bass.ds(g * G, G)].rearrange("p (t k) -> p t k", k=1).broadcast_to([P, G, HI]), ALU.is_equal))
                    dve.tensor_tensor(lo_hot[:, k], lane[:].rearrange("p (k h) -> p k h", k=1).broadcast_to([P, G, P]),
                                      lo[:, bass.ds(g * G, G)].rearrange("p (t k) -> p t k", k=1).broadcast_to([P, G, P]),
                                      ALU.is_equal).then_inc(s["lo_hot_ready"], 1)

                def logits(g, i, k):
                    dve.wait_ge(s["picked_ready"], g * 2 + 2)
                    dve.tensor_tensor(picked[:], C[:, 0, 0:G * HI * HEADS].rearrange("p (t h f) -> p t f h", t=G, h=HI),
                                      hi_hot[:, k].rearrange("p t (k h) -> p t k h", k=1).broadcast_to([P, G, HEADS, HI]),
                                      ALU.mult).then_inc(s["picked_read"], 1)
                    dve.wait_ge(s["picked_read"], g + 1)
                    L(dve.tensor_reduce(adst[:], picked[:], AX.X, ALU.add))
                    L(dve.tensor_tensor(shift[:], adst[:], per_edge(amax[:]), ALU.add))
                    L(leaky(shift[:], shift[:]))
                    dve.wait_ge(gathered[k % BUFS], (i * (UNROLL // BUFS) + k // BUFS + 1) * (G * 16))
                    L(dve.tensor_tensor(adst[:], adst[:], gath[:, k % BUFS, :, FEAT:FEAT + HEADS], ALU.add))
                    L(leaky(adst[:], adst[:]))
                    dve.tensor_tensor(logit[:], adst[:], shift[:], ALU.subtract).then_inc(s["logits_ready"], 1)

                def add_up(g):
                    for half in range(2):
                        qs = unit_blocks(dve, g, half)
                        for v in range(4):
                            u = half * 4 + v
                            bank, at = bank_of(u)
                            if u % 3 == 0:
                                dve.wait_ge(s["scattered"], g * 3 + bank)
                            here = acc[:, bass.ds(qs[v], HI), :]
                            L(dve.tensor_tensor(here, here, C[:, bank, at:at + HI * VALS].rearrange("p (h v) -> p h v", h=HI), ALU.add))

                def spread_out(g, k):
                    dve.wait_ge(s["weights_ready"], g + 1)
                    L(dve.tensor_copy(vals[:, :, FEAT:VALS], weight[:]))
                    h4 = vals[:, :, 0:FEAT].rearrange("p t (h d) -> p t h d", h=HEADS)
                    dve.tensor_tensor(h4, gath[:, k % BUFS, :, 0:FEAT].rearrange("p t (h d) -> p t h d", h=HEADS),
                                      weight[:].rearrange("p t (h k) -> p t h k", k=1).broadcast_to([P, G, HEADS, DIM]),
                                      ALU.mult).then_inc(s["rows_used"], 1)
                    dve.wait_ge(s["rows_used"], g + 1)
                    dve.tensor_tensor(spread[:], hi_hot[:, k].rearrange("p t (h k) -> p t h k", k=1).broadcast_to([P, G, HI, VALS]),
                                      vals[:].rearrange("p t (k v) -> p t k v", k=1).broadcast_to([P, G, HI, VALS]),
                                      ALU.mult).then_inc(s["spread_ready"], 1)

                def body(i, k, last=False):
                    g = i * UNROLL + k
                    left = UNROLL - 1 - k if last else UNROLL
                    spread_out(g, k)
                    if left >= 2:
                        one_hots(g + 2, (k + 2) % UNROLL)
                    if left >= 1:
                        logits(g + 1, i + (k + 1) // UNROLL, (k + 1) % UNROLL)
                    add_up(g)

                one_hots(0, 0)
                one_hots(1, 1)
                logits(0, 0, 0)
                with rolled(dve, 0, TRIPS - 1, step, UNROLL * (5 + UG + 2)) as i:
                    for k in range(UNROLL):
                        body(i, k)
                for k in range(UNROLL):
                    body(TRIPS - 1, k, True)

                agg, den = acc[:, :, 0:FEAT], acc[:, :, FEAT:VALS]
                L(dve.tensor_scalar(na[:], den, 1e-16, None, ALU.add))
                L(dve.reciprocal(nb[:], na[:]))
                dev = nodes[:, :, 0:FEAT]
                for h in range(HEADS):
                    L(dve.tensor_tensor(dev[:, :, h * DIM:(h + 1) * DIM], agg[:, :, h * DIM:(h + 1) * DIM],
                                        nb[:, :, h:h + 1].broadcast_to([P, NQ, DIM]), ALU.mult))
                L(dve.tensor_tensor(dev, dev, over_nodes(vecs[:, 0, :], FEAT), ALU.add))
                L(dve.tensor_reduce(na[:, :, 0], dev, AX.X, ALU.add))
                L(dve.tensor_scalar(na[:, :, 1], na[:, :, 0], 1.0 / FEAT, None, ALU.mult))
                dve.tensor_tensor(dev, dev, na[:, :, 1:2].broadcast_to([P, NQ, FEAT]), ALU.subtract).then_inc(s["squares_ready"], 1)
                dve.wait_ge(s["sqvar_ready"], 1)
                dve.tensor_reduce(na[:, :, 0], agg, AX.X, ALU.add).then_inc(s["squares_ready"], 1)
                dve.wait_ge(s["sqrt_ready"], 1)
                L(dve.reciprocal(na[:, :, 2], na[:, :, 1]))
                L(dve.tensor_tensor(dev, dev, over_nodes(vecs[:, 1, :], FEAT), ALU.mult))
                L(dve.tensor_reduce(nb[:], dev.rearrange("p q (h d) -> p q d h", h=HEADS), AX.X, ALU.add))
                L(dve.tensor_tensor(nb[:], nb[:], na[:, :, 2:3].broadcast_to([P, NQ, EXPERTS]), ALU.mult))
                L(dve.tensor_reduce(amax[:], vecs[:, 2, :].rearrange("p (h d) -> p d h", h=HEADS), AX.X, ALU.add))
                L(dve.tensor_tensor(nb[:], nb[:], over_nodes(amax[:], EXPERTS), ALU.add))
                L(dve.tensor_scalar(na[:], nb[:], 1.0 / HEADS, None, ALU.mult))
                rank, beat = acc[:, :, 0:EXPERTS], acc[:, :, EXPERTS]
                for e in range(EXPERTS):
                    L(dve.memset(rank[:, :, e], float(EXPERTS - 1 - e)))
                for e in range(EXPERTS):
                    for f in range(e + 1, EXPERTS):
                        L(dve.tensor_tensor(beat, na[:, :, e], na[:, :, f], ALU.is_ge))
                        L(dve.tensor_tensor(rank[:, :, e], rank[:, :, e], beat, ALU.subtract))
                        L(dve.tensor_tensor(rank[:, :, f], rank[:, :, f], beat, ALU.add))
                top, total = acc[:, :, EXPERTS], acc[:, :, EXPERTS + 1]
                L(dve.tensor_reduce(top, na[:], AX.X, ALU.max))
                dve.tensor_tensor(nb[:], na[:], acc[:, :, EXPERTS:EXPERTS + 1].broadcast_to([P, NQ, EXPERTS]), ALU.subtract).then_inc(s["exp_in"], 1)
                dve.wait_ge(s["exp_ready"], 1)
                L(dve.tensor_scalar(rank, rank, 1.5, None, ALU.is_lt))
                L(dve.tensor_tensor(nb[:], nb[:], rank, ALU.mult))
                L(dve.tensor_reduce(total, nb[:], AX.X, ALU.add))
                L(dve.reciprocal(top, total))
                L(dve.tensor_tensor(nb[:], nb[:], acc[:, :, EXPERTS:EXPERTS + 1].broadcast_to([P, NQ, EXPERTS]), ALU.mult))
                for r in range(3):
                    part = parts[:, :, r * EXPERTS:(r + 1) * EXPERTS]
                    if r < 2:
                        L(dve.tensor_copy(part, nb[:]))
                        L(dve.tensor_tensor(nb[:], nb[:], part, ALU.subtract))
                    else:
                        dve.tensor_copy(part, nb[:]).then_inc(s["gates_split"], 1)
                for k in range(NQ // GQ):
                    dve.wait_ge(s["gates_turned"], k + 1)
                    if k >= 4:
                        dve.wait_ge(gate_stored[k % 4], 16 * (k // 4))
                    dve.tensor_copy(gate_rows[:, k % 4, :], A[0:GQ * 3 * EXPERTS, k % 4, 0:P // 2].bitcast(BF16)).then_inc(s["gates_copied"], 1)

        with ExitStack() as ph:
            def tb(name, shape, dt=F32):
                return ph.enter_context(nc.sbuf_tensor(name, shape, dt))

            gate_t = tb("gate_t", [3 * EXPERTS, 2, PAIR_Q, P], BF16)
            mlp = tb("mlp3", [P, 4, 2, 2, CHUNK])
            X1 = tb("X1", [P, 4, CHUNK])
            gated = tb("gated", [P, 4, CHUNK])
            s = sems("gate_ready gated_ready folded summed3 sp_turns3 gate_loaded0 gate_loaded1")
            chunk_in = [ctx.enter_context(nc.semaphore(f"chunk_in{k}")) for k in range(4)]
            chunk_out = [ctx.enter_context(nc.semaphore(f"chunk_out{k}")) for k in range(4)]
            block = ph.enter_context(nc.Block())
            ROUNDS = B // 4
            PER = 2 * CHUNKS
            STEPS = 2 * PER

            out_rows = out.rearrange("b c (s k r) w -> b k s c (r w)", s=2, k=CHUNKS)

            @block.sync
            def _(sp):
                def load(n, k):
                    sp.dma_start(mlp[:, k], mlp_d[n].rearrange("s p j n -> p s j n")).then_inc(chunk_in[k], 16)
                    sp.dma_start(X1[:, k], x1_d[n]).then_inc(chunk_in[k], 16)

                def load_gates(pair, half):
                    sp.dma_start(gate_t[:, half], gate_d.rearrange("k q e l -> e (k q) l")[:, bass.ds(pair * PAIR_Q, PAIR_Q), :]).then_inc(s[f"gate_loaded{half}"], 16)

                load_gates(0, 0)
                for k in range(4):
                    load(k, k)
                load_gates(1, 1)

                def store_and_load(r, t, more):
                    k = t % 4
                    hold(sp, s["summed3"], r * STEPS + t + 1, s["sp_turns3"])
                    for h in range(2):
                        sp.dma_start(out_rows[r * 4 + t // CHUNKS, t % CHUNKS, h], X1[h * CH:(h + 1) * CH, k]).then_inc(chunk_out[k], 16)
                    if more or t < STEPS - 4:
                        hold(sp, chunk_out[k], (r * 4 + t // 4 + 1) * 32, s["sp_turns3"])
                        load(r * STEPS + t + 4, k)
                    if more and t % PER == PER - 1:
                        load_gates(r * 2 + 2 + t // PER, t // PER)

                with sp.Fori(0, ROUNDS - 1) as r:
                    for t in range(STEPS):
                        store_and_load(r, t, True)
                for t in range(STEPS):
                    store_and_load(ROUNDS - 1, t, False)
                for k in range(4):
                    sp.wait_ge(chunk_out[k], ROUNDS * STEPS // 4 * 32)

            @block.tensor
            def _(pe):
                def spread_gates(r, t, h, j, first):
                    w = (t * 2 + h) * 2 + j
                    n = (t % PER) // CHUNKS * HGT * WID + h * HALF + t % CHUNKS * CHUNK
                    if j == 0 and h == 0 and t % PER == 0:
                        pe.wait_ge(s[f"gate_loaded{t // PER}"], r * 16 + 16)
                    if w >= 4 or not first:
                        pe.wait_ge(s["gated_ready"], r * STEPS * 4 + w - 3)
                    pe.matmul(A[:, w % 4, 0:CHUNK], pick[:, 2 * j:2 * j + 2, :].rearrange("e k c -> e (k c)"),
                              gate_t[:, t // PER].rearrange("e q l -> e (q l)")[:, n:n + CHUNK], start=True, stop=True).then_inc(s["gate_ready"], 1)

                def fold_pair(r, t, h, j, first):
                    w = (t * 2 + h) * 2 + j
                    if h == 0 and j == 0 and (t >= 2 or not first):
                        pe.wait_ge(s["summed3"], r * STEPS + t - 1)
                    pe.wait_ge(s["gated_ready"], r * STEPS * 4 + w + 1)
                    pe.matmul(C[h * CH:(h + 1) * CH, t % 2, 0:CHUNK], fold[:], gated[:, w % 4, :],
                              start=(j == 0), stop=(j == 1)).then_inc(s["folded"], 1)

                def round_of(r, first):
                    todo = [(t, h, j) for t in range(STEPS) for h in range(2) for j in range(2)]
                    for w, at in enumerate(todo):
                        spread_gates(r, *at, first)
                        if w >= 2:
                            fold_pair(r, *todo[w - 2], first)
                    for at in todo[-2:]:
                        fold_pair(r, *at, first)

                round_of(0, True)
                with pe.Fori(1, ROUNDS) as r:
                    round_of(r, False)

            @block.vector
            def _(dve):
                def add_x1(r, t):
                    dve.wait_ge(s["folded"], (r * STEPS + t + 1) * 4)
                    dve.tensor_tensor(X1[:, t % 4], X1[:, t % 4], C[:, t % 2, 0:CHUNK], ALU.add).then_inc(s["summed3"], 1)

                def round_of(r, first):
                    for t in range(STEPS):
                        dve.wait_ge(chunk_in[t % 4], (r * 4 + t // 4 + 1) * 32)
                        for h in range(2):
                            for j in range(2):
                                w = (t * 2 + h) * 2 + j
                                dve.wait_ge(s["gate_ready"], r * STEPS * 4 + w + 1)
                                if w >= 4 or not first:
                                    dve.wait_ge(s["folded"], r * STEPS * 4 + w - 3)
                                dve.tensor_tensor(gated[:, w % 4, :], mlp[:, t % 4, h, j, :], A[:, w % 4, 0:CHUNK], ALU.mult).then_inc(s["gated_ready"], 1)
                        if t:
                            add_x1(r, t - 1)
                    add_x1(r, STEPS - 1)

                round_of(0, True)
                with dve.Fori(1, ROUNDS) as r:
                    round_of(r, False)


_INS = ['x', 'L0_conv_weight', 'L0_conv_bias', 'L0_ffn_W_gat', 'L0_ffn_att_src', 'L0_ffn_att_dst', 'L0_ffn_b_gat',
        'L0_ffn_ln_gamma', 'L0_ffn_ln_beta', 'L0_ffn_W1', 'L0_ffn_b1', 'L0_ffn_W2', 'L0_ffn_b2', 'L0_ffn_edge_index']


def kernel(**inputs):
    import numpy as _np
    import concourse.bacc as _bacc
    from concourse.bass_utils import run_bass_kernel_spmd as _run

    nc = _bacc.Bacc("TRN2", target_bir_lowering=False, num_devices=1)
    arrays, args = {}, []
    for name in _INS:
        a = _np.ascontiguousarray(inputs[name])
        arrays[f"in_{name}"] = a
        args.append(nc.dram_tensor(f"in_{name}", a.shape, mybir.dt.from_np(a.dtype), kind="ExternalInput").ap())
    args.append(nc.dram_tensor("out_0", (B, CH, HGT, WID), F32, kind="ExternalOutput").ap())
    build(nc, *args)
    r = _run(nc, [arrays], core_ids=[0])
    return r.results[0]["out_0"]
```

```python
from contextlib import ExitStack, contextmanager

import concourse.bass as bass
from concourse import mybir

F32 = mybir.dt.float32
BF16 = mybir.dt.bfloat16
F16 = mybir.dt.float16
I32 = mybir.dt.int32
U32 = mybir.dt.uint32
U16 = mybir.dt.uint16
ALU = mybir.AluOpType
ACT = mybir.ActivationFunctionType
AX = mybir.AxisListType

P = 128

B, CH, HGT, WID = 16, 64, 56, 56
HALF_ROWS = HGT // 2
HALF = HALF_ROWS * WID
CHUNKS = 4
CHUNK = HALF // CHUNKS
CHUNK_ROWS = HALF_ROWS // CHUNKS
TAPS = 9
M = B * HGT * WID
TOK = 112
TOK_TILES = HALF // TOK

GROUP = 36
FLAT = B * CH * HGT * WID
GROUPS_P = -(-FLAT // (GROUP * P))
QCHUNKS = 17
QGROUPS = GROUPS_P // QCHUNKS
FLAT_P = GROUPS_P * GROUP
assert QCHUNKS * QGROUPS == GROUPS_P
MAGIC = 1.5 * 2.0 ** 23
TINY = 2.0 ** -100
EXP_BITS = 0x7F800000
INV_BITS = 0x7F000000

EDGES = 262144
ECOLS = EDGES // P
HEADS, DIM = 4, 4
FEAT = HEADS * DIM
ROW = FEAT + 2 * HEADS
VALS = FEAT + HEADS
BLK = 1024
BLK_BITS, LO_BITS = 10, 7
HI = BLK // P
NB = M // BLK
NQ = M // P
SORT_TILES = 64
SG = ECOLS // SORT_TILES
STEP = 32
RUN = 4
RUN_BITS = 2
FIELDS = 3
RUN_COLS = -(-((P * SORT_TILES + NB * (RUN - 1)) // RUN) // P)
SLOT_COLS = RUN_COLS * RUN
U = 4
UNIT_RUN_BITS = 7
UG = 4
G = UG * U
BUFS = 4
UNROLL = 4
MAX_UNITS = (EDGES + SG * NB * (RUN - 1) + NB * (U * P - RUN)) // (U * P)
NG = -(-MAX_UNITS // UG)
TILES = NG * G
ID_W = -(-NG * UG // P)
PLACES = TILES // RUN
ALL_PLACES = PLACES + SG * RUN_COLS
assert 1 << RUN_BITS == RUN and 1 << UNIT_RUN_BITS == U * P // RUN == P
BLKS = NB + 1

EXPERTS, HID = 4, 128
GQ = 8
GATE_BUFS = 8
PAIR_Q = 2 * HGT * WID // P


class Signal:

    def __init__(self, sem):
        self.sem, self.base, self.k = sem, 0, 0

    @property
    def value(self):
        return self.base + self.k


def link(eng, instr, sig):
    instr.then_inc(sig.sem, 1)
    sig.k += 1
    eng.wait_ge(sig.sem, sig.value)


def hold(eng, sem, value, turns):
    eng.wait_ge(sem, value)
    eng.sem_inc(turns, 1)


@contextmanager
def rolled(eng, start, stop, sig, per_trip):
    first = sig.value
    with eng.Fori(start, stop) as i:
        sig.base, sig.k = (i - start) * per_trip + first, 0
        yield i
        assert sig.k == per_trip, sig.k
    sig.base, sig.k = first + (stop - start) * per_trip, 0


def build(nc, x, conv_w, conv_b, w_gat, att_src, att_dst, b_gat, ln_g, ln_b, w1, b1, w2, b2, edges, out):
    ctx = ExitStack()
    with ctx:
        def sb(name, shape, dt=F32):
            return ctx.enter_context(nc.sbuf_tensor(name, shape, dt))

        def sems(names):
            return {n: ctx.enter_context(nc.semaphore(n)) for n in names.split()}

        def dram(name, shape, dt=F32):
            return nc.dram_tensor(name, shape, dt).ap()

        xn_d = dram("xn_d", [P * FLAT_P])
        xq_d = dram("xq_d", [P * FLAT_P], BF16)
        x1_d = dram("x1_d", [B * CHUNKS, P, CHUNK])
        t_d = dram("t_d", [B * CHUNKS, P, CHUNK])
        mlp_d = dram("mlp_d", [B * CHUNKS, 2, P, 2, CHUNK])
        node_d = dram("node_d", [M, ROW])
        edge_d = dram("edge_d", [P * ALL_PLACES, RUN * FIELDS], F16)
        blk_d = dram("blk_d", [P * ID_W], I32)
        gate_d = dram("gate_d", [NQ // GQ, GQ, 3 * EXPERTS, P], BF16)

        ident = sb("ident", [P, P])
        ident_h = sb("ident_h", [P, P], BF16)
        ones = sb("ones", [P, P])
        below = sb("below", [P, P])
        halves = sb("halves", [P, P])
        lane = sb("lane", [P, P])
        unit_no = sb("unit_no", [P, ID_W])
        zero_row = sb("zero_row", [P, 512])
        eps_c = sb("eps_c", [P, 1])
        eps_t = sb("eps_t", [P, 1])
        scratch_i = sb("scratch_i", [P, P], I32)

        cbias = sb("cbias", [P, 1])
        proj = sb("proj", [P, 2, ROW])
        att = sb("att", [P, 2, FEAT])
        attw = sb("attw", [P, FEAT])
        vecs = sb("vecs", [P, 3, FEAT])
        w1s = sb("w1s", [P, EXPERTS, HID])
        b1s = sb("b1s", [P, EXPERTS])
        w2s = sb("w2s", [P, EXPERTS, CH])
        b2s = sb("b2s", [P, 2])
        pick = sb("pick", [3 * EXPERTS, EXPERTS, CH], BF16)
        fold = sb("fold", [P, CH])

        A = ctx.enter_context(nc.psum_tensor("A", [P, 4, 512], F32))
        C = ctx.enter_context(nc.psum_tensor("C", [P, 4, 512], F32))
        with ExitStack() as ph:
            def tb(name, shape, dt=F32):
                return ph.enter_context(nc.sbuf_tensor(name, shape, dt))

            cw = tb("cw", [P, CH, TAPS])
            cwq = tb("cwq", [P, CH, TAPS], BF16)
            cw_bd = tb("cw_bd", [P, TAPS, P], BF16)
            cw_t = tb("cw_t", [P, TAPS, P], BF16)
            src = tb("src", [P, ECOLS], I32)
            dst = tb("dst", [P, ECOLS], I32)
            X, D = [], []
            for t, edge_t in ((X, src), (D, dst)):
                t.append(tb(f"pixels{len(X)}{len(D)}", [P, CHUNKS, CHUNK])[:])
                t.append(edge_t[:].bitcast(F32)[:, 0:HALF].rearrange("p (c n) -> p c n", c=CHUNKS))
            S = tb("S", [P, CHUNKS, CHUNK])
            Q = [tb(f"Q{k}", [P, HALF_ROWS + 2, WID + 2], BF16) for k in range(2)]
            dev = tb("dev", [TOK, TOK_TILES, 2])
            rstd = tb("rstd", [TOK, TOK_TILES, 2])
            rows = tb("rows", [TOK, TOK_TILES, 2 * ROW])
            QN = QGROUPS * GROUP
            F = [X[k].rearrange("p c n -> p (c n)")[:, 0:QN].rearrange("p (g e) -> p g e", e=GROUP) for k in range(2)]
            Fq = [S[:].rearrange("p c n -> p (c n)").bitcast(BF16)[:, k * QN:(k + 1) * QN].rearrange("p (g e) -> p g e", e=GROUP) for k in range(2)]
            gmax = tb("gmax", [P, QGROUPS])
            ginv = tb("ginv", [P, QGROUPS])
            gscale = tb("gscale", [P, QGROUPS])

            rec = tb("rec", [P, ECOLS // STEP, FIELDS, STEP], F16)
            blk_h = tb("blk_h", [P, ECOLS], BF16)
            mask_h = tb("mask_h", [P, ECOLS], BF16)
            zeros_h = tb("zeros_h", [P, SG * NB], BF16)
            keep = tb("keep", [P, SG, BLKS], BF16)
            inj = tb("inj", [P, ECOLS])
            run = tb("run", [P, ECOLS])
            pos = tb("pos", [P, ECOLS])
            slot_lo, slot_col = (inj[:].bitcast(F16)[:, k * ECOLS:(k + 1) * ECOLS] for k in range(2))
            lane_h = tb("lane_h", [P, P, STEP], F16)
            local = tb("local", [P, SG, BLKS])
            delta = tb("delta", [P, SG, BLKS])
            jump = tb("jump", [P, NB, SG])
            hot_lo = tb("hot_lo", [P, 2, P, STEP], F16)
            hot_col = jump[:].rearrange("p b g -> p (b g)").bitcast(F16)[:, 0:SLOT_COLS * STEP].rearrange("p (c t) -> p c t", t=STEP)
            wide_rec = tb("wide_rec", [P, 2, FIELDS, SLOT_COLS, STEP], F16)
            table = wide_rec[:].rearrange("p b v c t -> p (b v c t)").bitcast(F32)
            flat_count, flat_runs, flat_before = (table[:, k * NB * SG:(k + 1) * NB * SG] for k in range(3))
            count, runs, before = (t.rearrange("p (b g) -> p b g", b=NB) for t in (flat_count, flat_runs, flat_before))
            table_g = hot_lo[:].rearrange("p b l t -> p (b l t)").bitcast(F32)
            runs_g, shift_g = (table_g[:, k * BLKS * SG:(k + 1) * BLKS * SG].rearrange("p (g b) -> p g b", g=SG) for k in range(2))
            units_i = tb("units_i", [P, NB], I32)
            units_b = tb("units_b", [P, NB])
            end_b = tb("end_b", [P, NB])
            start_b = tb("start_b", [P, NB])
            run_no = tb("run_no", [P, RUN_COLS])
            reached = tb("reached", [P, RUN_COLS, BLKS])
            place = tb("place", [P, RUN_COLS])
            place_i = tb("place_i", [P, RUN_COLS], I32)
            place_p = tb("place_p", [P, RUN_COLS], I32)
            slots = tb("slots", [P, 2, RUN_COLS], U32)
            run_slots = tb("run_slots", [P, 2, SLOT_COLS, FIELDS], F16)
            passed = tb("passed", [P, ID_W, NB])
            unit_blk = tb("unit_blk", [P, ID_W])
            unit_blk_i = tb("unit_blk_i", [P, ID_W], I32)

            s = sems(
                "const_ready weights_loaded edges_loaded vstep pstep counted prefix_ready blocks_ready blk_stored "
                "pads_written xn_pad spread_steps step_sums group_out group_slots dve_turns "
                "fields_ready mean_ready centred squared var_ready deviated rstd_ready rstd_spread normed "
                "quantised w_blocks w_turned w_ready "
                "conv_done summed mean2_ready centred2 squared2 var2_ready deviated2 rstd2_ready rstd2_spread tokens_ready "
                "projected rows_ready rows_stored sp_turns pool_turns "
                "x_loaded0 x_loaded1 xn_stored0 xn_stored1 f_loaded0 f_loaded1 q_stored0 q_stored1 "
                "c_loaded0 c_loaded1 x1_stored0 x1_stored1 t_stored0 t_stored1"
            )
            sent = [ctx.enter_context(nc.semaphore(f"sent{k}")) for k in range(2)]
            block = ph.enter_context(nc.Block())

            def pixels(t, b, h):
                return t.rearrange("b c (s r) w -> b s c (r w)", s=2)[b, h]

            xn_img = xn_d[0:FLAT].rearrange("(b c s n) -> b s c n", b=B, c=CH, s=2)
            xq_img = xq_d[0:FLAT].rearrange("(b c r w) -> b c r w", b=B, c=CH, r=HGT)
            xn_flat = xn_d.rearrange("(p j g e) -> p j g e", p=P, j=QCHUNKS, e=GROUP)
            xq_flat = xq_d.rearrange("(p j g e) -> p j g e", p=P, j=QCHUNKS, e=GROUP)
            node_img = node_d.rearrange("(b s j l) f -> b s l j f", b=B, s=2, l=TOK)
            WEIGHT_LOADS = 2 + 2 + 2 + 2 + 3 + 2 + 1 + 1 + 2

            @block.sync
            def _(sp):
                e_v = edges.rearrange("k (p t) -> k p t", p=P)
                sp.dma_start(dst[:], e_v[1]).then_inc(s["edges_loaded"], 16)
                sp.dma_start(src[:], e_v[0]).then_inc(s["edges_loaded"], 16)
                for h in range(2):
                    a = h * CH
                    sp.dma_start(cw[a:a + CH], conv_w.rearrange("o i h w -> o i (h w)")).then_inc(s["weights_loaded"], 16)
                    sp.dma_start(cbias[a:a + CH], conv_b.rearrange("(p k) -> p k", k=1)).then_inc(s["weights_loaded"], 16)
                    sp.dma_start(proj[a:a + CH, h, 0:FEAT], w_gat).then_inc(s["weights_loaded"], 16)
                    sp.dma_start(w1s[a:a + CH], w1.rearrange("e d f -> d e f")).then_inc(s["weights_loaded"], 16)
                for k, v in enumerate((b_gat, ln_g, ln_b)):
                    sp.dma_start(vecs[:, k, :], v.rearrange("(k f) -> k f", k=1).broadcast_to([P, FEAT])).then_inc(s["weights_loaded"], 16)
                for k, v in enumerate((att_src, att_dst)):
                    sp.dma_start(att[:, k, :], v.rearrange("(k h) d -> k (h d)", k=1).broadcast_to([P, FEAT])).then_inc(s["weights_loaded"], 16)
                sp.dma_start(b1s[:], b1.rearrange("e f -> f e"), allow_slow_non_contiguous=True).then_inc(s["weights_loaded"], 16)
                sp.dma_start(w2s[:], w2.rearrange("e f d -> f e d")).then_inc(s["weights_loaded"], 16)
                for k in range(2):
                    sp.dma_start(b2s[k * CH:(k + 1) * CH, :], b2.rearrange("(j k) c -> k c j", k=2)[k], allow_slow_non_contiguous=True).then_inc(s["weights_loaded"], 16)
                sp.wait_ge(s["const_ready"], 1)
                sp.dma_start(xn_d[FLAT:P * FLAT_P].rearrange("(k n) -> k n", k=1), zero_row[0:1, 0:P * FLAT_P - FLAT]).then_inc(s["xn_pad"], 16)
                def load_x(b, k):
                    for h in range(2):
                        sp.dma_start(X[k][h * CH:(h + 1) * CH].rearrange("p c n -> p (c n)"), pixels(x, b, h)).then_inc(s[f"x_loaded{k}"], 16)

                def store_normed(i, k, more):
                    hold(sp, s["normed"], i * 2 + k + 1, s["sp_turns"])
                    for h in range(2):
                        sp.dma_start(xn_img[i * 2 + k, h], D[k][h * CH:(h + 1) * CH].rearrange("p c n -> p (c n)")).then_inc(s[f"xn_stored{k}"], 16)
                    if more:
                        load_x(i * 2 + k + 2, k)
                load_x(0, 0)
                sp.wait_ge(s["fields_ready"], 1)
                load_x(1, 1)
                with sp.Fori(0, B // 2 - 1) as i:
                    for k in range(2):
                        store_normed(i, k, True)
                for k in range(2):
                    store_normed(B // 2 - 1, k, False)
                for k in range(2):
                    sp.wait_ge(s[f"xn_stored{k}"], B // 2 * 32)
                sp.wait_ge(s["xn_pad"], 16)

                def load_f(j, k):
                    sp.dma_start(F[k], xn_flat[:, j]).then_inc(s[f"f_loaded{k}"], 16)

                def store_q(i, k, more):
                    hold(sp, s["quantised"], i * 2 + k + 1, s["sp_turns"])
                    sp.dma_start(xq_flat[:, i * 2 + k], Fq[k]).then_inc(s[f"q_stored{k}"], 16)
                    if more:
                        load_f(i * 2 + k + 2, k)
                for k in range(2):
                    load_f(k, k)
                with sp.Fori(0, QCHUNKS // 2 - 1) as i:
                    for k in range(2):
                        store_q(i, k, True)
                for k in range(3):
                    store_q(QCHUNKS // 2 - 1 + k // 2, k % 2, k == 0)
                for k in range(2):
                    sp.wait_ge(s[f"q_stored{k}"], (QCHUNKS + 1 - k) // 2 * 16)

                def load_c(b, k):
                    for h in range(2):
                        r = 0 if h == 0 else HALF_ROWS - 1
                        sp.dma_start(Q[k][h * CH:(h + 1) * CH, 1 - h:1 - h + HALF_ROWS + 1, 1:WID + 1],
                                     xq_img[b, :, r:r + HALF_ROWS + 1, :]).then_inc(s[f"c_loaded{k}"], 16)
                        sp.dma_start(X[k][h * CH:(h + 1) * CH].rearrange("p c n -> p (c n)"), pixels(x, b, h)).then_inc(s[f"c_loaded{k}"], 16)

                def store_rows(b):
                    hold(sp, s["rows_ready"], b + 1, s["sp_turns"])
                    for h in range(2):
                        sp.dma_start(node_img[b, h], rows[:, :, h * ROW:(h + 1) * ROW]).then_inc(s["rows_stored"], 16)

                def store_pair(i, more):
                    for k in range(2):
                        b = i * 2 + k
                        hold(sp, s["summed"], b + 1, s["sp_turns"])
                        sp.dma_start(x1_d[bass.ds(b * CHUNKS, CHUNKS)].rearrange("c p n -> p c n"), X[k]).then_inc(s[f"x1_stored{k}"], 16)
                        if not (isinstance(b, int) and b == 0):
                            store_rows(b - 1)
                        hold(sp, s["tokens_ready"], b + 1, s["sp_turns"])
                        sp.dma_start(t_d[bass.ds(b * CHUNKS, CHUNKS)].rearrange("c p n -> p c n"), D[k]).then_inc(s[f"t_stored{k}"], 16)
                        if more:
                            hold(sp, s[f"x1_stored{k}"], i * 16 + 16, s["sp_turns"])
                            load_c(b + 2, k)
                for k in range(2):
                    load_c(k, k)
                store_pair(0, True)
                with sp.Fori(1, B // 2 - 1) as i:
                    store_pair(i, True)
                store_pair(B // 2 - 1, False)
                store_rows(B - 1)
                for k in range(2):
                    sp.wait_ge(s[f"x1_stored{k}"], B // 2 * 16)
                    sp.wait_ge(s[f"t_stored{k}"], B // 2 * 16)
                sp.wait_ge(s["rows_stored"], B * 32)
                sp.wait_ge(s["blk_stored"], 16)

            @block.gpsimd
            def _(pool):
                step = Signal(s["pstep"])
                link(pool, pool.memset(ident[:], 0.0), step)
                link(pool, pool.affine_select(out=ident[:], in_=ident[:], compare_op=ALU.not_equal, fill=1.0, base=0,
                                              pattern=[[-1, P]], channel_multiplier=1), step)
                link(pool, pool.tensor_copy(ident_h[:], ident[:]), step)
                link(pool, pool.memset(ones[:], 1.0), step)
                link(pool, pool.affine_select(out=below[:], in_=ones[:], compare_op=ALU.is_gt, fill=0.0, base=0,
                                              pattern=[[1, P]], channel_multiplier=-1), step)
                link(pool, pool.iota(scratch_i[:], pattern=[[1, P]], base=0, channel_multiplier=0), step)
                link(pool, pool.tensor_copy(lane[:], scratch_i[:]), step)
                link(pool, pool.iota(scratch_i[:, 0:ID_W], pattern=[[1, ID_W]], base=0, channel_multiplier=ID_W), step)
                link(pool, pool.tensor_copy(unit_no[:], scratch_i[:, 0:ID_W]), step)
                link(pool, pool.memset(zero_row[:], 0.0), step)
                link(pool, pool.memset(halves[:], 0.0), step)
                for h in range(2):
                    link(pool, pool.memset(halves[h * CH:(h + 1) * CH, h * CH:(h + 1) * CH], 1.0 / CH), step)
                link(pool, pool.memset(eps_c[:], 1e-6), step)
                link(pool, pool.memset(eps_t[:], 1e-5), step)
                for k in range(2):
                    link(pool, pool.memset(Q[k][:], 0.0), step)
                link(pool, pool.memset(cw_bd[:], 0.0), step)
                link(pool, pool.memset(zeros_h[:], 0.0), step)
                link(pool, pool.memset(inj[:], 0.0), step)
                link(pool, pool.memset(keep[:], 1.0), step)
                link(pool, pool.memset(keep[:, :, 0:1], 0.0), step)
                link(pool, pool.iota(scratch_i[:, 0:RUN_COLS], pattern=[[P, RUN_COLS]], base=0, channel_multiplier=1), step)
                link(pool, pool.tensor_copy(run_no[:], scratch_i[:, 0:RUN_COLS]), step)
                link(pool, pool.tensor_copy(lane_h[:], lane[:].rearrange("p (l k) -> p l k", k=1).broadcast_to([P, P, STEP])), step)
                link(pool, pool.memset(pick[:], 0.0), step)
                for r in range(3):
                    link(pool, pool.affine_select(out=pick[:], in_=pick[:], compare_op=ALU.not_equal, fill=1.0, base=-r * EXPERTS,
                                                  pattern=[[-1, EXPERTS], [0, CH]], channel_multiplier=1), step)
                link(pool, pool.memset(fold[:], 0.0), step)
                for r in range(2):
                    link(pool, pool.affine_select(out=fold[:], in_=fold[:], compare_op=ALU.not_equal, fill=1.0, base=-r * CH,
                                                  pattern=[[-1, CH]], channel_multiplier=1), step)
                pool.memset(scratch_i[:], 0).then_inc(s["const_ready"], 1)
                n = TILES * FIELDS // 8
                for k in range(8):
                    pool.dma_start(edge_d.rearrange("(p n) e -> p (n e)", p=P)[:, k * n:(k + 1) * n], zeros_h[:, 0:n].bitcast(F16)).then_inc(s["pads_written"], 16)
                pool.wait_ge(s["pads_written"], 8 * 16)

                with pool.Fori(0, SG // 2) as i:
                    for k in range(2):
                        hold(pool, s["group_slots"], i * 2 + k + 1, s["pool_turns"])
                        hold(pool, s["group_out"], i * 2 + k + 1, s["pool_turns"])
                        for c in range(RUN_COLS):
                            pool.indirect_dma_start(edge_d, bass.IndirectOffsetOnAxis(ap=slots[:, k, c:c + 1], axis=0),
                                                    run_slots[:, k, c * RUN:(c + 1) * RUN, :].rearrange("p c v -> p (c v)"), None).then_inc(sent[k], 16)
                for k in range(2):
                    pool.wait_ge(sent[k], SG // 2 * RUN_COLS * 16)

            def mean_of(pe, src_t, done):
                for c in range(CHUNKS):
                    mm = pe.matmul(A[:, c, 0:CHUNK], halves[:], src_t[:, c, :], start=True, stop=True)
                mm.then_inc(done, 1)

            VAR_AT = 512 - 2 * TOK_TILES

            def variance_of(pe, k, done):
                squares = S[:].rearrange("p c n -> p (c n)")
                for j in range(TOK_TILES):
                    mm = pe.matmul(C[0:TOK, k, VAR_AT + j * 2:VAR_AT + (j + 1) * 2], squares[:, j * TOK:(j + 1) * TOK],
                                   halves[:].rearrange("p (h c) -> p h c", h=2)[:, :, 0], start=True, stop=True)
                mm.then_inc(done, 1)

            def spread_rstd(pe, out_ps, done):
                for j in range(TOK_TILES):
                    for h in range(2):
                        mm = pe.matmul(out_ps[h * CH:(h + 1) * CH, j // 4, (j % 4) * TOK:(j % 4 + 1) * TOK],
                                       rstd[:, j, h:h + 1].broadcast_to([TOK, CH]), ident[0:TOK, 0:TOK], start=True, stop=True)
                mm.then_inc(done, 1)

            @block.tensor
            def _(pe):
                pe.wait_ge(s["const_ready"], 1)
                pe.wait_ge(s["counted"], 1)
                n = NB * SG // 4
                for k in range(4):
                    pe.matmul(A[:, k, 0:n], below[:], flat_count[:, k * n:(k + 1) * n], start=True, stop=True)
                    mm = pe.matmul(C[:, k, 0:n], ones[:], flat_count[:, k * n:(k + 1) * n], start=True, stop=True)
                mm.then_inc(s["prefix_ready"], 1)
                pe.wait_ge(s["w_blocks"], 1)
                for t in range(TAPS):
                    mm = pe.transpose(C[:].bitcast(BF16)[:, t // 4, (t % 4) * P:(t % 4 + 1) * P], cw_bd[:, t, :], ident_h[:])
                mm.then_inc(s["w_turned"], 1)
                pe.wait_ge(s["w_ready"], 1)

                def sort_step(g, k, j):
                    if j == 0 and not (isinstance(g, int) and g < 2):
                        pe.wait_ge(s["group_out"], g - 1)
                    pe.wait_ge(s["spread_steps"], g * 2 + j + 1)
                    fields = wide_rec[:, j].rearrange("p v c t -> p (v c) t")
                    for t in range(STEP):
                        mm = pe.matmul(C[:, k, 0:FIELDS * SLOT_COLS], hot_lo[:, j, :, t], fields[:, :, t],
                                       start=(j == 0 and t == 0), stop=(j == 1 and t == STEP - 1))
                    mm.then_inc(s["step_sums"], 1)

                def norm_pair(i, last=False):
                    for k in range(2):
                        pe.wait_ge(s["squared"], i * 2 + k + 1)
                        variance_of(pe, k, s["var_ready"])
                        pe.wait_ge(s["rstd_ready"], i * 2 + k + 1)
                        spread_rstd(pe, C, s["rstd_spread"])
                        if not (last and k == 1):
                            pe.wait_ge(s[f"x_loaded{1 - k}"], (i + k) * 32 + 32)
                            mean_of(pe, X[1 - k], s["mean_ready"])
                pe.wait_ge(s["x_loaded0"], 32)
                mean_of(pe, X[0], s["mean_ready"])
                with pe.Fori(0, B // 2 - 1) as i:
                    norm_pair(i)
                norm_pair(B // 2 - 1, True)
                for k in range(2):
                    for j in range(2):
                        sort_step(k, k, j)
                with pe.Fori(1, SG // 4) as i:
                    for k in range(2):
                        for j in range(2):
                            sort_step(i * 2 + k, k, j)
                for j in range(2):
                    sort_step(SG // 2, 0, j)

                def convolve(i, k):
                    pe.wait_ge(s[f"c_loaded{k}"], i * 64 + 64)
                    for c in range(CHUNKS):
                        for t in range(TAPS):
                            r0 = c * CHUNK_ROWS + t // 3
                            mm = pe.matmul(A[:, c, 0:CHUNK], cw_t[:, t, :], Q[k][:, r0:r0 + CHUNK_ROWS, t % 3:t % 3 + WID],
                                           start=(t == 0), stop=(t == TAPS - 1))
                    mm.then_inc(s["conv_done"], 1)

                def project(b, k):
                    if not (isinstance(b, int) and b == 0):
                        pe.wait_ge(s["rows_ready"], b)
                    tokens = D[k].rearrange("p c n -> p (c n)")
                    for j in range(TOK_TILES):
                        mm = pe.matmul(C[0:TOK, 2 + j // 7, (j % 7) * 2 * ROW:(j % 7 + 1) * 2 * ROW],
                                       tokens[:, j * TOK:(j + 1) * TOK], proj[:].rearrange("p s f -> p (s f)"), start=True, stop=True)
                    mm.then_inc(s["projected"], 1)

                def image_pair(i, last=False):
                    for k in range(2):
                        b, g = i * 2 + k, i * 2 + k + SG // 2 + 1
                        pe.wait_ge(s["summed"], b + 1)
                        mean_of(pe, X[k], s["mean2_ready"])
                        if not (isinstance(b, int) and b == 0):
                            project(b - 1, 1 - k)
                        pe.wait_ge(s["squared2"], b + 1)
                        variance_of(pe, k, s["var2_ready"])
                        if not (last and k == 1):
                            sort_step(g, 1 - k, 0)
                        pe.wait_ge(s["rstd2_ready"], b + 1)
                        spread_rstd(pe, A, s["rstd2_spread"])
                        pe.wait_ge(s["tokens_ready"], b + 1)
                        if not (last and k == 1):
                            convolve(i + k, 1 - k)
                            sort_step(g, 1 - k, 1)
                convolve(0, 0)
                image_pair(0)
                with pe.Fori(1, B // 2 - 1) as i:
                    image_pair(i)
                image_pair(B // 2 - 1, True)
                project(B - 1, 1)

            @block.scalar
            def _(act):
                act.wait_ge(s["const_ready"], 1)
                act.wait_ge(s["blocks_ready"], 1)
                act.dma_start(blk_d.rearrange("(p k) -> p k", p=P), unit_blk_i[:]).then_inc(s["blk_stored"], 16)

                def group_out(i, k):
                    act.wait_ge(s["step_sums"], i * 4 + k * 2 + 2)
                    if not (isinstance(i, int) and i == 0):
                        act.wait_ge(sent[k], i * (RUN_COLS * 16))
                    act.copy(run_slots[:, k].rearrange("p c v -> p v c"),
                             C[:, k, 0:FIELDS * SLOT_COLS].rearrange("p (v c) -> p v c", v=FIELDS)).then_inc(s["group_out"], 1)

                def deviations(eps, k, ready):
                    act.activation(dev[:].rearrange("p j h -> p (j h)"), C[0:TOK, k, VAR_AT:VAR_AT + 2 * TOK_TILES], ACT.Sqrt, bias=eps[0:TOK]).then_inc(ready, 1)

                with act.Fori(0, B // 2) as i:
                    for k in range(2):
                        act.wait_ge(s["centred"], i * 2 + k + 1)
                        act.activation(S[:], D[k], ACT.Square).then_inc(s["squared"], 1)
                        act.wait_ge(s["var_ready"], i * 2 + k + 1)
                        deviations(eps_c, k, s["deviated"])
                for k in range(2):
                    group_out(0, k)
                with act.Fori(1, SG // 4) as i:
                    for k in range(2):
                        group_out(i, k)
                group_out(SG // 4, 0)
                def rows_out(b):
                    act.wait_ge(s["projected"], b + 1)
                    if not (isinstance(b, int) and b == 0):
                        act.wait_ge(s["rows_stored"], b * 32)
                    act.copy(rows[:].rearrange("p (k j) f -> p k (j f)", k=2), C[0:TOK, 2:4, 0:14 * ROW]).then_inc(s["rows_ready"], 1)

                def image_pair(i, last=False):
                    for k in range(2):
                        b = i * 2 + k
                        act.wait_ge(s["centred2"], b + 1)
                        act.activation(S[:], D[k], ACT.Square).then_inc(s["squared2"], 1)
                        if not (isinstance(b, int) and b == 0):
                            rows_out(b - 1)
                        act.wait_ge(s["var2_ready"], b + 1)
                        deviations(eps_t, k, s["deviated2"])
                        if not (last and k == 1):
                            group_out(i + SG // 4 + k, 1 - k)
                image_pair(0)
                with act.Fori(1, B // 2 - 1) as i:
                    image_pair(i)
                image_pair(B // 2 - 1, True)
                rows_out(B - 1)

            @block.vector
            def _(dve):
                step = Signal(s["vstep"])

                def L(instr):
                    link(dve, instr, step)

                dve.wait_ge(s["edges_loaded"], 32)
                field_i = run[:].bitcast(I32)
                L(dve.tensor_scalar(field_i, dst[:], BLK_BITS, None, ALU.arith_shift_right))
                L(dve.tensor_copy(blk_h[:], field_i))
                by_group = mask_h[:].rearrange("p (g t) -> p g t", g=SG)
                for b in range(NB):
                    L(dve.tensor_scalar(mask_h[:], blk_h[:], float(b), None, ALU.is_equal))
                    for n in (SORT_TILES // 2, SORT_TILES // 4):
                        L(dve.tensor_tensor(by_group[:, :, 0:n], by_group[:, :, 0:n], by_group[:, :, n:2 * n], ALU.add))
                    L(dve.tensor_reduce(count[:, b, :], by_group[:, :, 0:SORT_TILES // 4], AX.X, ALU.add))
                dve.engine_nop().then_inc(s["counted"], 1)
                by_step = field_i.rearrange("p (n t) -> p n t", t=STEP)
                rest_i = pos[:].bitcast(I32)
                L(dve.tensor_scalar(field_i, src[:], LO_BITS, None, ALU.arith_shift_right))
                L(dve.tensor_copy(rec[:, :, 0, :], by_step))
                L(dve.tensor_scalar(field_i, dst[:], P - 1, None, ALU.bitwise_and))
                L(dve.tensor_copy(rec[:, :, 2, :], by_step))
                L(dve.tensor_scalar(rest_i, src[:], P - 1, None, ALU.bitwise_and))
                L(dve.tensor_scalar(field_i, dst[:], BLK - P, None, ALU.bitwise_and))
                L(dve.scalar_tensor_tensor(out=rec[:, :, 1, :], in0=by_step, scalar=float(P), in1=rest_i.rearrange("p (n t) -> p n t", t=STEP), op0=ALU.add, op1=ALU.add))
                dve.engine_nop().then_inc(s["fields_ready"], 1)

                def banks(t):
                    return t.rearrange("p (k n) -> p k n", k=4)
                n = NB * SG // 4
                runs_i = field_i[:, 0:NB * SG]
                dve.wait_ge(s["const_ready"], 1)
                dve.wait_ge(s["prefix_ready"], 1)
                L(dve.tensor_scalar(banks(runs_i), C[:, :, 0:n], float(RUN - 1), None, ALU.add))
                L(dve.tensor_scalar(runs_i, runs_i, RUN_BITS, None, ALU.arith_shift_right))
                L(dve.tensor_copy(flat_runs, runs_i))
                L(dve.tensor_tensor_scan(flat_before, flat_runs, zeros_h[:], 0.0, ALU.add, ALU.add))
                L(dve.tensor_tensor(flat_before, flat_before, flat_runs, ALU.subtract))
                L(dve.tensor_reduce(start_b[:], runs, AX.X, ALU.add))
                L(dve.tensor_scalar(units_i[:], start_b[:], float(P - 1), None, ALU.add))
                L(dve.tensor_scalar(units_i[:], units_i[:], UNIT_RUN_BITS, None, ALU.arith_shift_right))
                L(dve.tensor_copy(units_b[:], units_i[:]))
                L(dve.tensor_tensor_scan(end_b[:], units_b[:], zero_row[:, 0:NB], 0.0, ALU.add, ALU.add))
                L(dve.tensor_tensor(start_b[:], end_b[:], units_b[:], ALU.subtract))
                L(dve.tensor_scalar(start_b[:], start_b[:], float(P), None, ALU.mult))
                L(dve.tensor_tensor(passed[:], end_b[:].rearrange("p (k n) -> p k n", k=1).broadcast_to([P, ID_W, NB]),
                                    unit_no[:].rearrange("p (n k) -> p n k", k=1).broadcast_to([P, ID_W, NB]), ALU.is_le))
                L(dve.tensor_reduce(unit_blk[:], passed[:], AX.X, ALU.add))
                L(dve.tensor_scalar(unit_blk_i[:], unit_blk[:], float(NB - 1), float(HI), ALU.min, ALU.mult))
                dve.engine_nop().then_inc(s["blocks_ready"], 1)
                L(dve.tensor_tensor(start_b[:], start_b[:], before[:, :, 0], ALU.subtract))
                L(dve.tensor_tensor(shift_g[:, :, 0:NB].rearrange("p g b -> p b g"), before,
                                    start_b[:].rearrange("p (b k) -> p b k", k=1).broadcast_to([P, NB, SG]), ALU.add))
                L(dve.tensor_scalar(shift_g[:, :, NB], lane[:, 0:SG], float(P * RUN_COLS), float(P * PLACES), ALU.mult, ALU.add))
                L(dve.tensor_copy(runs_g[:, :, 0:NB], runs.rearrange("p b g -> p g b")))
                L(dve.memset(runs_g[:, :, NB:BLKS], 0.0))
                L(dve.tensor_tensor_scan(local[:].rearrange("p g b -> p (g b)"), keep[:].rearrange("p g b -> p (g b)"),
                                         runs_g.rearrange("p g b -> p (g b)"), 0.0, ALU.mult, ALU.add))
                L(dve.tensor_tensor(local[:], local[:], runs_g, ALU.subtract))
                L(dve.tensor_tensor(shift_g, shift_g, local[:], ALU.subtract))
                L(dve.tensor_copy(delta[:, :, 0:1], shift_g[:, :, 0:1]))
                L(dve.tensor_tensor(delta[:, :, 1:BLKS], shift_g[:, :, 1:BLKS], shift_g[:, :, 0:NB], ALU.subtract))
                L(dve.tensor_scalar(before, local[:, :, 0:NB].rearrange("p g b -> p b g"), float(RUN), -1.0, ALU.mult, ALU.add))
                L(dve.tensor_tensor(banks(flat_before), banks(flat_before), A[:, :, 0:n], ALU.add))
                L(dve.tensor_copy(jump[:, :, 0:1], before[:, :, 0:1]))
                L(dve.tensor_tensor(jump[:, :, 1:SG], before[:, :, 1:SG], before[:, :, 0:SG - 1], ALU.subtract))
                L(dve.tensor_tensor(jump[:, :, 1:SG], jump[:, :, 1:SG], count[:, :, 0:SG - 1], ALU.subtract))
                L(dve.memset(pos[:], 0.0))

                def count_up(b):
                    dve.tensor_scalar(mask_h[:], blk_h[:], lane[:, bass.ds(b, 1)], None, ALU.is_equal)
                    L(dve.tensor_copy(inj[:].rearrange("p (g t) -> p g t", g=SG)[:, :, 0], jump[:, bass.ds(b, 1), :].rearrange("p k g -> p (k g)")))
                    L(dve.tensor_tensor_scan(run[:], mask_h[:], inj[:], 0.0, ALU.add, ALU.add))
                    dve.sem_inc(s["dve_turns"], 1)

                def take_places():
                    L(dve.copy_predicated(pos[:], mask_h[:].bitcast(U16), run[:]))

                def one_hot_step(i, k, j):
                    g = i * 2 + k
                    if not (isinstance(g, int) and g == 0):
                        dve.wait_ge(s["step_sums"], g * 2 + j - 1)
                    cols = bass.ds((g * 2 + j) * STEP, STEP)

                    def over(v, n):
                        return v.rearrange("p (k t) -> p k t", k=1).broadcast_to([P, n, STEP])
                    L(dve.tensor_tensor(hot_lo[:, j], lane_h[:], over(slot_lo[:, cols], P), ALU.is_equal))
                    L(dve.tensor_tensor(hot_col, lane_h[:, 0:SLOT_COLS, :], over(slot_col[:, cols], SLOT_COLS), ALU.is_equal))

                def spread_step(i, k, j):
                    dve.tensor_tensor(wide_rec[:, j], hot_col.rearrange("p (k c) t -> p k c t", k=1).broadcast_to([P, FIELDS, SLOT_COLS, STEP]),
                                      rec[:, bass.ds(i * 4 + k * 2 + j, 1), :, :].rearrange("p k v t -> p v k t").broadcast_to([P, FIELDS, SLOT_COLS, STEP]),
                                      ALU.mult).then_inc(s["spread_steps"], 1)

                def group_places(i, k):
                    here = bass.ds(i * 2 + k, 1)
                    L(dve.tensor_tensor(reached[:], local[:, here, :].broadcast_to([P, RUN_COLS, BLKS]),
                                        run_no[:].rearrange("p (c k) -> p c k", k=1).broadcast_to([P, RUN_COLS, BLKS]), ALU.is_le))
                    L(dve.tensor_tensor(reached[:], reached[:], delta[:, here, :].broadcast_to([P, RUN_COLS, BLKS]), ALU.mult))
                    L(dve.tensor_reduce(place[:], reached[:], AX.X, ALU.add))
                    L(dve.tensor_tensor(place_i[:], place[:], run_no[:], ALU.add))
                    L(dve.tensor_scalar(place_p[:], place_i[:], P - 1, None, ALU.bitwise_and))
                    L(dve.tensor_scalar(place_i[:], place_i[:], LO_BITS, None, ALU.arith_shift_right))
                    if not (isinstance(i, int) and i == 0):
                        dve.wait_ge(sent[k], i * (RUN_COLS * 16))
                    dve.scalar_tensor_tensor(out=slots[:, k, :].bitcast(I32), in0=place_p[:], scalar=float(ALL_PLACES), in1=place_i[:],
                                             op0=ALU.mult, op1=ALU.add).then_inc(s["group_slots"], 1)

                SORT_LINKS = 2 * 2 + 6

                def quantise(vals, whole, quant, n):
                    def wide(v):
                        return v.rearrange("p (n k) -> p n k", k=1).broadcast_to([P, n, GROUP])
                    L(dve.tensor_reduce(gmax[:, 0:n], vals, AX.X, ALU.max, apply_absolute_value=True))
                    L(dve.tensor_scalar(gmax[:, 0:n], gmax[:, 0:n], TINY, None, ALU.max))
                    L(dve.tensor_scalar(gscale[:, 0:n].bitcast(I32), gmax[:, 0:n].bitcast(I32), EXP_BITS, None, ALU.bitwise_and))
                    L(dve.tensor_scalar(ginv[:, 0:n].bitcast(I32), gscale[:, 0:n].bitcast(I32), -1.0, float(INV_BITS), ALU.mult, ALU.add))
                    L(dve.tensor_scalar(ginv[:, 0:n], ginv[:, 0:n], 128.0, None, ALU.mult))
                    L(dve.tensor_scalar(gscale[:, 0:n], gscale[:, 0:n], 1.0 / 128.0, None, ALU.mult))
                    L(dve.tensor_tensor(vals, vals, wide(ginv[:, 0:n]), ALU.mult))
                    L(dve.tensor_scalar(vals, vals, MAGIC, MAGIC + 127.0, ALU.add, ALU.min))
                    L(dve.tensor_scalar(whole, vals, MAGIC - 128.0, MAGIC, ALU.max, ALU.subtract))
                    return dve.tensor_tensor(quant, whole, wide(gscale[:, 0:n]), ALU.mult)

                dve.wait_ge(s["weights_loaded"], 16 * WEIGHT_LOADS)
                v = cw[:].rearrange("p (n i) t -> p n (i t)", i=GROUP // TAPS)
                vq = cwq[:].rearrange("p (n i) t -> p n (i t)", i=GROUP // TAPS)
                L(quantise(v, vq, vq, CH * TAPS // GROUP))
                for h in range(2):
                    L(dve.tensor_copy(cw_bd[h * CH:(h + 1) * CH, :, h * CH:(h + 1) * CH],
                                      cwq[h * CH:(h + 1) * CH].rearrange("p i t -> p t i")))
                for h in range(2):
                    L(dve.memset(proj[(1 - h) * CH:(2 - h) * CH, h, :], 0.0))
                for h in range(2):
                    a = slice(h * CH, (h + 1) * CH)
                    for k in range(2):
                        L(dve.tensor_tensor(attw[a, :], proj[a, h, 0:FEAT], att[a, k, :], ALU.mult))
                        L(dve.tensor_reduce(proj[a, h, FEAT + k * HEADS:FEAT + (k + 1) * HEADS],
                                            attw[a, :].rearrange("p (h d) -> p h d", h=HEADS), AX.X, ALU.add))
                dve.engine_nop().then_inc(s["w_blocks"], 1)
                dve.wait_ge(s["w_turned"], 1)
                L(dve.tensor_copy(cw_t[:, 0:8].rearrange("p (b t) o -> p b (t o)", b=2), C[:].bitcast(BF16)[:, 0:2, 0:512]))
                dve.tensor_copy(cw_t[:, 8], C[:].bitcast(BF16)[:, 2, 0:P]).then_inc(s["w_ready"], 1)

                per_image = 3
                assert B * per_image <= NB

                def scale(t, by, done):
                    flat, split = t.rearrange("p c n -> p (c n)"), 3 * 4 * TOK
                    L(dve.tensor_tensor(flat[:, 0:split].rearrange("p (k n) -> p k n", k=3), flat[:, 0:split].rearrange("p (k n) -> p k n", k=3),
                                        by[:, 0:3, 0:4 * TOK], ALU.mult))
                    dve.tensor_tensor(flat[:, split:HALF], flat[:, split:HALF], by[:, 3, 0:HALF - split], ALU.mult).then_inc(done, 1)

                def norm_pair(i):
                    for k in range(2):
                        b = i * 2 + k
                        dve.wait_ge(s["mean_ready"], b + 1)
                        if not (isinstance(i, int) and i == 0):
                            dve.wait_ge(s[f"xn_stored{k}"], i * 32)
                        dve.tensor_tensor(D[k], X[k], A[:, :, 0:CHUNK], ALU.subtract).then_inc(s["centred"], 1)
                        count_up(b * per_image)
                        take_places()
                        count_up(b * per_image + 1)
                        dve.wait_ge(s["deviated"], b + 1)
                        dve.reciprocal(rstd[:], dev[:]).then_inc(s["rstd_ready"], 1)
                        take_places()
                        count_up(b * per_image + 2)
                        dve.wait_ge(s["rstd_spread"], b + 1)
                        scale(D[k], C, s["normed"])
                        take_places()
                norm_pair(0)
                with rolled(dve, 1, B // 2, step, 2 * (1 + per_image * 3)) as i:
                    norm_pair(i)
                for r in range(B * per_image, NB):
                    count_up(r)
                    take_places()
                slot_i = field_i
                L(dve.tensor_copy(slot_i, pos[:]))
                L(dve.tensor_scalar(rest_i, slot_i, RUN_BITS, P - 1, ALU.arith_shift_right, ALU.bitwise_and))
                L(dve.tensor_copy(slot_lo, rest_i))
                L(dve.tensor_scalar(rest_i, slot_i, RUN_BITS + LO_BITS, None, ALU.arith_shift_right))
                L(dve.tensor_scalar(slot_i, slot_i, RUN - 1, None, ALU.bitwise_and))
                L(dve.scalar_tensor_tensor(out=slot_col, in0=rest_i, scalar=float(RUN), in1=slot_i, op0=ALU.mult, op1=ALU.add))

                def quantise_chunk(i, k):
                    dve.wait_ge(s[f"f_loaded{k}"], i * 16 + 16)
                    if not (isinstance(i, int) and i == 0):
                        dve.wait_ge(s[f"q_stored{k}"], i * 16)
                    quantise(F[k], Fq[k], Fq[k], QGROUPS).then_inc(s["quantised"], 1)

                def quantise_and_sort(i, k):
                    quantise_chunk(i, k)
                    for j in range(2):
                        one_hot_step(i, k, j)
                        spread_step(i, k, j)
                    group_places(i, k)
                for k in range(2):
                    quantise_and_sort(0, k)
                with rolled(dve, 1, QCHUNKS // 2, step, 2 * (9 + SORT_LINKS)) as i:
                    for k in range(2):
                        quantise_and_sort(i, k)
                quantise_and_sort(QCHUNKS // 2, 0)

                def image_pair(i, last=False):
                    for k in range(2):
                        b, at = i * 2 + k, (i + SG // 4 + k, 1 - k)
                        sorts = not (last and k == 1)
                        if sorts:
                            one_hot_step(*at, 0)
                        dve.wait_ge(s["conv_done"], b + 1)
                        dve.scalar_tensor_tensor(out=X[k], in0=A[:, :, 0:CHUNK], scalar=cbias[:], in1=X[k],
                                                 op0=ALU.add, op1=ALU.add).then_inc(s["summed"], 1)
                        if sorts:
                            spread_step(*at, 0)
                        dve.wait_ge(s["mean2_ready"], b + 1)
                        if not (isinstance(i, int) and i == 0):
                            dve.wait_ge(s[f"t_stored{k}"], i * 16)
                        dve.tensor_tensor(D[k], X[k], A[:, :, 0:CHUNK], ALU.subtract).then_inc(s["centred2"], 1)
                        if sorts:
                            group_places(*at)
                        dve.wait_ge(s["deviated2"], b + 1)
                        dve.reciprocal(rstd[:], dev[:]).then_inc(s["rstd2_ready"], 1)
                        if sorts:
                            one_hot_step(*at, 1)
                            spread_step(*at, 1)
                        dve.wait_ge(s["rstd2_spread"], b + 1)
                        scale(D[k], A, s["tokens_ready"])
                image_pair(0)
                with rolled(dve, 1, B // 2 - 1, step, 2 * (1 + SORT_LINKS)) as i:
                    image_pair(i)
                image_pair(B // 2 - 1, True)

        with ExitStack() as ph:
            def tb(name, shape, dt=F32):
                return ph.enter_context(nc.sbuf_tensor(name, shape, dt))

            nodes = tb("nodes", [P, NQ, ROW])
            acc = tb("acc", [P, NQ, VALS])
            srt = tb("srt", [P, TILES, FIELDS], F16)
            lo = srt[:, :, 2]
            hi = tb("hi", [P, TILES], BF16)
            src_no = tb("src_no", [P, TILES], I32)
            blk_row = tb("blk_row", [1, P * ID_W], I32)
            amax = tb("amax", [P, HEADS])
            amax_t = tb("amax_t", [HEADS, 1])
            amax_d = tb("amax_d", [HEADS, HEADS])
            na = tb("na", [P, NQ, HEADS])
            nb = tb("nb", [P, NQ, HEADS])
            lo_hot = tb("lo_hot", [P, UNROLL, G, P])
            hi_hot = tb("hi_hot", [P, UNROLL, G, HI])
            lo_hot_t = tb("lo_hot_t", [P, G, P])
            dst_rows = tb("dst_rows", [P, 2, UG, HI, HEADS])
            gath = tb("gath", [P, BUFS, G, ROW])
            places = tb("places", [P, BUFS, G], U32)
            picked = tb("picked", [P, G, HEADS, HI])
            adst = tb("adst", [P, G, HEADS])
            shift = tb("shift", [P, G, HEADS])
            logit = tb("logit", [P, G, HEADS])
            weight = tb("weight", [P, G, HEADS])
            vals = tb("vals", [P, G, VALS])
            spread = tb("spread", [P, G, HI, VALS])
            gate_rows = tb("gate_rows", [GQ * 3 * EXPERTS, GATE_BUFS, P], BF16)
            T = tb("T", [P, CHUNK])
            hid = tb("hid", [P, CHUNK])
            mlp = tb("mlp", [P, 2, 2, CHUNK])
            s = sems(
                "nodes_loaded sorted_loaded src_ready vstep2 amax_rows amax_turned amax_diag amax_spread self_logits self_weights "
                "lo_hot_ready dst_rows_ready turned turned_copied picked_ready picked_read logits_ready weights_ready rows_used "
                "spread_ready scattered places_ready pool_turns2 sp_turns2 act_turns2 "
                "t_loaded0 t_loaded1 t_used0 t_used1 hidden gelu_ready pair_done pair_out "
                "squares_ready sqvar_ready sqrt_ready exp_in exp_ready gates_split gates_turned gates_copied"
            )
            mlp_stored = [ctx.enter_context(nc.semaphore(f"mlp_stored{h}")) for h in range(2)]
            gathered = [ctx.enter_context(nc.semaphore(f"gathered{k}")) for k in range(BUFS)]
            gate_stored = [ctx.enter_context(nc.semaphore(f"gate_stored{k}")) for k in range(GATE_BUFS)]
            block = ph.enter_context(nc.Block())

            parts = nodes[:].rearrange("p q f -> p (q f)")[:, 0:NQ * 3 * EXPERTS // 2].bitcast(BF16).rearrange("p (q e) -> p q e", e=3 * EXPERTS)

            def over_nodes(v, n):
                return v.rearrange("p (k f) -> p k f", k=1).broadcast_to([P, NQ, n])

            def bank_of(u):
                return 1 + u // 2, u % 2 * HI * VALS

            def unit_blocks(eng, g):
                return nc.values_load_multi_w_load_instructions(
                    blk_row[0:1, bass.ds(g * UG, UG)], engines=[eng.engine], min_val=0, max_val=NQ - HI,
                    skip_runtime_bounds_check_because="the blocks are clamped to the last one where they are made")[1]

            MLP_CHUNKS = B * CHUNKS
            MLP_TRIPS = MLP_CHUNKS * 2 // UNROLL
            TRIPS = -(-NG // UNROLL)
            LAST = NG - (TRIPS - 1) * UNROLL
            assert MLP_TRIPS < TRIPS and UG == 4 and LAST >= 3

            @block.sync
            def _(sp):
                sp.dma_start(srt[:].rearrange("p c k -> p (c k)"), edge_d.rearrange("(p n) e -> p (n e)", p=P)[:, 0:TILES * FIELDS]).then_inc(s["sorted_loaded"], 16)
                sp.dma_start(blk_row[:], blk_d.rearrange("(k n) -> k n", k=1)).then_inc(s["sorted_loaded"], 16)
                for k in range(4):
                    n = NQ // 4
                    sp.dma_start(nodes[:, k * n:(k + 1) * n, :], node_d.rearrange("(q l) f -> l q f", l=P)[:, k * n:(k + 1) * n, :]).then_inc(s["nodes_loaded"], 16)
                for h in range(2):
                    sp.dma_start(T[h * CH:(h + 1) * CH], t_d[0, h * CH:(h + 1) * CH]).then_inc(s[f"t_loaded{h}"], 16)
                with sp.Fori(1, MLP_CHUNKS) as m:
                    for h in range(2):
                        hold(sp, s[f"t_used{h}"], m, s["sp_turns2"])
                        sp.dma_start(T[h * CH:(h + 1) * CH], t_d[m, h * CH:(h + 1) * CH]).then_inc(s[f"t_loaded{h}"], 16)
                for k in range(NQ // GQ):
                    sp.wait_ge(s["gates_copied"], k + 1)
                    sp.dma_start(gate_d[k].rearrange("q e l -> (q e) l"), gate_rows[:, k % GATE_BUFS, :]).then_inc(gate_stored[k % GATE_BUFS], 16)
                for k in range(GATE_BUFS):
                    sp.wait_ge(gate_stored[k], 16 * len(range(k, NQ // GQ, GATE_BUFS)))

            @block.gpsimd
            def _(pool):
                step = Signal(s["places_ready"])
                pool.wait_ge(s["src_ready"], 1)

                def gather(i, k, n):
                    if not (isinstance(i, int) and i == 0):
                        pool.wait_ge(s["rows_used"], (i - 1) * BUFS + k + n)
                    link(pool, pool.tensor_copy(places[:, k:k + n, :].bitcast(I32).rearrange("p n t -> p (n t)"),
                                                src_no[:, bass.ds((i * BUFS + k) * G, n * G)]), step)
                    pool.sem_inc(s["pool_turns2"], 1)
                    for b in range(k, k + n):
                        for j in range(G):
                            pool.indirect_dma_start(gath[:, b, j, :], None, node_d,
                                                    bass.IndirectOffsetOnAxis(ap=places[:, b, j:j + 1], axis=0)).then_inc(gathered[b], 16)
                for k in range(0, BUFS, 2):
                    gather(0, k, 2)
                with rolled(pool, 1, NG // BUFS, step, BUFS // 2) as i:
                    for k in range(0, BUFS, 2):
                        gather(i, k, 2)
                for k in range(0, NG % BUFS, 2):
                    gather(NG // BUFS, k, min(2, NG % BUFS - k))

            @block.scalar
            def _(act):
                act.wait_ge(s["self_logits"], 1)
                act.activation(nb[:], nb[:], ACT.Exp).then_inc(s["self_weights"], 1)

                def turned_copy(g, half):
                    act.wait_ge(s["turned"], g * 2 + half + 1)
                    if not (isinstance(g, int) and g == 0):
                        act.wait_ge(s["picked_ready"], g * 2 - 1 + half)
                    for c in range(2):
                        t = half * G // 2 + c * 4
                        act.copy(lo_hot_t[:, t:t + 4, :].rearrange("p t e -> p (t e)"), A[:, c, :]).then_inc(s["turned_copied"], 1)

                def weigh(g):
                    act.wait_ge(s["logits_ready"], g + 1)
                    act.activation(weight[:], logit[:], ACT.Exp).then_inc(s["weights_ready"], 1)

                def gelu(m, h, e):
                    v = (m * 2 + h) * EXPERTS + e
                    act.wait_ge(s["hidden"], v + 1)
                    act.activation(hid[:], A[:, 2, 0:CHUNK], ACT.Gelu, bias=b1s[:, e:e + 1]).then_inc(s["gelu_ready"], 1)

                def pair_out(m, h, j):
                    if j == 0 and not (isinstance(m, int) and m == 0):
                        act.wait_ge(mlp_stored[h], m * 16)
                    act.wait_ge(s["pair_done"], (m * 2 + h) * 2 + j + 1)
                    act.activation(mlp[:, h, j, :], A[:, 3, 0:CHUNK], ACT.Identity, bias=b2s[:, j:j + 1]).then_inc(s["pair_out"], 1)
                    if j == 1:
                        act.wait_ge(s["pair_out"], (m * 2 + h) * 2 + 2)
                        act.sem_inc(s["act_turns2"], 1)
                        act.dma_start(mlp_d[m, h].rearrange("p j n -> p (j n)"), mlp[:, h].rearrange("p j n -> p (j n)")).then_inc(mlp_stored[h], 16)

                def stage_dst(g, k):
                    if not (isinstance(g, int) and g < 2):
                        act.wait_ge(s["picked_ready"], g * 2 - 2)
                        act.sem_inc(s["act_turns2"], 1)
                    qs = unit_blocks(act, g)
                    for v in range(UG):
                        act.copy(dst_rows[:, k % 2, v], nodes[:, bass.ds(qs[v], HI), FEAT + HEADS:ROW]).then_inc(s["dst_rows_ready"], 1)

                def body(i, k, with_mlp, last=False):
                    g = i * UNROLL + k
                    m, h = i * (UNROLL // 2) + k // 2, k % 2
                    left = LAST - 1 - k if last else UNROLL
                    if with_mlp:
                        gelu(m, h, 0)
                    if left >= 3:
                        stage_dst(g + 3, k + 3)
                    if with_mlp:
                        gelu(m, h, 1)
                        pair_out(m, h, 0)
                        gelu(m, h, 2)
                    if left >= 2:
                        turned_copy(g + 2, 0)
                    if with_mlp:
                        gelu(m, h, 3)
                    if left >= 1:
                        weigh(g + 1)
                    if left >= 2:
                        turned_copy(g + 2, 1)
                    if with_mlp:
                        pair_out(m, h, 1)

                act.wait_ge(s["sorted_loaded"], 32)
                act.wait_ge(s["nodes_loaded"], 64)
                for k in range(2):
                    stage_dst(k, k)
                for g in range(2):
                    for half in range(2):
                        turned_copy(g, half)
                stage_dst(2, 2)
                weigh(0)
                for k in range(UNROLL):
                    body(0, k, True)
                with act.Fori(1, MLP_TRIPS) as i:
                    for k in range(UNROLL):
                        body(i, k, True)
                with act.Fori(MLP_TRIPS, TRIPS - 1) as i:
                    for k in range(UNROLL):
                        body(i, k, False)
                for k in range(LAST):
                    body(TRIPS - 1, k, False, True)
                for h in range(2):
                    act.wait_ge(mlp_stored[h], MLP_CHUNKS * 16)
                act.wait_ge(s["squares_ready"], 1)
                act.activation(acc[:, :, 0:FEAT], nodes[:, :, 0:FEAT], ACT.Square).then_inc(s["sqvar_ready"], 1)
                act.wait_ge(s["squares_ready"], 2)
                act.activation(na[:, :, 1], na[:, :, 0], ACT.Sqrt, bias=eps_t[:], scale=1.0 / FEAT).then_inc(s["sqrt_ready"], 1)
                act.wait_ge(s["exp_in"], 1)
                act.activation(nb[:], nb[:], ACT.Exp).then_inc(s["exp_ready"], 1)

            @block.tensor
            def _(pe):
                pe.wait_ge(s["amax_rows"], 1)
                pe.transpose(C[0:HEADS, 1, 0:P], amax[:], ident[:]).then_inc(s["amax_turned"], 1)
                pe.wait_ge(s["amax_diag"], 1)
                pe.matmul(A[:, 3, 0:HEADS], ones[0:HEADS, :], amax_d[:], start=True, stop=True).then_inc(s["amax_spread"], 1)

                def turn(g, k, half):
                    if half == 0:
                        pe.wait_ge(s["lo_hot_ready"], g + 1)
                    if not (isinstance(g, int) and g == 0 and half == 0):
                        pe.wait_ge(s["turned_copied"], g * 4 + half * 2)
                    for j in range(G // 2):
                        mm = pe.transpose(A[:, j // 4, (j % 4) * P:(j % 4 + 1) * P], lo_hot[:, k, half * G // 2 + j, :], ident[:])
                    mm.then_inc(s["turned"], 1)

                def pick_dst(g, k, half):
                    pe.wait_ge(s["turned_copied"], g * 4 + half * 2 + 2)
                    if half == 0 and not (isinstance(g, int) and g == 0):
                        pe.wait_ge(s["picked_read"], g)
                    pe.wait_ge(s["dst_rows_ready"], g * UG + (half + 1) * UG // 2)
                    for t in range(half * G // 2, (half + 1) * G // 2):
                        mm = pe.matmul(C[:, 0, t * HI * HEADS:(t + 1) * HI * HEADS], lo_hot_t[:, t, :],
                                       dst_rows[:, k % 2, t // U].rearrange("p h f -> p (h f)"), start=True, stop=True)
                    mm.then_inc(s["picked_ready"], 1)

                def scatter(g, k, units):
                    if units[0] == 0:
                        pe.wait_ge(s["spread_ready"], g + 1)
                    for u in units:
                        bank, at = bank_of(u)
                        for j in range(U):
                            mm = pe.matmul(C[:, bank, at:at + HI * VALS], lo_hot[:, k, u * U + j, :],
                                           spread[:, u * U + j].rearrange("p h v -> p (h v)"), start=(j == 0), stop=(j == U - 1))
                        if u % 2:
                            mm.then_inc(s["scattered"], 1)

                def up(m, h, e):
                    a = slice(h * CH, (h + 1) * CH)
                    if e == 0:
                        pe.wait_ge(s[f"t_loaded{h}"], m * 16 + 16)
                    pe.matmul(A[:, 2, 0:CHUNK], w1s[a, e, :], T[a, :], start=True, stop=True).then_inc(s["hidden"], 1)
                    if e == EXPERTS - 1:
                        pe.wait_ge(s["hidden"], (m * 2 + h) * EXPERTS + EXPERTS)
                        pe.sem_inc(s[f"t_used{h}"], 1)

                def down(m, h, e):
                    v = m * 2 + h
                    pe.wait_ge(s["gelu_ready"], v * EXPERTS + e + 1)
                    if e % 2 == 0 and not (isinstance(m, int) and m == 0 and h == 0 and e == 0):
                        pe.wait_ge(s["pair_out"], v * 2 + e // 2)
                    a = slice(e % 2 * CH, (e % 2 + 1) * CH)
                    mm = pe.matmul(A[a, 3, 0:CHUNK], w2s[:, e, :], hid[:], start=True, stop=True)
                    if e % 2:
                        mm.then_inc(s["pair_done"], 1)

                def body(i, k, with_mlp, last=False):
                    g, k2 = i * UNROLL + k, (k + 2) % UNROLL
                    m, h = i * (UNROLL // 2) + k // 2, k % 2
                    turns = not last or k + 2 < LAST

                    def mlp_step(e):
                        if with_mlp:
                            if e:
                                down(m, h, e - 1)
                            if e < EXPERTS:
                                up(m, h, e)
                    mlp_step(0)
                    scatter(g, k, range(0, 2))
                    mlp_step(1)
                    scatter(g, k, range(2, UG))
                    mlp_step(2)
                    if turns:
                        turn(g + 2, k2, 0)
                    mlp_step(3)
                    if turns:
                        turn(g + 2, k2, 1)
                        pick_dst(g + 2, k2, 0)
                    mlp_step(4)
                    if turns:
                        pick_dst(g + 2, k2, 1)

                pe.wait_ge(s["sorted_loaded"], 32)
                pe.wait_ge(s["nodes_loaded"], 64)
                for g in range(2):
                    for half in range(2):
                        turn(g, g, half)
                        pick_dst(g, g, half)
                for k in range(UNROLL):
                    body(0, k, True)
                with pe.Fori(1, MLP_TRIPS) as i:
                    for k in range(UNROLL):
                        body(i, k, True)
                with pe.Fori(MLP_TRIPS, TRIPS - 1) as i:
                    for k in range(UNROLL):
                        body(i, k, False)
                for k in range(LAST):
                    body(TRIPS - 1, k, False, True)
                for k in range(NQ // GQ):
                    if k == 0:
                        pe.wait_ge(s["gates_split"], 1)
                    if k >= 4:
                        pe.wait_ge(s["gates_copied"], k - 3)
                    pe.transpose(A[0:GQ * 3 * EXPERTS, k % 4, 0:P // 2].bitcast(BF16), parts[:, k * GQ:(k + 1) * GQ, :].rearrange("p q e -> p (q e)"), ident_h[:]).then_inc(s["gates_turned"], 1)

            @block.vector
            def _(dve):
                step = Signal(s["vstep2"])

                def L(instr):
                    link(dve, instr, step)

                dve.wait_ge(s["sorted_loaded"], 32)
                mixed_i = spread[:].rearrange("p t h v -> p (t h v)").bitcast(I32)[:, 0:TILES]
                L(dve.tensor_copy(mixed_i, srt[:, :, 1]))
                L(dve.tensor_scalar(src_no[:], mixed_i, P - 1, None, ALU.bitwise_and))
                dve.scalar_tensor_tensor(out=src_no[:], in0=srt[:, :, 0], scalar=float(P), in1=src_no[:], op0=ALU.mult, op1=ALU.add).then_inc(s["src_ready"], 1)
                L(dve.tensor_scalar(mixed_i, mixed_i, LO_BITS, None, ALU.arith_shift_right))
                L(dve.tensor_copy(hi[:], mixed_i))

                def one_hots(g, k):
                    L(dve.tensor_tensor(hi_hot[:, k], lane[:, 1:HI + 1].rearrange("p (k h) -> p k h", k=1).broadcast_to([P, G, HI]),
                                        hi[:, bass.ds(g * G, G)].rearrange("p (t k) -> p t k", k=1).broadcast_to([P, G, HI]), ALU.is_equal))
                    dve.tensor_tensor(lo_hot[:, k], lane[:].rearrange("p (k h) -> p k h", k=1).broadcast_to([P, G, P]),
                                      lo[:, bass.ds(g * G, G)].rearrange("p (t k) -> p t k", k=1).broadcast_to([P, G, P]),
                                      ALU.is_equal).then_inc(s["lo_hot_ready"], 1)

                one_hots(0, 0)
                one_hots(1, 1)

                dve.wait_ge(s["nodes_loaded"], 64)
                a_src, a_dst = nodes[:, :, FEAT:FEAT + HEADS], nodes[:, :, FEAT + HEADS:ROW]
                dve.tensor_reduce(amax[:], a_src.rearrange("p q f -> p f q"), AX.X, ALU.max).then_inc(s["amax_rows"], 1)
                dve.wait_ge(s["amax_turned"], 1)
                L(dve.tensor_reduce(amax_t[:], C[0:HEADS, 1, 0:P], AX.X, ALU.max))
                dve.tensor_scalar(amax_d[:], ident[0:HEADS, 0:HEADS], amax_t[:], None, ALU.mult).then_inc(s["amax_diag"], 1)
                dve.wait_ge(s["amax_spread"], 1)
                L(dve.tensor_copy(amax[:], A[:, 3, 0:HEADS]))

                def leaky(out_t, v):
                    return dve.scalar_tensor_tensor(out=out_t, in0=v, scalar=0.2, in1=v, op0=ALU.mult, op1=ALU.max)

                L(dve.tensor_tensor(na[:], a_dst, over_nodes(amax[:], HEADS), ALU.add))
                L(leaky(na[:], na[:]))
                L(dve.tensor_tensor(nb[:], a_src, a_dst, ALU.add))
                L(leaky(nb[:], nb[:]))
                dve.tensor_tensor(nb[:], nb[:], na[:], ALU.subtract).then_inc(s["self_logits"], 1)
                dve.wait_ge(s["self_weights"], 1)
                L(dve.tensor_copy(acc[:, :, FEAT:VALS], nb[:]))
                for h in range(HEADS):
                    L(dve.tensor_tensor(acc[:, :, h * DIM:(h + 1) * DIM], nodes[:, :, h * DIM:(h + 1) * DIM],
                                        nb[:, :, h:h + 1].broadcast_to([P, NQ, DIM]), ALU.mult))

                def per_edge(v):
                    return v.rearrange("p (k f) -> p k f", k=1).broadcast_to([P, G, HEADS])

                def logits(g, i, k):
                    dve.wait_ge(s["picked_ready"], g * 2 + 2)
                    dve.tensor_tensor(picked[:], C[:, 0, 0:G * HI * HEADS].rearrange("p (t h f) -> p t f h", t=G, h=HI),
                                      hi_hot[:, k].rearrange("p t (k h) -> p t k h", k=1).broadcast_to([P, G, HEADS, HI]),
                                      ALU.mult).then_inc(s["picked_read"], 1)
                    dve.wait_ge(s["picked_read"], g + 1)
                    L(dve.tensor_reduce(adst[:], picked[:], AX.X, ALU.add))
                    L(dve.tensor_tensor(shift[:], adst[:], per_edge(amax[:]), ALU.add))
                    L(leaky(shift[:], shift[:]))
                    dve.wait_ge(gathered[k % BUFS], (i * (UNROLL // BUFS) + k // BUFS + 1) * (G * 16))
                    L(dve.tensor_tensor(adst[:], adst[:], gath[:, k % BUFS, :, FEAT:FEAT + HEADS], ALU.add))
                    L(leaky(adst[:], adst[:]))
                    dve.tensor_tensor(logit[:], adst[:], shift[:], ALU.subtract).then_inc(s["logits_ready"], 1)

                def add_up(g):
                    qs = unit_blocks(dve, g)
                    for u in range(UG):
                        bank, at = bank_of(u)
                        if u % 2 == 0:
                            dve.wait_ge(s["scattered"], g * 2 + bank)
                        here = acc[:, bass.ds(qs[u], HI), :]
                        L(dve.tensor_tensor(here, here, C[:, bank, at:at + HI * VALS].rearrange("p (h v) -> p h v", h=HI), ALU.add))

                def spread_out(g, k):
                    dve.wait_ge(s["weights_ready"], g + 1)
                    L(dve.tensor_copy(vals[:, :, FEAT:VALS], weight[:]))
                    h4 = vals[:, :, 0:FEAT].rearrange("p t (h d) -> p t h d", h=HEADS)
                    dve.tensor_tensor(h4, gath[:, k % BUFS, :, 0:FEAT].rearrange("p t (h d) -> p t h d", h=HEADS),
                                      weight[:].rearrange("p t (h k) -> p t h k", k=1).broadcast_to([P, G, HEADS, DIM]),
                                      ALU.mult).then_inc(s["rows_used"], 1)
                    dve.wait_ge(s["rows_used"], g + 1)
                    dve.tensor_tensor(spread[:], hi_hot[:, k].rearrange("p t (h k) -> p t h k", k=1).broadcast_to([P, G, HI, VALS]),
                                      vals[:].rearrange("p t (k v) -> p t k v", k=1).broadcast_to([P, G, HI, VALS]),
                                      ALU.mult).then_inc(s["spread_ready"], 1)

                def body(i, k, last=False):
                    g = i * UNROLL + k
                    left = LAST - 1 - k if last else UNROLL
                    spread_out(g, k)
                    if left >= 2:
                        one_hots(g + 2, (k + 2) % UNROLL)
                    if left >= 1:
                        logits(g + 1, i + (k + 1) // UNROLL, (k + 1) % UNROLL)
                    add_up(g)

                logits(0, 0, 0)
                with rolled(dve, 0, TRIPS - 1, step, UNROLL * (5 + UG + 2)) as i:
                    for k in range(UNROLL):
                        body(i, k)
                for k in range(LAST):
                    body(TRIPS - 1, k, True)

                agg, den = acc[:, :, 0:FEAT], acc[:, :, FEAT:VALS]
                L(dve.tensor_scalar(na[:], den, 1e-16, None, ALU.add))
                L(dve.reciprocal(nb[:], na[:]))
                dev = nodes[:, :, 0:FEAT]
                for h in range(HEADS):
                    L(dve.tensor_tensor(dev[:, :, h * DIM:(h + 1) * DIM], agg[:, :, h * DIM:(h + 1) * DIM],
                                        nb[:, :, h:h + 1].broadcast_to([P, NQ, DIM]), ALU.mult))
                L(dve.tensor_tensor(dev, dev, over_nodes(vecs[:, 0, :], FEAT), ALU.add))
                L(dve.tensor_reduce(na[:, :, 0], dev, AX.X, ALU.add))
                L(dve.tensor_scalar(na[:, :, 1], na[:, :, 0], 1.0 / FEAT, None, ALU.mult))
                dve.tensor_tensor(dev, dev, na[:, :, 1:2].broadcast_to([P, NQ, FEAT]), ALU.subtract).then_inc(s["squares_ready"], 1)
                scaled = lo_hot[:].rearrange("p b t l -> p (b t l)")[:, 0:NQ * FEAT].rearrange("p (q f) -> p q f", q=NQ)
                dve.wait_ge(s["squares_ready"], 1)
                L(dve.tensor_tensor(scaled, dev, over_nodes(vecs[:, 1, :], FEAT), ALU.mult))
                dve.wait_ge(s["sqvar_ready"], 1)
                dve.tensor_reduce(na[:, :, 0], agg, AX.X, ALU.add).then_inc(s["squares_ready"], 1)
                L(dve.tensor_reduce(nb[:], scaled.rearrange("p q (h d) -> p q d h", h=HEADS), AX.X, ALU.add))
                dve.wait_ge(s["sqrt_ready"], 1)
                L(dve.reciprocal(na[:, :, 2], na[:, :, 1]))
                L(dve.tensor_tensor(nb[:], nb[:], na[:, :, 2:3].broadcast_to([P, NQ, EXPERTS]), ALU.mult))
                L(dve.tensor_reduce(amax[:], vecs[:, 2, :].rearrange("p (h d) -> p d h", h=HEADS), AX.X, ALU.add))
                L(dve.tensor_tensor(nb[:], nb[:], over_nodes(amax[:], EXPERTS), ALU.add))
                L(dve.tensor_scalar(na[:], nb[:], 1.0 / HEADS, None, ALU.mult))
                rank, beat = acc[:, :, 0:EXPERTS], acc[:, :, EXPERTS]
                for e in range(EXPERTS):
                    L(dve.memset(rank[:, :, e], float(EXPERTS - 1 - e)))
                for e in range(EXPERTS):
                    for f in range(e + 1, EXPERTS):
                        L(dve.tensor_tensor(beat, na[:, :, e], na[:, :, f], ALU.is_ge))
                        L(dve.tensor_tensor(rank[:, :, e], rank[:, :, e], beat, ALU.subtract))
                        L(dve.tensor_tensor(rank[:, :, f], rank[:, :, f], beat, ALU.add))
                top, total = acc[:, :, EXPERTS], acc[:, :, EXPERTS + 1]
                L(dve.tensor_reduce(top, na[:], AX.X, ALU.max))
                dve.tensor_tensor(nb[:], na[:], acc[:, :, EXPERTS:EXPERTS + 1].broadcast_to([P, NQ, EXPERTS]), ALU.subtract).then_inc(s["exp_in"], 1)
                dve.wait_ge(s["exp_ready"], 1)
                L(dve.tensor_scalar(rank, rank, 1.5, None, ALU.is_lt))
                L(dve.tensor_tensor(nb[:], nb[:], rank, ALU.mult))
                L(dve.tensor_reduce(total, nb[:], AX.X, ALU.add))
                L(dve.reciprocal(top, total))
                L(dve.tensor_tensor(nb[:], nb[:], acc[:, :, EXPERTS:EXPERTS + 1].broadcast_to([P, NQ, EXPERTS]), ALU.mult))
                for r in range(3):
                    part = parts[:, :, r * EXPERTS:(r + 1) * EXPERTS]
                    if r < 2:
                        L(dve.tensor_copy(part, nb[:]))
                        L(dve.tensor_tensor(nb[:], nb[:], part, ALU.subtract))
                    else:
                        dve.tensor_copy(part, nb[:]).then_inc(s["gates_split"], 1)
                for k in range(NQ // GQ):
                    dve.wait_ge(s["gates_turned"], k + 1)
                    if k >= GATE_BUFS:
                        dve.wait_ge(gate_stored[k % GATE_BUFS], 16 * (k // GATE_BUFS))
                    dve.tensor_copy(gate_rows[:, k % GATE_BUFS, :], A[0:GQ * 3 * EXPERTS, k % 4, 0:P // 2].bitcast(BF16)).then_inc(s["gates_copied"], 1)

        with ExitStack() as ph:
            def tb(name, shape, dt=F32):
                return ph.enter_context(nc.sbuf_tensor(name, shape, dt))

            gate_t = tb("gate_t", [3 * EXPERTS, 2, PAIR_Q, P], BF16)
            NBUF, AHEAD = 8, 6
            mlp = tb("mlp3", [P, NBUF, 2, 2, CHUNK])
            X1 = tb("X1", [P, NBUF, CHUNK])
            gated = tb("gated", [P, 4, CHUNK])
            s = sems("gate_ready gated_ready folded summed3 sp_turns3 gate_loaded0 gate_loaded1")
            chunk_in = [ctx.enter_context(nc.semaphore(f"chunk_in{k}")) for k in range(NBUF)]
            chunk_out = [ctx.enter_context(nc.semaphore(f"chunk_out{k}")) for k in range(NBUF)]
            block = ph.enter_context(nc.Block())
            ROUNDS = B // 4
            PER = 2 * CHUNKS
            STEPS = 2 * PER

            out_rows = out.rearrange("b c (s k r) w -> b k s c (r w)", s=2, k=CHUNKS)

            @block.sync
            def _(sp):
                def load(n, k):
                    sp.dma_start(mlp[:, k], mlp_d[n].rearrange("s p j n -> p s j n")).then_inc(chunk_in[k], 16)
                    sp.dma_start(X1[:, k], x1_d[n]).then_inc(chunk_in[k], 16)

                def load_gates(pair, half):
                    sp.dma_start(gate_t[:, half], gate_d.rearrange("k q e l -> e (k q) l")[:, bass.ds(pair * PAIR_Q, PAIR_Q), :]).then_inc(s[f"gate_loaded{half}"], 16)

                load_gates(0, 0)
                for k in range(AHEAD):
                    load(k, k)
                load_gates(1, 1)

                def store_and_load(r, t, more, first=False):
                    k, ahead = t % NBUF, (t + AHEAD) % NBUF
                    hold(sp, s["summed3"], r * STEPS + t + 1, s["sp_turns3"])
                    for h in range(2):
                        sp.dma_start(out_rows[r * 4 + t // CHUNKS, t % CHUNKS, h], X1[h * CH:(h + 1) * CH, k]).then_inc(chunk_out[k], 16)
                    if more or t < STEPS - AHEAD:
                        if not first or t >= NBUF - AHEAD:
                            hold(sp, chunk_out[ahead], (r * (STEPS // NBUF) + (t + AHEAD) // NBUF) * 32, s["sp_turns3"])
                        load(r * STEPS + t + AHEAD, ahead)
                    if more and t % PER == PER - 1:
                        load_gates(r * 2 + 2 + t // PER, t // PER)

                for t in range(STEPS):
                    store_and_load(0, t, True, True)
                with sp.Fori(1, ROUNDS - 1) as r:
                    for t in range(STEPS):
                        store_and_load(r, t, True)
                for t in range(STEPS):
                    store_and_load(ROUNDS - 1, t, False)
                for k in range(NBUF):
                    sp.wait_ge(chunk_out[k], ROUNDS * STEPS // NBUF * 32)

            @block.tensor
            def _(pe):
                def spread_gates(r, t, h, j, first):
                    w = (t * 2 + h) * 2 + j
                    n = (t % PER) // CHUNKS * HGT * WID + h * HALF + t % CHUNKS * CHUNK
                    if j == 0 and h == 0 and t % PER == 0:
                        pe.wait_ge(s[f"gate_loaded{t // PER}"], r * 16 + 16)
                    if w >= 4 or not first:
                        pe.wait_ge(s["gated_ready"], r * STEPS * 4 + w - 3)
                    pe.matmul(A[:, w % 4, 0:CHUNK], pick[:, 2 * j:2 * j + 2, :].rearrange("e k c -> e (k c)"),
                              gate_t[:, t // PER].rearrange("e q l -> e (q l)")[:, n:n + CHUNK], start=True, stop=True).then_inc(s["gate_ready"], 1)

                def fold_pair(r, t, h, j, first):
                    w = (t * 2 + h) * 2 + j
                    if h == 0 and j == 0 and (t >= 2 or not first):
                        pe.wait_ge(s["summed3"], r * STEPS + t - 1)
                    pe.wait_ge(s["gated_ready"], r * STEPS * 4 + w + 1)
                    pe.matmul(C[h * CH:(h + 1) * CH, t % 2, 0:CHUNK], fold[:], gated[:, w % 4, :],
                              start=(j == 0), stop=(j == 1)).then_inc(s["folded"], 1)

                def round_of(r, first):
                    todo = [(t, h, j) for t in range(STEPS) for h in range(2) for j in range(2)]
                    for w, at in enumerate(todo):
                        spread_gates(r, *at, first)
                        if w >= 2:
                            fold_pair(r, *todo[w - 2], first)
                    for at in todo[-2:]:
                        fold_pair(r, *at, first)

                round_of(0, True)
                with pe.Fori(1, ROUNDS) as r:
                    round_of(r, False)

            @block.vector
            def _(dve):
                def add_x1(r, t):
                    dve.wait_ge(s["folded"], (r * STEPS + t + 1) * 4)
                    dve.tensor_tensor(X1[:, t % NBUF], X1[:, t % NBUF], C[:, t % 2, 0:CHUNK], ALU.add).then_inc(s["summed3"], 1)

                def round_of(r, first):
                    for t in range(STEPS):
                        dve.wait_ge(chunk_in[t % NBUF], (r * (STEPS // NBUF) + t // NBUF + 1) * 32)
                        for h in range(2):
                            for j in range(2):
                                w = (t * 2 + h) * 2 + j
                                dve.wait_ge(s["gate_ready"], r * STEPS * 4 + w + 1)
                                if w >= 4 or not first:
                                    dve.wait_ge(s["folded"], r * STEPS * 4 + w - 3)
                                dve.tensor_tensor(gated[:, w % 4, :], mlp[:, t % NBUF, h, j, :], A[:, w % 4, 0:CHUNK], ALU.mult).then_inc(s["gated_ready"], 1)
                        if t:
                            add_x1(r, t - 1)
                    add_x1(r, STEPS - 1)

                round_of(0, True)
                with dve.Fori(1, ROUNDS) as r:
                    round_of(r, False)


_INS = ['x', 'L0_conv_weight', 'L0_conv_bias', 'L0_ffn_W_gat', 'L0_ffn_att_src', 'L0_ffn_att_dst', 'L0_ffn_b_gat',
        'L0_ffn_ln_gamma', 'L0_ffn_ln_beta', 'L0_ffn_W1', 'L0_ffn_b1', 'L0_ffn_W2', 'L0_ffn_b2', 'L0_ffn_edge_index']


def kernel(**inputs):
    import numpy as _np
    import concourse.bacc as _bacc
    from concourse.bass_utils import run_bass_kernel_spmd as _run

    nc = _bacc.Bacc("TRN2", target_bir_lowering=False, num_devices=1)
    arrays, args = {}, []
    for name in _INS:
        a = _np.ascontiguousarray(inputs[name])
        arrays[f"in_{name}"] = a
        args.append(nc.dram_tensor(f"in_{name}", a.shape, mybir.dt.from_np(a.dtype), kind="ExternalInput").ap())
    args.append(nc.dram_tensor("out_0", (B, CH, HGT, WID), F32, kind="ExternalOutput").ap())
    build(nc, *args)
    r = _run(nc, [arrays], core_ids=[0])
    return r.results[0]["out_0"]
```
